# Optimizing a Trainium2 kernel written in Bass

```python
import numpy as np
import jax
import jax.numpy as jnp

def _softmax(x, axis=-1):
    return jax.nn.softmax(x, axis=axis)

def _gelu(x):
    return jax.nn.gelu(x, approximate=True)

def _silu(x):
    return jax.nn.silu(x)

def _sigmoid(x):
    return jax.nn.sigmoid(x)

def _layernorm(x, axis=-1, eps=1e-05):
    m = jnp.mean(x, axis=axis, keepdims=True)
    v = jnp.var(x, axis=axis, keepdims=True)
    return (x - m) / jnp.sqrt(v + eps)

def _scatter_add(tgt, idx, src, axis=0):
    return tgt.at[idx].add(src)

def _segment_sum(src, seg, n):
    return jax.ops.segment_sum(src, seg, n)
kernel_name = 'mk_flamingo_gated_d1_seqx_r8_e68fba'

def setup_inputs(seed: int=0):
    np.random.seed(seed)
    _w = jnp.asarray

    def _rec_inputs():
        import jax
        import jax.numpy as jnp
        _rk = jax.random.key(seed)
        x = -0.0003929 + 0.9999 * jax.random.normal(jax.random.fold_in(_rk, 1), (64, 128, 128), jnp.float32)
        _lenS = 128 - jax.random.randint(jax.random.fold_in(_rk, 7), (64,), 0, max(1, 128 // 4) + 1, jnp.int32)
        _lenS2 = 77 - jax.random.randint(jax.random.fold_in(_rk, 8), (64,), 0, max(1, 77 // 4) + 1, jnp.int32)
        _ctx_768P = jax.random.normal(jax.random.fold_in(_rk, 11), (64, 16, 96), jnp.float32)
        _ctx_768c = jax.random.dirichlet(jax.random.fold_in(_rk, 511), 0.3 * jnp.ones((16,), jnp.float32), (64, 77))
        _ctx_768t = jnp.einsum('bsk,bkd->bsd', _ctx_768c, _ctx_768P)
        _ctx_768t = _ctx_768t * jax.lax.rsqrt(jnp.mean(jnp.square(_ctx_768t)) + 1e-12) * 0.953939
        ctx_768 = -0.00055796 + 0.999787 * (_ctx_768t + 0.3 * jax.random.normal(jax.random.fold_in(_rk, 611), (64, 77, 96), jnp.float32))
        _g = jax.random.normal(jax.random.fold_in(_rk, 9001), (2, 1), jnp.float32)
        _g = jnp.sign(_g) * jnp.maximum(jnp.abs(_g), 1.0) + (_g == 0) * 1.0
        g_xattn = _g[0]
        g_ffn = _g[1]
        return (x, ctx_768, g_xattn, g_ffn)
    x, ctx_768, g_xattn, g_ffn = _rec_inputs()

    def _L0_xattn_setup():
        import jax, jax.numpy as jnp
        import numpy as np
        IMAGE_DIM = 128
        TEXT_DIM = 96
        NUM_HEADS = 16
        HEAD_DIM = IMAGE_DIM // NUM_HEADS
        key = jax.random.key(seed)
        ks = jax.random.split(key, 14)
        B, N, M = (4, 512, 64)
        s_img = 1.0 / np.sqrt(IMAGE_DIM)
        s_txt = 1.0 / np.sqrt(TEXT_DIM)
        s_ff = 1.0 / np.sqrt(2 * IMAGE_DIM)
        return {'x': jax.random.normal(ks[0], (B, N, IMAGE_DIM), jnp.float32), 'y': jax.random.normal(ks[1], (B, M, TEXT_DIM), jnp.float32), 'Wq': jax.random.normal(ks[2], (IMAGE_DIM, IMAGE_DIM), jnp.float32) * s_img, 'bq': jax.random.normal(ks[3], (IMAGE_DIM,), jnp.float32) * s_img, 'Wk': jax.random.normal(ks[4], (TEXT_DIM, IMAGE_DIM), jnp.float32) * s_txt, 'bk': jax.random.normal(ks[5], (IMAGE_DIM,), jnp.float32) * s_txt, 'Wv': jax.random.normal(ks[6], (TEXT_DIM, IMAGE_DIM), jnp.float32) * s_txt, 'bv': jax.random.normal(ks[7], (IMAGE_DIM,), jnp.float32) * s_txt, 'W1': jax.random.normal(ks[8], (IMAGE_DIM, 2 * IMAGE_DIM), jnp.float32) * s_img, 'b1': jax.random.normal(ks[9], (2 * IMAGE_DIM,), jnp.float32) * s_img, 'W2': jax.random.normal(ks[10], (2 * IMAGE_DIM, IMAGE_DIM), jnp.float32) * s_ff, 'b2': jax.random.normal(ks[11], (IMAGE_DIM,), jnp.float32) * s_ff}
    _L0_xattn_all = _L0_xattn_setup()
    _L0_xattn_in = {k: v for k, v in _L0_xattn_all.items() if k in ('Wq', 'bq', 'Wk', 'bk', 'Wv', 'bv', 'W1', 'b1', 'W2', 'b2')}
    del _L0_xattn_all

    def _L0_ffn_setup():
        import jax, jax.numpy as jnp
        import numpy as np
        DIM = 128
        HEADS = 16
        HD = DIM // HEADS
        M = 32
        E = 4
        K = 2
        HID = 256
        MID = 256
        LB = 0.01
        EPS = 1.1920929e-07

        def _rms(x, w):
            return x * jax.lax.rsqrt(jnp.mean(x * x, axis=-1, keepdims=True) + EPS) * w

        def _gelu(x):
            return jax.nn.gelu(x, approximate=False)
        key = jax.random.key(seed)
        ks = jax.random.split(key, 20)
        d = DIM
        w = lambda k, s: jax.random.normal(k, s, jnp.float32) * 0.02
        return {'x': jax.random.normal(ks[0], (4, 128, d), jnp.float32), 'n1_w': jnp.ones((d,), jnp.float32), 'n2_w': jnp.ones((d,), jnp.float32), 'wq': w(ks[1], (d, d)), 'wk': w(ks[2], (d, d)), 'wv': w(ks[3], (d, d)), 'wo': w(ks[4], (d, d)), 'qn_w': jnp.ones((HD,), jnp.float32), 'kn_w': jnp.ones((HD,), jnp.float32), 'gate_w': w(ks[5], (E, d)), 'e0_up': w(ks[6], (HID, d)), 'e0_down': w(ks[7], (d, HID)), 'e1_w1': w(ks[8], (HID, d)), 'e1_w2': w(ks[9], (HID, d)), 'e1_down': w(ks[10], (d, HID)), 'e2_l1': w(ks[11], (MID, d)), 'e2_l2': w(ks[12], (HID, MID)), 'e2_l3': w(ks[13], (MID, HID)), 'e2_l4': w(ks[14], (d, MID)), 'e3_down': w(ks[15], (d, d)), 'e3_up': w(ks[16], (HID, d)), 'e3_out': w(ks[17], (d, HID))}
    _L0_ffn_all = _L0_ffn_setup()
    _L0_ffn_in = {k: v for k, v in _L0_ffn_all.items() if k in ('n1_w', 'n2_w', 'wq', 'wk', 'wv', 'wo', 'qn_w', 'kn_w', 'gate_w', 'e0_up', 'e0_down', 'e1_w1', 'e1_w2', 'e1_down', 'e2_l1', 'e2_l2', 'e2_l3', 'e2_l4', 'e3_down', 'e3_up', 'e3_out')}
    del _L0_ffn_all
    return {'x': x, 'ctx_768': ctx_768, 'g_xattn': g_xattn, 'g_ffn': g_ffn, 'L0_xattn_Wq': _L0_xattn_in['Wq'], 'L0_xattn_bq': _L0_xattn_in['bq'], 'L0_xattn_Wk': _L0_xattn_in['Wk'], 'L0_xattn_bk': _L0_xattn_in['bk'], 'L0_xattn_Wv': _L0_xattn_in['Wv'], 'L0_xattn_bv': _L0_xattn_in['bv'], 'L0_xattn_W1': _L0_xattn_in['W1'], 'L0_xattn_b1': _L0_xattn_in['b1'], 'L0_xattn_W2': _L0_xattn_in['W2'], 'L0_xattn_b2': _L0_xattn_in['b2'], 'L0_ffn_n1_w': _L0_ffn_in['n1_w'], 'L0_ffn_n2_w': _L0_ffn_in['n2_w'], 'L0_ffn_wq': _L0_ffn_in['wq'], 'L0_ffn_wk': _L0_ffn_in['wk'], 'L0_ffn_wv': _L0_ffn_in['wv'], 'L0_ffn_wo': _L0_ffn_in['wo'], 'L0_ffn_qn_w': _L0_ffn_in['qn_w'], 'L0_ffn_kn_w': _L0_ffn_in['kn_w'], 'L0_ffn_gate_w': _L0_ffn_in['gate_w'], 'L0_ffn_e0_up': _L0_ffn_in['e0_up'], 'L0_ffn_e0_down': _L0_ffn_in['e0_down'], 'L0_ffn_e1_w1': _L0_ffn_in['e1_w1'], 'L0_ffn_e1_w2': _L0_ffn_in['e1_w2'], 'L0_ffn_e1_down': _L0_ffn_in['e1_down'], 'L0_ffn_e2_l1': _L0_ffn_in['e2_l1'], 'L0_ffn_e2_l2': _L0_ffn_in['e2_l2'], 'L0_ffn_e2_l3': _L0_ffn_in['e2_l3'], 'L0_ffn_e2_l4': _L0_ffn_in['e2_l4'], 'L0_ffn_e3_down': _L0_ffn_in['e3_down'], 'L0_ffn_e3_up': _L0_ffn_in['e3_up'], 'L0_ffn_e3_out': _L0_ffn_in['e3_out']}

def reference(x, ctx_768, g_xattn, g_ffn, L0_xattn_Wq, L0_xattn_bq, L0_xattn_Wk, L0_xattn_bk, L0_xattn_Wv, L0_xattn_bv, L0_xattn_W1, L0_xattn_b1, L0_xattn_W2, L0_xattn_b2, L0_ffn_n1_w, L0_ffn_n2_w, L0_ffn_wq, L0_ffn_wk, L0_ffn_wv, L0_ffn_wo, L0_ffn_qn_w, L0_ffn_kn_w, L0_ffn_gate_w, L0_ffn_e0_up, L0_ffn_e0_down, L0_ffn_e1_w1, L0_ffn_e1_w2, L0_ffn_e1_down, L0_ffn_e2_l1, L0_ffn_e2_l2, L0_ffn_e2_l3, L0_ffn_e2_l4, L0_ffn_e3_down, L0_ffn_e3_up, L0_ffn_e3_out):
    import jax
    import jax.numpy as jnp

    def _L0_xattn_ref(x, y, Wq, bq, Wk, bk, Wv, bv, W1, b1, W2, b2):
        import jax, jax.numpy as jnp
        import numpy as np
        IMAGE_DIM = 128
        TEXT_DIM = 96
        NUM_HEADS = 16
        HEAD_DIM = IMAGE_DIM // NUM_HEADS
        B, N, _ = x.shape
        M = y.shape[1]
        q = (x @ Wq + bq).reshape(B, N, NUM_HEADS, HEAD_DIM)
        k = (y @ Wk + bk).reshape(B, M, NUM_HEADS, HEAD_DIM)
        v = (y @ Wv + bv).reshape(B, M, NUM_HEADS, HEAD_DIM)
        scale = 1.0 / np.sqrt(HEAD_DIM)
        scores = jnp.einsum('bnhd,bmhd->bhnm', q, k) * scale
        attn = jax.nn.softmax(scores, axis=-1)
        out = jnp.einsum('bhnm,bmhd->bnhd', attn, v).reshape(B, N, IMAGE_DIM)
        h = jax.nn.relu(out @ W1 + b1)
        return h @ W2 + b2

    def _L0_ffn_ref(x, n1_w, n2_w, wq, wk, wv, wo, qn_w, kn_w, gate_w, e0_up, e0_down, e1_w1, e1_w2, e1_down, e2_l1, e2_l2, e2_l3, e2_l4, e3_down, e3_up, e3_out):
        import jax, jax.numpy as jnp
        import numpy as np
        DIM = 128
        HEADS = 16
        HD = DIM // HEADS
        M = 32
        E = 4
        K = 2
        HID = 256
        MID = 256
        LB = 0.01
        EPS = 1.1920929e-07

        def _rms(x, w):
            return x * jax.lax.rsqrt(jnp.mean(x * x, axis=-1, keepdims=True) + EPS) * w

        def _gelu(x):
            return jax.nn.gelu(x, approximate=False)
        B, T, C = x.shape
        h = _rms(x, n1_w)
        heads = lambda w_: (h @ w_.T).reshape(B, T, HEADS, HD).transpose(0, 2, 1, 3)
        q = _rms(heads(wq), qn_w)
        k = _rms(heads(wk), kn_w)
        v = heads(wv)
        scores = jnp.einsum('bhqd,bhkd->bhqk', q, k) * HD ** (-0.5)
        causal = jnp.tril(jnp.ones((T, T), bool))
        scores = jnp.where(causal[None, None], scores, -jnp.inf)
        attn = jax.nn.softmax(scores, axis=-1)
        ao = jnp.einsum('bhqk,bhkd->bhqd', attn, v).transpose(0, 2, 1, 3).reshape(B, T, C) @ wo.T
        ao = ao.at[:, :, :M].set(0.0)
        x = x + ao
        xf = _rms(x, n2_w).reshape(-1, C)
        N = xf.shape[0]
        logits = jnp.nan_to_num(xf @ gate_w.T)
        probs = jax.nn.softmax(logits, axis=-1)
        topv, topi = jax.lax.top_k(probs, K)
        topv = topv / (topv.sum(-1, keepdims=True) + 1e-08)
        wts = jnp.zeros((N, E), x.dtype).at[jnp.arange(N)[:, None], topi].add(topv)
        o0 = _gelu(xf @ e0_up.T) @ e0_down.T
        o1 = jax.nn.silu(xf @ e1_w1.T) * (xf @ e1_w2.T) @ e1_down.T
        o2 = _gelu(_gelu(_gelu(xf @ e2_l1.T) @ e2_l2.T) @ e2_l3.T) @ e2_l4.T
        o3 = _gelu(_gelu(xf @ e3_down.T) @ e3_up.T) @ e3_out.T
        moe = wts[:, 0:1] * o0 + wts[:, 1:2] * o1 + wts[:, 2:3] * o2 + wts[:, 3:4] * o3
        moe = moe.reshape(B, T, C).at[:, :, :M].set(0.0)
        return x + moe
    x = x + jnp.tanh(g_xattn[0]) * _L0_xattn_ref(_layernorm(x, axis=-1), ctx_768, L0_xattn_Wq, L0_xattn_bq, L0_xattn_Wk, L0_xattn_bk, L0_xattn_Wv, L0_xattn_bv, L0_xattn_W1, L0_xattn_b1, L0_xattn_W2, L0_xattn_b2)
    x = x + jnp.tanh(g_ffn[0]) * _L0_ffn_ref(_layernorm(x, axis=-1), L0_ffn_n1_w, L0_ffn_n2_w, L0_ffn_wq, L0_ffn_wk, L0_ffn_wv, L0_ffn_wo, L0_ffn_qn_w, L0_ffn_kn_w, L0_ffn_gate_w, L0_ffn_e0_up, L0_ffn_e0_down, L0_ffn_e1_w1, L0_ffn_e1_w2, L0_ffn_e1_down, L0_ffn_e2_l1, L0_ffn_e2_l2, L0_ffn_e2_l3, L0_ffn_e2_l4, L0_ffn_e3_down, L0_ffn_e3_up, L0_ffn_e3_out)
    return x

_drawn_inputs = setup_inputs


def setup_inputs(seed=0):
    import zlib

    import numpy as np

    out = dict(_drawn_inputs(seed))
    spreads = {'L0_ffn_n1_w': (1.0, 0.2),
     'L0_ffn_n2_w': (1.0, 0.2),
     'L0_ffn_qn_w': (1.0, 0.6),
     'L0_ffn_kn_w': (1.0, 0.6)}
    factors = {'L0_xattn_bq': 3.589,
     'L0_xattn_bk': 64.0,
     'L0_ffn_e1_w1': 3.546,
     'L0_ffn_e1_w2': 3.544,
     'L0_ffn_e1_down': 3.515,
     'L0_ffn_e2_l1': 8.0,
     'L0_ffn_e2_l2': 8.0,
     'L0_ffn_e2_l3': 8.0,
     'L0_ffn_e2_l4': 8.0,
     'L0_ffn_e3_down': 7.605,
     'L0_ffn_e3_up': 7.57,
     'L0_ffn_e3_out': 7.509,
     'L0_ffn_e0_up': 8.0,
     'L0_ffn_e0_down': 8.0}
    for name, (base, spread) in spreads.items():
        noise = np.random.default_rng([zlib.crc32(name.encode()), seed]).standard_normal(out[name].shape)
        drawn = base * np.exp(spread * noise) if base else spread * noise
        out[name] = jnp.asarray(drawn.astype(out[name].dtype))
    for name, factor in factors.items():
        out[name] = (out[name] * factor).astype(out[name].dtype)
    return out
```

```python
from contextlib import ExitStack

import numpy as np

import concourse.bass as bass
from concourse import mybir

F32 = mybir.dt.float32
BF16 = mybir.dt.bfloat16
I32 = mybir.dt.int32
ALU = mybir.AluOpType
ACT = mybir.ActivationFunctionType
AX_X = mybir.AxisListType.X

P = 128
BATCHES, TOKENS, DIM = 64, 128, 128
CTX, TEXT = 77, 96
HEADS, HD = 16, 8
HID, EXPERTS, MASKED = 256, 4, 32
KEPT = DIM - MASKED
GB = 4
GROUPS = BATCHES // GB
GT = GB * TOKENS
SLOTS = 6
ROWS = 64
USED = SLOTS * HD
PAIRS = HEADS // 2
UNITS = 4
LN_EPS, RMS_EPS = 1e-5, 1.1920929e-07
BIG = 3.4028234663852886e38
SCALE = float(HD) ** -0.5
RSQRT_SEED = 0x5F3759DF

Q_FIRST, Q_SECOND, Q_THIRD = (0, 3, 1), (3, 5, 1), (5, 6, 1)
K_FIRST, K_SECOND, K_THIRD = (1, 6, 2), (2, 5, 2), (0, 1, 1)


def head_of(u, i):
    return 8 * (u // 2) + u % 2 + 2 * i


HEAD_ORDER = [head_of(u, i) for u in range(UNITS) for i in range(4)]

EARLY = [("wq", 128), ("wk", 128), ("wv", 128), ("bq", 128), ("bk", 128), ("bv", 128), ("w1", 256),
         ("w2", 256), ("b1", 2), ("b2", 128), ("gx", 1), ("gf", 1), ("ident", 128)]
LATE = [("n1w", 1), ("n2w", 1), ("qnw", 128), ("knw", 128), ("wqkv", 384), ("wo", KEPT), ("gate", 4),
        ("before", 16), ("e0_up", 256), ("e0_down", 2 * KEPT), ("e1_w1", 256), ("e1_w2", 256),
        ("e1_down", 2 * KEPT), ("e2_l1", 256), ("e2_l2", 512), ("e2_l3", 512), ("e2_l4", 2 * KEPT),
        ("e3_down", 128), ("e3_up", 256), ("e3_out", 2 * KEPT)]
CONSTS = [("ident", 128), ("causal", 4 * P), ("pick", 8 * P)]


def columns(parts):
    at, out = 0, {}
    for name, n in parts:
        out[name] = (at, at + n)
        at += n
    return out, at



def attention_steps():
    steps = []
    for b in range(2):
        steps += [("stq", b), ("stk", b)]
    steps += [("s1", 0, u) for u in range(UNITS)]
    steps += [("stq", 2), ("stk", 2)]
    steps += [("s1", 1, u) for u in range(UNITS)]
    steps += [("nmT", 0)] + [("s2", 0, u) for u in range(UNITS)]
    steps += [("stq", 3), ("stk", 3)]
    steps += [("s1", 2, u) for u in range(UNITS)]
    steps += [("nmT", 1)] + [("s2", 1, u) for u in range(UNITS)]
    steps += [("pv", 0)]
    steps += [("s1", 3, u) for u in range(UNITS)]
    steps += [("nmT", 2), ("bt", 0)] + [("s2", 2, u) for u in range(UNITS)]
    steps += [("pv", 1)]
    steps += [("nmT", 3), ("bt", 1)] + [("s2", 3, u) for u in range(UNITS)]
    steps += [("pv", 2), ("bt", 2), ("pv", 3), ("bt", 3)]
    return steps


X_STEPS = [("ln",), ("xk",), ("xv",), ("xnT",), ("xq",), ("split",)] + attention_steps() + \
    [("oT",), ("w1", 0), ("w1", 1), ("w2",)]
S_STEPS = [("ln",), ("hT",), ("qk", 0), ("qk", 1), ("v",), ("qkn",), ("split",)] + attention_steps() + \
    [("oT",), ("wo",), ("xf",), ("xfT",), ("gate",)]
M_STEPS = [("e3", "down", 0), ("e0", "up", 0), ("e0", "up", 1), ("e2", "l1", 0), ("e2", "l1", 1),
           ("e3", "up", 0), ("e3", "up", 1), ("e2", "l2", 0), ("e2", "l2", 1), ("e0", "out"),
           ("e2", "l3", 0), ("e2", "l3", 1), ("e3", "out"), ("e1", "w1", 0), ("e1", "w2", 0),
           ("e1", "w1", 1), ("e1", "w2", 1), ("e2", "out"), ("e1", "out")]
OFFSET = {"X": 0, "S": 1, "M": 2}
LAST = GROUPS + 1
LOOP = (3, GROUPS)


def merged():
    spans = {"X": (0.02, 1.0), "S": (0.0, 0.97), "M": (0.0, 0.5)}
    out = []
    for order, (stage, steps) in enumerate((("M", M_STEPS), ("S", S_STEPS), ("X", X_STEPS))):
        a, b = spans[stage]
        for n, s in enumerate(steps):
            out.append((a + (b - a) * n / (len(steps) - 1), order, n, stage, s))
    return [(stage, s) for _, _, _, stage, s in sorted(out)]


STEPS = merged()
RINGS = {"scores": [0, 1, 2], "mixed": [3, 4, 5], "experts": [6, 7]}


def ring_of(stage, step):
    if step[0] in ("ln", "split", "qkn", "xf"):
        return None
    if stage == "M":
        return "experts"
    return "scores" if step[0] in ("s1", "s2") else "mixed"


def place_banks():
    bank, seen = {}, {r: 0 for r in RINGS}
    for stage, step in STEPS:
        r = ring_of(stage, step)
        if r:
            bank[stage, step] = RINGS[r][seen[r] % len(RINGS[r])]
            seen[r] += 1
    return bank


BANK = place_banks()

PER = {"x_load": 16, "y_load": 16, "x_ln": 21, "x_xn": 5, "x_p1": 2, "x_r": 2, "x_p2": 2, "x_p3": 2,
       "x_nm": 8, "x_rc": 4, "s_ln": 37, "s_h": 8, "s_sq": 1, "s_qn": 16, "s_p1": 2, "s_r": 2,
       "s_p2": 2, "s_p3": 2, "s_nm": 8, "s_rc": 4, "s_pm": 16, "s_ss": 4, "s_r3": 12, "s_xf": 4,
       "s_F": 1, "s_g": 21, "s_ge": 1, "store": 16}


def active(stage, t):
    return 0 <= t - OFFSET[stage] < GROUPS


def uses_before(bank, t):
    return sum(1 for tt in range(t) for key, k in BANK.items() if k == bank and active(key[0], tt))


PER_ITERATION = {k: sum(1 for v in BANK.values() if v == k) for k in range(8)}
USES_BEFORE = {(k, t): uses_before(k, t) for k in range(8) for t in range(LAST + 1)}


class Now:

    def __init__(self, t, reg=None):
        self.t, self.reg = t, reg

    def group(self, stage):
        g = self.t - OFFSET[stage]
        return g if self.reg is None else self.reg + g

    def had(self, stage, back=1):
        return self.reg is not None or self.t - OFFSET[stage] - back >= 0

    def _count(self, per, first):
        return first if self.reg is None else self.reg * per + first

    def at(self, name, stage, k, back=0):
        g = self.t - OFFSET[stage] - back
        return None if g < 0 else self._count(PER[name], g * PER[name] + k)

    def use(self, stage, step, back=0):
        bank = BANK[stage, step]
        t = self.t - back
        if not active(stage, t):
            return None
        n = 1
        for key in STEPS:
            if key == (stage, step):
                break
            n += BANK.get(key) == bank and active(key[0], t)
        return self._count(PER_ITERATION[bank], USES_BEFORE[bank, t] + n)


class Chain:

    def __init__(self, sems, name, now, stage):
        self.sem, self.name, self.now, self.stage, self.k = sems[name], name, now, stage, 0

    def next(self):
        self.k += 1
        return self.value()

    def value(self):
        return self.now.at(self.name, self.stage, self.k)

    def end(self):
        assert self.k == PER[self.name], (self.name, self.k)


def gated_block(nc, x, ctx_t, early, late, consts, out):
    E_AT, E_N = columns(EARLY)
    L_AT, L_N = columns(LATE)
    C_AT, C_N = columns(CONSTS)
    with ExitStack() as ctx:
        def sb(name, shape, dt=F32):
            return ctx.enter_context(nc.sbuf_tensor(name, shape, dt))

        banks = [ctx.enter_context(nc.psum_tensor(f"bank{k}", [P, 512], F32)) for k in range(8)]
        filled = [ctx.enter_context(nc.semaphore(f"filled{k}")) for k in range(8)]
        emptied = [ctx.enter_context(nc.semaphore(f"emptied{k}")) for k in range(8)]
        sems = {name: ctx.enter_context(nc.semaphore(name)) for name in PER}
        early_in = ctx.enter_context(nc.semaphore("early_in"))
        late_in = ctx.enter_context(nc.semaphore("late_in"))
        consts_in = ctx.enter_context(nc.semaphore("consts_in"))
        cleared = ctx.enter_context(nc.semaphore("cleared"))
        setup = ctx.enter_context(nc.semaphore("setup"))
        passed = ctx.enter_context(nc.semaphore("passed"))
        gates = ctx.enter_context(nc.semaphore("gates"))

        ew = sb("ew", [P, E_N])
        lw = sb("lw", [P, L_N])
        cw = sb("cw", [P, C_N], BF16)

        def e_(name):
            return ew[:, E_AT[name][0]:E_AT[name][1]]

        def l_(name):
            return lw[:, L_AT[name][0]:L_AT[name][1]]

        def c_(name):
            return cw[:, C_AT[name][0]:C_AT[name][1]]

        tg = sb("tg", [P, 2])
        b2g = sb("b2g", [P, DIM])
        qkw = sb("qkw", [P, DIM])
        x_in = sb("x_in", [P, GB, DIM])
        yT = sb("yT", [TEXT, GB, CTX])
        x_stat, x_mv = sb("x_stat", [P, GB, 6]), sb("x_mv", [P, GB, 2])
        x_small = sb("x_small", [P, 6, GB])
        xn, xb, xnT = sb("xn", [P, GB, DIM]), sb("xb", [P, GB, DIM]), sb("xnT", [P, GT])
        nat = {(s, o): sb(f"nat{s}{o}", [P, GT]) for s in "XS" for o in "qk"}
        rest = nat
        part = {(s, o): sb(f"part{s}{o}", [P, GB * HEADS, 8, HD], BF16) for s in "XS" for o in "qk"}
        stackT = {(s, o): sb(f"stackT{s}{o}", [P, GB, PAIRS, TOKENS if (s, o) != ("X", "k") else CTX], BF16)
                  for s in "XS" for o in "qk"}
        v_nat = {"X": sb("v_x", [CTX, GB, HEADS, 32]), "S": sb("v_s", [P, GB, HEADS, 32])}
        nmax = {s: sb(f"nmax{s}", [P, GB, HEADS]) for s in "XS"}
        nmax_parts = {s: sb(f"nmax_parts{s}", [P, GB, 2, 64], BF16) for s in "XS"}
        nmaxT = {s: sb(f"nmaxT{s}", [P, GB, TOKENS], BF16) for s in "XS"}
        prob = {"X": sb("prob_x", [CTX, 2, UNITS, 512]), "S": sb("prob_s", [P, 2, UNITS, 512])}
        qkr, sq = (prob["S"][:, n, 0:2, :].rearrange("p u (a o d) -> p (u a) o d", a=2, o=2) for n in range(2))
        raw = {s: sb(f"raw{s}", [P, 512]) for s in "XS"}
        rsum = {s: sb(f"rsum{s}", [P, GB, HEADS]) for s in "XS"}
        att = {s: sb(f"att{s}", [P, GB, DIM]) for s in "XS"}
        attT = {s: sb(f"attT{s}", [P, GT]) for s in "XS"}
        hx = sb("hx", [P, 2, GT])
        x2 = sb("x2", [P, GB, DIM])
        s_stat, s_mv = sb("s_stat", [P, GB, 6]), sb("s_mv", [P, GB, 2])
        s_small = sb("s_small", [P, 12, GB])
        hn, xl, hT = sb("hn", [P, GB, DIM]), sb("xl", [P, GB, DIM]), sb("hT", [P, GT])
        ssq, qk_small = sb("ssq", [P, P]), sb("qk_small", [P, 4, P])
        ss3, r3_small = sb("ss3", [P, GB]), sb("r3_small", [P, 5, GB])
        xf = junk = hn
        g_eq = sb("g_eq", [P, GB * EXPERTS], I32)
        g_val = sb("g_val", [P, 8, GB * EXPERTS])
        g_row = sb("g_row", [P, 6, GB])
        g_pair = sb("g_pair", [P, 2, GB, EXPERTS, EXPERTS])
        xfT = sb("xfT", [P, GT])
        wts = sb("wts", [P, GB * EXPERTS])
        fin = sb("fin", [P, GB, DIM])
        act = {n: sb(f"act_{n}", [P, 2, GT]) for n in ("e0", "e2a", "e2b", "e3")}
        act["e1"] = act["e0"]
        act["e2c"] = act["e2a"]
        e3d = sb("e3d", [P, GT])
        silu = act["e2b"]

        def bank_of(stage, step):
            return banks[BANK[stage, step]]

        def bank16(stage, step):
            return banks[BANK[stage, step]][:].bitcast(BF16)

        made = {key: filled[k] for key, k in BANK.items()}
        taken = {key: emptied[k] for key, k in BANK.items()}

        def waits_alone(eng):
            eng.sem_inc(passed, 1)

        def run(eng, emit):
            def iteration(now):
                for stage, step in STEPS:
                    if now.reg is not None or active(stage, now.t):
                        emit(now, stage, step)

            for t in range(LOOP[0]):
                iteration(Now(t))
            with eng.Fori(0, LOOP[1] - LOOP[0]) as reg:
                iteration(Now(LOOP[0], reg))
            for t in range(LOOP[1], LAST + 1):
                iteration(Now(t))

        block = ctx.enter_context(nc.Block())

        @block.sync
        def _(sp):
            sp.dma_start(ew[:], early).then_inc(early_in, 16)
            sp.dma_start(cw[:], consts).then_inc(consts_in, 16)

            def emit(now, stage, step):
                if (stage, step) == ("X", ("ln",)):
                    g = now.group("X")
                    if now.had("X"):
                        sp.wait_ge(sems["x_xn"], now.at("x_xn", "X", 5, back=1))
                    sp.dma_start(x_in[:].rearrange("p b d -> p (b d)"),
                                 x[:, bass.ds(g * GT, GT)]).then_inc(sems["x_load"], 16)
                    if now.had("X"):
                        sp.wait_ge(made["X", ("xv",)], now.use("X", ("xv",), back=1))
                    sp.dma_start(yT[:].rearrange("p b m -> p (b m)"),
                                 ctx_t[:, bass.ds(g * (GB * CTX), GB * CTX)]).then_inc(sems["y_load"], 16)
                    if now.t == 0:
                        sp.dma_start(lw[:], late).then_inc(late_in, 16)
                if (stage, step) == ("M", ("e1", "out")):
                    sp.wait_ge(taken["M", ("e1", "out")], now.use("M", ("e1", "out")))
                    sp.dma_start(out[:, bass.ds(now.group("M") * GT, GT)],
                                 fin[:].rearrange("p b d -> p (b d)")).then_inc(sems["store"], 16)

            run(sp, emit)
            sp.wait_ge(sems["store"], 16 * GROUPS)

        @block.gpsimd
        def _(pool):
            for s in "XS":
                for o in "qk":
                    pool.memset(part[s, o][:], 0.0).then_inc(cleared, 1)
                pool.memset(nmax_parts[s][:], 0.0).then_inc(cleared, 1)
                pool.memset(v_nat[s][:], 0.0).then_inc(cleared, 1)
            pool.wait_ge(cleared, 8)
            for s in "XS":
                pool.memset(v_nat[s][:, :, :, HD:HD + 1], 1.0).then_inc(cleared, 1)
            pool.wait_ge(setup, 2)

            def emit(now, stage, step):
                if (stage, step) == ("X", ("ln",)):
                    ch = Chain(sems, "x_xn", now, "X")
                    pool.wait_ge(sems["x_ln"], now.at("x_ln", "X", 21))
                    if now.had("X"):
                        pool.wait_ge(made["X", ("xnT",)], now.use("X", ("xnT",), back=1))
                    waits_alone(pool)
                    for b in range(GB):
                        pool.tensor_scalar(xn[:, b, :], x_in[:, b, :], x_small[:, 4, b:b + 1],
                                                   x_small[:, 5, b:b + 1], ALU.mult, ALU.add).then_inc(ch.sem, 1)
                        ch.next()
                    if now.had("X"):
                        pool.wait_ge(taken["X", ("w2",)], now.use("X", ("w2",), back=1))
                    pool.tensor_tensor(xb[:], x_in[:], b2g[:].unsqueeze(1).broadcast_to([P, GB, DIM]),
                                               ALU.add).then_inc(ch.sem, 1)
                    ch.next()
                    ch.end()
                if (stage, step) == ("S", ("ln",)):
                    ch = Chain(sems, "s_h", now, "S")
                    pool.wait_ge(sems["s_ln"], now.at("s_ln", "S", 37))
                    if now.had("S"):
                        pool.wait_ge(made["S", ("xfT",)], now.use("S", ("xfT",), back=1))
                    if now.had("S"):
                        pool.wait_ge(sems["s_F"], now.at("s_F", "S", 1, back=1))
                    waits_alone(pool)
                    for b in range(GB):
                        pool.tensor_scalar(hn[:, b, :], x2[:, b, :], s_small[:, 10, b:b + 1],
                                                   s_small[:, 11, b:b + 1], ALU.mult, ALU.add).then_inc(ch.sem, 1)
                        ch.next()
                    for b in range(GB):
                        pool.tensor_scalar(xl[:, b, :], x2[:, b, :], s_small[:, 4, b:b + 1],
                                                   s_small[:, 5, b:b + 1], ALU.mult, ALU.add).then_inc(ch.sem, 1)
                        ch.next()
                    ch.end()
                if stage == "S" and step[0] == "s2":
                    _, b, u = step
                    pool.wait_ge(taken["S", step], now.use("S", step))
                    waits_alone(pool)
                    pv = prob["S"][:, b % 2, u, :].rearrange("m (i n) -> m i n", i=4)
                    pool.affine_select(out=pv, in_=pv, compare_op=ALU.is_ge, fill=0.0, base=0,
                                       pattern=[[0, 4], [1, TOKENS]], channel_multiplier=-1
                                       ).then_inc(sems["s_pm"], 1)
                if (stage, step) == ("S", ("xf",)):
                    pool.wait_ge(sems["s_r3"], now.at("s_r3", "S", 12))
                    waits_alone(pool)
                    for b in range(GB):
                        pool.tensor_scalar(xf[:, b, :], xl[:, b, :], r3_small[:, 4, b:b + 1], None,
                                           ALU.mult).then_inc(sems["s_xf"], 1)

            run(pool, emit)

        @block.scalar
        def _(sc):
            sc.wait_ge(early_in, 16)
            sc.activation(tg[:], ew[:, E_AT["gx"][0]:E_AT["gf"][1]], ACT.Tanh).then_inc(gates, 1)
            sc.wait_ge(late_in, 16)

            def first_parts(now, stage, o, slots, src):
                n = CTX if (stage, o) == ("X", "k") else P
                a, b, c = slots
                k = b - a if c == 1 else len(range(a, b, c))
                return sc.activation(part[stage, o][0:n, :, a:b:c, :],
                                     src[0:n].rearrange("p (h d) -> p h d", d=HD).unsqueeze(2)
                                     .broadcast_to([n, GB * HEADS, k, HD]), ACT.Copy)

            def parts(now, stage):
                pre = stage.lower()
                if stage == "X":
                    sc.wait_ge(taken["X", ("xq",)], now.use("X", ("xq",)))
                    sc.wait_ge(taken["X", ("xk",)], now.use("X", ("xk",)))
                else:
                    sc.wait_ge(sems["s_qn"], now.at("s_qn", "S", 16))
                for o in "qk":
                    if now.had(stage):
                        sc.wait_ge(made[stage, (f"st{o}", GB - 1)], now.use(stage, (f"st{o}", GB - 1), back=1))
                if now.t == OFFSET[stage]:
                    sc.wait_ge(cleared, 10)
                for o in "qk":
                    first_parts(now, stage, o, Q_FIRST if o == "q" else K_FIRST, nat[stage, o][:]
                                ).then_inc(sems[f"{pre}_p1"], 1)
                for n, o in enumerate("qk"):
                    sc.wait_ge(sems[f"{pre}_r"], now.at(f"{pre}_r", stage, n + 1))
                    first_parts(now, stage, o, Q_SECOND if o == "q" else K_SECOND, rest[stage, o][:]
                                ).then_inc(sems[f"{pre}_p2"], 1)

            def emit(now, stage, step):
                kind = step[0]
                if ring_of(stage, step):
                    src = bank_of(stage, step)
                if stage == "X" and kind == "xnT":
                    sc.wait_ge(made[stage, step], now.use(stage, step))
                    if now.had("X"):
                        sc.wait_ge(made["X", ("xq",)], now.use("X", ("xq",), back=1))
                    sc.copy(xnT[:], src[:]).then_inc(taken[stage, step], 1)
                elif kind == "split":
                    parts(now, stage)
                elif kind == "nmT":
                    b = step[1]
                    sc.wait_ge(made[stage, step], now.use(stage, step))
                    if now.had(stage):
                        sc.wait_ge(made[stage, ("s2", b, UNITS - 1)], now.use(stage, ("s2", b, UNITS - 1), back=1))
                    sc.copy(nmaxT[stage][:, b, :], bank16(stage, step)[:, 0:TOKENS]).then_inc(taken[stage, step], 1)
                elif kind == "s2":
                    b, u = step[1:]
                    n = CTX if stage == "X" else P
                    sc.wait_ge(made[stage, step], now.use(stage, step))
                    user, back = ("pv", (b - 2) % GB), int(b < 2)
                    if now.had(stage, back):
                        sc.wait_ge(made[stage, user], now.use(stage, user, back))
                    sc.activation(prob[stage][0:n, b % 2, u, :], src[0:n, :], ACT.Exp, scale=SCALE
                            ).then_inc(taken[stage, step], 1)
                elif kind == "pv":
                    sc.wait_ge(made[stage, step], now.use(stage, step))
                    b = step[1]
                    user, back = ("bt", (b - 1) % GB), int(b == 0)
                    if now.had(stage, back):
                        sc.wait_ge(made[stage, user], now.use(stage, user, back))
                    sc.copy(raw[stage][:], src[:]).then_inc(taken[stage, step], 1)
                elif kind == "oT":
                    sc.wait_ge(made[stage, step], now.use(stage, step))
                    if stage == "X":
                        if now.had("X"):
                            sc.wait_ge(made["X", ("w1", 1)], now.use("X", ("w1", 1), back=1))
                    else:
                        if now.had("S"):
                            sc.wait_ge(made["S", ("wo",)], now.use("S", ("wo",), back=1))
                    sc.copy(attT[stage][:], src[:]).then_inc(taken[stage, step], 1)
                elif stage == "X" and kind == "w1":
                    c = step[1]
                    sc.wait_ge(made[stage, step], now.use(stage, step))
                    if now.had("X"):
                        sc.wait_ge(made["X", ("w2",)], now.use("X", ("w2",), back=1))
                    sc.activation(hx[:, c, :], src[:], ACT.Relu,
                                        bias=e_("b1")[:, c:c + 1]).then_inc(taken[stage, step], 1)
                elif stage == "S" and kind == "hT":
                    sc.wait_ge(made[stage, step], now.use(stage, step))
                    if now.had("S"):
                        sc.wait_ge(made["S", ("v",)], now.use("S", ("v",), back=1))
                    sc.activation(hT[:], src[:], ACT.Identity, scale=l_("n1w")).then_inc(taken[stage, step], 1)
                elif stage == "S" and kind == "qk":
                    c = step[1]
                    sc.wait_ge(made[stage, step], now.use(stage, step))
                    if now.had("S"):
                        sc.wait_ge(made["S", ("pv", GB - 2)], now.use("S", ("pv", GB - 2), back=1))
                    sc.copy(qkr[:, 2 * c:2 * c + 2, :, :].rearrange("p b o d -> p (b o d)"), src[:]
                            ).then_inc(taken[stage, step], 1)
                elif stage == "S" and kind == "qkn":
                    sc.wait_ge(taken["S", ("qk", 0)], now.use("S", ("qk", 0)))
                    sc.wait_ge(taken["S", ("qk", 1)], now.use("S", ("qk", 1)))
                    sc.activation(sq[:], qkr[:], ACT.Square).then_inc(sems["s_sq"], 1)
                elif stage == "S" and kind == "v":
                    sc.wait_ge(made[stage, step], now.use(stage, step))
                    if now.had("S"):
                        sc.wait_ge(made["S", ("pv", GB - 1)], now.use("S", ("pv", GB - 1), back=1))
                    sc.copy(v_nat["S"][:, :, :, 0:HD],
                                  src[:].rearrange("p (b h d) -> p b h d", b=GB, h=HEADS)
                                          ).then_inc(taken[stage, step], 1)
                elif stage == "S" and kind == "xf":
                    sc.wait_ge(taken["S", ("wo",)], now.use("S", ("wo",)))
                    if now.had("S"):
                        sc.wait_ge(sems["s_r3"], now.at("s_r3", "S", 12, back=1))
                    if now.had("S"):
                        sc.wait_ge(sems["s_ss"], now.at("s_ss", "S", GB, back=1))
                    for b in range(GB):
                        sc.activation(junk[:, b, :], xl[:, b, :], ACT.Square,
                                      accum_out=ss3[:, b:b + 1]).then_inc(sems["s_ss"], 1)
                elif stage == "S" and kind == "xfT":
                    sc.wait_ge(made[stage, step], now.use(stage, step))
                    if now.reg is not None or active("M", now.t):
                        sc.wait_ge(made["M", ("e1", "w2", 1)], now.use("M", ("e1", "w2", 1)))
                    sc.activation(xfT[:], src[:], ACT.Identity, scale=l_("n2w")).then_inc(taken[stage, step], 1)
                elif stage == "S" and kind == "gate":
                    sc.wait_ge(sems["s_g"], now.at("s_g", "S", 6))
                    sc.activation(g_val[:, 3, :], g_val[:, 2, :], ACT.Exp).then_inc(sems["s_ge"], 1)
                elif stage == "M" and step[1] == "w1":
                    c = step[2]
                    sc.wait_ge(made[stage, step], now.use(stage, step))
                    if now.had("M"):
                        sc.wait_ge(taken["M", ("e1", "w2", c)], now.use("M", ("e1", "w2", c), back=1))
                    sc.activation(silu[:, c, :], src[:], ACT.Silu).then_inc(taken[stage, step], 1)
                elif stage == "M" and step[1] not in ("w2", "out"):
                    e, what, c = step
                    dst = {"e0up": (act["e0"], "out"), "e2l1": (act["e2a"], ("e2", "l2", 1)),
                           "e2l2": (act["e2b"], ("e2", "l3", 1)), "e2l3": (act["e2c"], "out"),
                           "e3up": (act["e3"], "out"), "e3down": (e3d, ("e3", "up", 1))}[e + what]
                    reader = (e, "out") if dst[1] == "out" else dst[1]
                    sc.wait_ge(made[stage, step], now.use(stage, step))
                    if now.had("M"):
                        sc.wait_ge(made["M", reader], now.use("M", reader, back=1))
                    o = e3d[:] if what == "down" else dst[0][:, c, :]
                    sc.activation(o, src[:], ACT.Gelu).then_inc(taken[stage, step], 1)

            run(sc, emit)

        @block.vector
        def _(dve):
            dve.wait_ge(early_in, 16)
            dve.wait_ge(late_in, 16)
            dve.wait_ge(gates, 1)
            dve.tensor_scalar(b2g[:], e_("b2"), tg[:, 0:1], None, ALU.mult).then_inc(setup, 1)
            dve.tensor_tensor(qkw[:], l_("qnw"), l_("knw"), ALU.mult).then_inc(setup, 1)
            dve.wait_ge(setup, 2)

            def rsqrt(ch, y, a, t1, t2):
                dve.tensor_scalar(t1.bitcast(I32), a.bitcast(I32), 1, None, ALU.logical_shift_right).then_inc(ch.sem, 1)
                dve.wait_ge(ch.sem, ch.next())
                dve.tensor_scalar(y.bitcast(I32), t1.bitcast(I32), -1.0, float(RSQRT_SEED),
                                          ALU.mult, ALU.add).then_inc(ch.sem, 1)
                dve.wait_ge(ch.sem, ch.next())
                for _ in range(3):
                    dve.scalar_tensor_tensor(out=t1, in0=y, scalar=-0.5, in1=y,
                                                     op0=ALU.mult, op1=ALU.mult).then_inc(ch.sem, 1)
                    dve.wait_ge(ch.sem, ch.next())
                    dve.tensor_tensor(t2, t1, a, ALU.mult).then_inc(ch.sem, 1)
                    dve.wait_ge(ch.sem, ch.next())
                    dve.scalar_tensor_tensor(out=y, in0=t2, scalar=1.5, in1=y,
                                                     op0=ALU.add, op1=ALU.mult).then_inc(ch.sem, 1)
                    dve.wait_ge(ch.sem, ch.next())

            def layer_norm(ch, src, stat, mv, small):
                for b in range(GB):
                    dve.bn_stats(stat[:, b, :], src[:, b, :]).then_inc(ch.sem, 1)
                    ch.next()
                dve.wait_ge(ch.sem, ch.value())
                waits_alone(dve)
                for b in range(GB):
                    dve.bn_aggr(mv[:, b, :], stat[:, b, :]).then_inc(ch.sem, 1)
                    ch.next()
                dve.wait_ge(ch.sem, ch.value())
                dve.tensor_scalar(small[:, 0, :], mv[:, :, 1], LN_EPS, None, ALU.add).then_inc(ch.sem, 1)
                dve.wait_ge(ch.sem, ch.next())
                rsqrt(ch, small[:, 4, :], small[:, 0, :], small[:, 1, :], small[:, 2, :])
                dve.scalar_tensor_tensor(out=small[:, 5, :], in0=mv[:, :, 0], scalar=-1.0,
                                                 in1=small[:, 4, :], op0=ALU.mult, op1=ALU.mult).then_inc(ch.sem, 1)
                dve.wait_ge(ch.sem, ch.next())

            def split(now, stage):
                pre = stage.lower()
                for n, o in enumerate("qk"):
                    rows = CTX if (stage, o) == ("X", "k") else P
                    one = Q_FIRST[0] if o == "q" else K_FIRST[0]
                    dve.wait_ge(sems[f"{pre}_p1"], now.at(f"{pre}_p1", stage, n + 1))
                    dve.tensor_tensor(rest[stage, o][0:rows].rearrange("p (h d) -> p h d", d=HD),
                                      nat[stage, o][0:rows].rearrange("p (h d) -> p h d", d=HD),
                                      part[stage, o][0:rows, :, one, :], ALU.subtract
                                      ).then_inc(sems[f"{pre}_r"], 1)
                for n, o in enumerate("qk"):
                    rows = CTX if (stage, o) == ("X", "k") else P
                    two = Q_SECOND[0] if o == "q" else K_SECOND[0]
                    three = Q_THIRD[0] if o == "q" else K_THIRD[0]
                    dve.wait_ge(sems[f"{pre}_p2"], now.at(f"{pre}_p2", stage, n + 1))
                    dve.tensor_tensor(part[stage, o][0:rows, :, three, :],
                                      rest[stage, o][0:rows].rearrange("p (h d) -> p h d", d=HD),
                                      part[stage, o][0:rows, :, two, :], ALU.subtract
                                      ).then_inc(sems[f"{pre}_p3"], 1)

            def emit(now, stage, step):
                kind = step[0]
                if ring_of(stage, step):
                    src = bank_of(stage, step)
                pre = stage.lower()
                if (stage, kind) == ("X", "ln"):
                    ch = Chain(sems, "x_ln", now, "X")
                    dve.wait_ge(sems["x_load"], now.at("x_load", "X", 16))
                    if now.had("X"):
                        dve.wait_ge(sems["x_xn"], now.at("x_xn", "X", 4, back=1))
                    layer_norm(ch, x_in, x_stat, x_mv, x_small)
                    ch.end()
                elif (stage, kind) == ("X", "xq") or (stage, kind) == ("X", "xk"):
                    o = kind[1]
                    rows = P if o == "q" else CTX
                    dve.wait_ge(made[stage, step], now.use(stage, step))
                    if now.had("X"):
                        dve.wait_ge(sems["x_p1"], now.at("x_p1", "X", 2, back=1))
                    dve.tensor_tensor(
                        nat["X", o][0:rows].rearrange("p (b c) -> p b c", b=GB),
                        src[0:rows].rearrange("p (b c) -> p b c", b=GB),
                        e_("b" + o)[0:rows].unsqueeze(1).broadcast_to([rows, GB, DIM]), ALU.add
                                ).then_inc(taken[stage, step], 1)
                elif (stage, kind) == ("X", "xv"):
                    dve.wait_ge(made[stage, step], now.use(stage, step))
                    if now.had("X"):
                        dve.wait_ge(made["X", ("pv", GB - 1)], now.use("X", ("pv", GB - 1), back=1))
                    if now.t == 0:
                        dve.wait_ge(cleared, 10)
                    dve.tensor_tensor(
                        v_nat["X"][:, :, :, 0:HD], src[0:CTX].rearrange("p (b h d) -> p b h d", b=GB, h=HEADS),
                        e_("bv")[0:CTX].rearrange("p (h d) -> p h d", h=HEADS).unsqueeze(1)
                        .broadcast_to([CTX, GB, HEADS, HD]), ALU.add).then_inc(taken[stage, step], 1)
                elif kind == "split":
                    split(now, stage)
                elif kind in ("stq", "stk"):
                    o, b = kind[2], step[1]
                    n = CTX if (stage, o) == ("X", "k") else TOKENS
                    dve.wait_ge(made[stage, step], now.use(stage, step))
                    if now.had(stage):
                        dve.wait_ge(made[stage, ("s2", b, UNITS - 1)], now.use(stage, ("s2", b, UNITS - 1), back=1))
                    dve.tensor_copy(
                        stackT[stage, o][:, b, :, :],
                        bank16(stage, step)[:, 0:PAIRS * (n + n % 2)]
                        .rearrange("p (j n) -> p j n", j=PAIRS)[:, :, 0:n]).then_inc(taken[stage, step], 1)
                elif kind == "s1":
                    _, b, u = step
                    n = CTX if stage == "X" else TOKENS
                    dve.wait_ge(made[stage, step], now.use(stage, step))
                    dve.tensor_reduce(nmax[stage][:, b, 4 * u:4 * u + 4],
                                            src[:, 0:4 * n].rearrange("p (i m) -> p i m", i=4), AX_X, ALU.max,
                                            negate=True).then_inc(taken[stage, step], 1)
                    if u == UNITS - 1:
                        dve.wait_ge(taken[stage, step], now.use(stage, step))
                        if now.had(stage):
                            dve.wait_ge(made[stage, ("nmT", b)], now.use(stage, ("nmT", b), back=1))
                        if now.t == OFFSET[stage] and b == 0:
                            dve.wait_ge(cleared, 10)
                        both = nmax[stage][:, b, :].unsqueeze(1).broadcast_to([P, 2, HEADS])
                        hi, lo = nmax_parts[stage][:, b, :, 0:16], nmax_parts[stage][:, b, :, 16:32]
                        dve.tensor_copy(hi, both).then_inc(sems[f"{pre}_nm"], 1)
                        dve.wait_ge(sems[f"{pre}_nm"], now.at(f"{pre}_nm", stage, 2 * b + 1))
                        dve.tensor_tensor(lo, both, hi, ALU.subtract).then_inc(sems[f"{pre}_nm"], 1)
                elif kind == "bt":
                    b = step[1]
                    dve.wait_ge(made[stage, step], now.use(stage, step))
                    if b == 0:
                        if now.had(stage):
                            dve.wait_ge(made[stage, ("oT",)], now.use(stage, ("oT",), back=1))
                    heads = src[:].rearrange("p (h c) -> p h c", c=32)
                    dve.reciprocal(rsum[stage][:, b, :], heads[:, :, HD]).then_inc(sems[f"{pre}_rc"], 1)
                    dve.wait_ge(sems[f"{pre}_rc"], now.at(f"{pre}_rc", stage, b + 1))
                    dve.tensor_tensor(att[stage][:, b, :].rearrange("p (h d) -> p h d", d=HD),
                                            heads[:, :, 0:HD],
                                            rsum[stage][:, b, :].unsqueeze(2).broadcast_to([P, HEADS, HD]),
                                            ALU.mult).then_inc(taken[stage, step], 1)
                elif (stage, kind) == ("X", "w2"):
                    dve.wait_ge(made[stage, step], now.use(stage, step))
                    dve.wait_ge(sems["x_xn"], now.at("x_xn", "X", 5))
                    if now.reg is not None or active("S", now.t):
                        dve.wait_ge(sems["s_F"], now.at("s_F", "S", 1))
                        dve.wait_ge(sems["s_h"], now.at("s_h", "S", 8))
                    dve.scalar_tensor_tensor(out=x2[:].rearrange("p b d -> p (b d)"), in0=src[:],
                                                   scalar=tg[:, 0:1], in1=xb[:].rearrange("p b d -> p (b d)"),
                                                   op0=ALU.mult, op1=ALU.add).then_inc(taken[stage, step], 1)
                elif (stage, kind) == ("S", "ln"):
                    ch = Chain(sems, "s_ln", now, "S")
                    if now.had("X"):
                        dve.wait_ge(taken["X", ("w2",)], now.use("X", ("w2",), back=1))
                    if now.had("S"):
                        dve.wait_ge(sems["s_h"], now.at("s_h", "S", 8, back=1))
                    layer_norm(ch, x2, s_stat, s_mv, s_small)
                    dve.tensor_tensor(s_small[:, 6, :], s_small[:, 4, :], s_small[:, 4, :], ALU.mult
                            ).then_inc(ch.sem, 1)
                    dve.wait_ge(ch.sem, ch.next())
                    dve.tensor_tensor(s_small[:, 7, :], s_small[:, 6, :], s_mv[:, :, 1], ALU.mult).then_inc(ch.sem, 1)
                    dve.wait_ge(ch.sem, ch.next())
                    dve.tensor_scalar(s_small[:, 8, :], s_small[:, 7, :], RMS_EPS, None, ALU.add).then_inc(ch.sem, 1)
                    dve.wait_ge(ch.sem, ch.next())
                    rsqrt(ch, s_small[:, 9, :], s_small[:, 8, :], s_small[:, 1, :], s_small[:, 2, :])
                    dve.tensor_tensor(s_small[:, 10, :], s_small[:, 4, :], s_small[:, 9, :], ALU.mult
                            ).then_inc(ch.sem, 1)
                    dve.wait_ge(ch.sem, ch.next())
                    dve.tensor_tensor(s_small[:, 11, :], s_small[:, 5, :], s_small[:, 9, :], ALU.mult
                            ).then_inc(ch.sem, 1)
                    dve.wait_ge(ch.sem, ch.next())
                    ch.end()
                elif (stage, kind) == ("S", "qkn"):
                    ch = Chain(sems, "s_qn", now, "S")
                    dve.wait_ge(sems["s_sq"], now.at("s_sq", "S", 1))
                    dve.wait_ge(taken["S", ("qk", 0)], now.use("S", ("qk", 0)))
                    dve.wait_ge(taken["S", ("qk", 1)], now.use("S", ("qk", 1)))
                    if now.had("S"):
                        dve.wait_ge(sems["s_p1"], now.at("s_p1", "S", 2, back=1))
                    dve.tensor_reduce(ssq[:], sq[:].rearrange("p b o (h d) -> p (b o h) d", d=HD),
                                              AX_X, ALU.add).then_inc(ch.sem, 1)
                    dve.wait_ge(ch.sem, ch.next())
                    dve.tensor_scalar(qk_small[:, 0, :], ssq[:], 1.0 / HD, RMS_EPS, ALU.mult, ALU.add
                            ).then_inc(ch.sem, 1)
                    dve.wait_ge(ch.sem, ch.next())
                    rsqrt(ch, qk_small[:, 3, :], qk_small[:, 0, :], qk_small[:, 1, :], qk_small[:, 2, :])
                    r = qk_small[:, 3, :].rearrange("p (b o h) -> p b o h", b=GB, o=2)
                    for n, o in enumerate("qk"):
                        dve.tensor_tensor(
                            nat["S", o][:].rearrange("p (b h d) -> p b h d", b=GB, h=HEADS),
                            qkr[:, :, n, :].rearrange("p b (h d) -> p b h d", h=HEADS),
                            r[:, :, n, :].unsqueeze(3).broadcast_to([P, GB, HEADS, HD]), ALU.mult).then_inc(ch.sem, 1)
                        dve.wait_ge(ch.sem, ch.next())
                    dve.tensor_tensor(nat["S", "q"][:].rearrange("p (b c) -> p b c", b=GB),
                                              nat["S", "q"][:].rearrange("p (b c) -> p b c", b=GB),
                                              qkw[:].unsqueeze(1).broadcast_to([P, GB, DIM]), ALU.mult
                                                      ).then_inc(ch.sem, 1)
                    dve.wait_ge(ch.sem, ch.next())
                    ch.end()
                elif (stage, kind) == ("S", "wo"):
                    dve.wait_ge(made[stage, step], now.use(stage, step))
                    dve.wait_ge(sems["s_h"], now.at("s_h", "S", 8))
                    dve.tensor_tensor(xl[:, :, MASKED:DIM],
                                            src[:, 0:GB * KEPT].rearrange("p (b c) -> p b c", b=GB),
                                            xl[:, :, MASKED:DIM], ALU.add).then_inc(taken[stage, step], 1)
                elif (stage, kind) == ("S", "xf"):
                    ch = Chain(sems, "s_r3", now, "S")
                    dve.wait_ge(sems["s_ss"], now.at("s_ss", "S", GB))
                    if now.had("S"):
                        dve.wait_ge(sems["s_xf"], now.at("s_xf", "S", GB, back=1))
                    dve.tensor_scalar(r3_small[:, 0, :], ss3[:], 1.0 / DIM, RMS_EPS, ALU.mult, ALU.add
                            ).then_inc(ch.sem, 1)
                    dve.wait_ge(ch.sem, ch.next())
                    rsqrt(ch, r3_small[:, 4, :], r3_small[:, 0, :], r3_small[:, 1, :], r3_small[:, 2, :])
                    ch.end()
                    dve.wait_ge(taken["S", ("wo",)], now.use("S", ("wo",)))
                    if now.reg is not None or active("M", now.t):
                        dve.wait_ge(sems["store"], now.at("store", "M", 16))
                    if now.had("S"):
                        dve.wait_ge(sems["s_xf"], now.at("s_xf", "S", GB, back=1))
                    dve.scalar_tensor_tensor(out=fin[:].rearrange("p b d -> p (b d)"),
                                             in0=xl[:].rearrange("p b d -> p (b d)"), scalar=tg[:, 1:2],
                                             in1=x2[:].rearrange("p b d -> p (b d)"), op0=ALU.mult,
                                             op1=ALU.add).then_inc(sems["s_F"], 1)
                elif (stage, kind) == ("S", "gate"):
                    ch = Chain(sems, "s_g", now, "S")
                    n = GB * EXPERTS

                    def v(k):
                        return g_val[:, k, :]

                    def rows(k):
                        return g_val[:, k, :].rearrange("p (b e) -> p b e", b=GB)

                    def over(k):
                        return g_row[:, k, :].unsqueeze(2).broadcast_to([P, GB, EXPERTS])

                    dve.wait_ge(made[stage, step], now.use(stage, step))
                    dve.tensor_copy(v(0), src[:, 0:n]).then_inc(taken[stage, step], 1)
                    dve.wait_ge(taken[stage, step], now.use(stage, step))
                    dve.tensor_tensor(g_eq[:], v(0), v(0), ALU.is_equal).then_inc(ch.sem, 1)
                    ch.next()
                    dve.tensor_scalar(v(1), v(0), -BIG, BIG, ALU.max, ALU.min).then_inc(ch.sem, 1)
                    ch.next()
                    dve.memset(v(2), 0.0).then_inc(ch.sem, 1)
                    dve.wait_ge(ch.sem, ch.next())
                    waits_alone(dve)
                    dve.copy_predicated(v(2), g_eq[:], v(1)).then_inc(ch.sem, 1)
                    dve.wait_ge(ch.sem, ch.next())
                    dve.tensor_reduce(g_row[:, 0, :], rows(2), AX_X, ALU.max, negate=True).then_inc(ch.sem, 1)
                    dve.wait_ge(ch.sem, ch.next())
                    dve.tensor_tensor(rows(2), rows(2), over(0), ALU.add).then_inc(ch.sem, 1)
                    dve.wait_ge(ch.sem, ch.next())
                    dve.wait_ge(sems["s_ge"], now.at("s_ge", "S", 1))
                    dve.tensor_reduce(g_row[:, 1, :], rows(3), AX_X, ALU.add).then_inc(ch.sem, 1)
                    dve.wait_ge(ch.sem, ch.next())
                    dve.reciprocal(g_row[:, 2, :], g_row[:, 1, :]).then_inc(ch.sem, 1)
                    dve.wait_ge(ch.sem, ch.next())
                    dve.tensor_tensor(rows(4), rows(3), over(2), ALU.mult).then_inc(ch.sem, 1)
                    dve.wait_ge(ch.sem, ch.next())
                    other = rows(4).unsqueeze(2).broadcast_to([P, GB, EXPERTS, EXPERTS])
                    own = rows(4).unsqueeze(3).broadcast_to([P, GB, EXPERTS, EXPERTS])
                    before = l_("before").rearrange("p (e f) -> p e f", e=EXPERTS).unsqueeze(1) \
                        .broadcast_to([P, GB, EXPERTS, EXPERTS])
                    dve.tensor_tensor(g_pair[:, 0], other, own, ALU.is_gt).then_inc(ch.sem, 1)
                    ch.next()
                    dve.tensor_tensor(g_pair[:, 1], other, own, ALU.is_equal).then_inc(ch.sem, 1)
                    dve.wait_ge(ch.sem, ch.next())
                    dve.tensor_tensor(g_pair[:, 1], g_pair[:, 1], before, ALU.mult).then_inc(ch.sem, 1)
                    dve.wait_ge(ch.sem, ch.next())
                    dve.tensor_tensor(g_pair[:, 0], g_pair[:, 0], g_pair[:, 1], ALU.add).then_inc(ch.sem, 1)
                    dve.wait_ge(ch.sem, ch.next())
                    dve.tensor_reduce(rows(5), g_pair[:, 0], AX_X, ALU.add).then_inc(ch.sem, 1)
                    dve.wait_ge(ch.sem, ch.next())
                    dve.tensor_scalar(v(6), v(5), 1.5, None, ALU.is_lt).then_inc(ch.sem, 1)
                    dve.wait_ge(ch.sem, ch.next())
                    dve.tensor_tensor(v(7), v(6), v(4), ALU.mult).then_inc(ch.sem, 1)
                    dve.wait_ge(ch.sem, ch.next())
                    dve.tensor_reduce(g_row[:, 3, :], rows(7), AX_X, ALU.add).then_inc(ch.sem, 1)
                    dve.wait_ge(ch.sem, ch.next())
                    dve.tensor_scalar(g_row[:, 4, :], g_row[:, 3, :], 1e-8, None, ALU.add).then_inc(ch.sem, 1)
                    dve.wait_ge(ch.sem, ch.next())
                    dve.reciprocal(g_row[:, 5, :], g_row[:, 4, :]).then_inc(ch.sem, 1)
                    dve.wait_ge(ch.sem, ch.next())
                    dve.tensor_tensor(rows(1), rows(7), over(5), ALU.mult).then_inc(ch.sem, 1)
                    dve.wait_ge(ch.sem, ch.next())
                    dve.tensor_scalar(wts[:], v(1), tg[:, 1:2], None, ALU.mult).then_inc(ch.sem, 1)
                    dve.wait_ge(ch.sem, ch.next())
                    ch.end()
                elif stage == "M" and step[1] == "w2":
                    c = step[2]
                    dve.wait_ge(made[stage, step], now.use(stage, step))
                    dve.wait_ge(taken["M", ("e1", "w1", c)], now.use("M", ("e1", "w1", c)))
                    if now.had("M"):
                        dve.wait_ge(made["M", ("e1", "out")], now.use("M", ("e1", "out"), back=1))
                    dve.tensor_tensor(act["e1"][:, c, :], src[:], silu[:, c, :], ALU.mult
                            ).then_inc(taken[stage, step], 1)
                elif stage == "M" and step[1] == "out":
                    e = int(step[0][1])
                    dve.wait_ge(made[stage, step], now.use(stage, step))
                    outs = [s for s in M_STEPS if s[1] == "out"]
                    at = outs.index(step)
                    if at:
                        dve.wait_ge(taken["M", outs[at - 1]], now.use("M", outs[at - 1]))
                    else:
                        dve.wait_ge(sems["s_F"], now.at("s_F", "M", 1))
                        dve.wait_ge(sems["s_g"], now.at("s_g", "M", PER["s_g"]))
                    for b in range(GB):
                        ins = dve.scalar_tensor_tensor(
                            out=fin[:, b, MASKED:DIM], in0=src[:, b * KEPT:(b + 1) * KEPT],
                            scalar=wts[:, b * EXPERTS + e:b * EXPERTS + e + 1], in1=fin[:, b, MASKED:DIM],
                            op0=ALU.mult, op1=ALU.add)
                    ins.then_inc(taken[stage, step], 1)

            run(dve, emit)

        @block.tensor
        def _(pe):
            pe.wait_ge(early_in, 16)
            pe.wait_ge(consts_in, 16)
            ident = e_("ident")
            ident16 = c_("ident")

            def latest(stage, step, *made):
                last = {}
                for key in sorted(made, key=STEPS.index):
                    if BANK[key] != BANK[stage, step]:
                        last[BANK[key]] = key
                return last.values()

            def transposes(dst, src, stage, step):
                for b in range(GB):
                    ins = pe.transpose(dst[:, b * P:(b + 1) * P], src[:, b, :], ident)
                ins.then_inc(made[stage, step], 1)

            def attention(now, stage, step):
                kind, b = step[0], step[1]
                dst = bank_of(stage, step)
                keys = CTX if stage == "X" else P
                pre = stage.lower()
                q, k = stackT[stage, "q"], stackT[stage, "k"]
                if kind in ("stq", "stk"):
                    o = kind[2]
                    n = keys if o == "k" else P
                    pe.wait_ge(sems[f"{pre}_p3"], now.at(f"{pre}_p3", stage, 1 + (o == "k")))
                    dst = bank16(stage, step)
                    for j in range(PAIRS):
                        h = b * HEADS + 2 * j
                        at = j * (n + n % 2)
                        ins = pe.transpose(dst[:, at:at + n],
                                           part[stage, o][0:n, h:h + 2, :, :].rearrange("p h s d -> p (h s d)"),
                                           ident16[0:n, 0:n])
                elif kind == "s1":
                    u = step[2]
                    for source in latest(stage, step, (stage, ("stq", b)), (stage, ("stk", b))):
                        pe.wait_ge(taken[source], now.use(*source))
                    if stage == "S":
                        pe.matmul(dst[:, :], ident16, c_("causal"), start=True, stop=False)
                    for i in range(4):
                        h = head_of(u, i)
                        r = ROWS * (h % 2)
                        ins = pe.matmul(dst[:, i * keys:(i + 1) * keys], q[r:r + USED, b, h // 2, :],
                                        k[r:r + USED, b, h // 2, :], start=stage == "X", stop=stage == "X" or i == 3)
                elif kind == "nmT":
                    pe.wait_ge(sems[f"{pre}_nm"], now.at(f"{pre}_nm", stage, 2 * b + 2))
                    ins = pe.transpose(bank16(stage, step)[:, 0:TOKENS],
                                       nmax_parts[stage][:, b, :, :].rearrange("p a c -> p (a c)"), ident16)
                elif kind == "s2":
                    u = step[2]
                    for source in latest(stage, step, (stage, ("nmT", b))):
                        pe.wait_ge(taken[source], now.use(*source))
                    for i in range(4):
                        h = head_of(u, i)
                        r = ROWS * (h % 2)
                        c = 4 * (u // 2) + i
                        pe.matmul(dst[0:keys, i * P:(i + 1) * P],
                                  c_("pick")[r:r + ROWS, c * P:c * P + keys],
                                  nmaxT[stage][r:r + ROWS, b, :], start=i == 0, stop=False)
                    for i in range(4):
                        h = head_of(u, i)
                        r = ROWS * (h % 2)
                        ins = pe.matmul(dst[0:keys, i * P:(i + 1) * P], k[r:r + USED, b, h // 2, :],
                                        q[r:r + USED, b, h // 2, :], start=False, stop=i == 3)
                elif kind == "pv":
                    if stage == "X":
                        for source in latest(stage, step, ("X", ("xv",)), *[("X", ("s2", b, u)) for u in range(UNITS)]):
                            pe.wait_ge(taken[source], now.use(*source))
                    else:
                        for source in latest(stage, step, ("S", ("v",))):
                            pe.wait_ge(taken[source], now.use(*source))
                        pe.wait_ge(sems["s_pm"], now.at("s_pm", "S", 4 * b + 4))
                    for u in range(UNITS):
                        for i in range(4):
                            ins = pe.matmul(dst[32 * i:32 * i + 32, u * P:(u + 1) * P],
                                            v_nat[stage][0:keys, b, head_of(u, i), :],
                                            prob[stage][0:keys, b % 2, u, i * P:(i + 1) * P],
                                            start=True, stop=True, skip_group_check=True)
                elif kind == "bt":
                    for source in latest(stage, step, (stage, ("pv", b))):
                        pe.wait_ge(taken[source], now.use(*source))
                    for u in range(UNITS):
                        ins = pe.transpose(dst[:, u * P:(u + 1) * P], raw[stage][:, u * P:(u + 1) * P], ident)
                ins.then_inc(made[stage, step], 1)

            def emit(now, stage, step):
                kind = step[0]
                if not ring_of(stage, step):
                    return
                n = now.use(stage, step)
                if now.reg is not None or n > 1:
                    pe.wait_ge(taken[stage, step], n - 1)
                dst = bank_of(stage, step)
                if stage != "M" and kind in ("stq", "stk", "s1", "nmT", "s2", "pv", "bt"):
                    attention(now, stage, step)
                elif (stage, kind) == ("X", "xnT"):
                    pe.wait_ge(sems["x_xn"], now.at("x_xn", "X", 4))
                    transposes(dst, xn, stage, step)
                elif (stage, kind) == ("X", "xq"):
                    for source in latest(stage, step, ("X", ("xnT",))):
                        pe.wait_ge(taken[source], now.use(*source))
                    for b in range(GB):
                        ins = pe.matmul(dst[:, b * P:(b + 1) * P], xnT[:, b * P:(b + 1) * P], e_("wq"),
                                        start=True, stop=True)
                    ins.then_inc(made[stage, step], 1)
                elif stage == "X" and kind in ("xk", "xv"):
                    pe.wait_ge(sems["y_load"], now.at("y_load", "X", 16))
                    for b in range(GB):
                        ins = pe.matmul(dst[0:CTX, b * P:(b + 1) * P], yT[:, b, :],
                                        e_("w" + kind[1])[0:TEXT], start=True, stop=True)
                    ins.then_inc(made[stage, step], 1)
                elif kind == "oT":
                    for source in latest(stage, step, *[(stage, ("bt", b)) for b in range(GB)]):
                        pe.wait_ge(taken[source], now.use(*source))
                    transposes(dst, att[stage], stage, step)
                elif (stage, kind) == ("X", "w1"):
                    c = step[1]
                    for source in latest(stage, step, ("X", ("oT",))):
                        pe.wait_ge(taken[source], now.use(*source))
                    pe.matmul(dst[:, :], e_("w1")[:, c * P:(c + 1) * P], attT["X"][:], start=True, stop=True
                            ).then_inc(made[stage, step], 1)
                elif (stage, kind) == ("X", "w2"):
                    for source in latest(stage, step, ("X", ("w1", 0)), ("X", ("w1", 1))):
                        pe.wait_ge(taken[source], now.use(*source))
                    for b in range(GB):
                        for c in range(2):
                            ins = pe.matmul(dst[:, b * P:(b + 1) * P], hx[:, c, b * P:(b + 1) * P],
                                            e_("w2")[:, c * P:(c + 1) * P], start=c == 0, stop=c == 1)
                    ins.then_inc(made[stage, step], 1)
                elif (stage, kind) == ("S", "hT"):
                    pe.wait_ge(sems["s_h"], now.at("s_h", "S", 4))
                    if now.t == OFFSET["S"]:
                        pe.wait_ge(late_in, 16)
                    transposes(dst, hn, stage, step)
                elif (stage, kind) == ("S", "qk"):
                    for source in latest(stage, step, ("S", ("hT",))):
                        pe.wait_ge(taken[source], now.use(*source))
                    for n in range(2):
                        b = 2 * step[1] + n
                        ins = pe.matmul(dst[:, n * 256:(n + 1) * 256], hT[:, b * P:(b + 1) * P],
                                        l_("wqkv")[:, 0:256], start=True, stop=True)
                    ins.then_inc(made[stage, step], 1)
                elif (stage, kind) == ("S", "v"):
                    for b in range(GB):
                        ins = pe.matmul(dst[:, b * P:(b + 1) * P], hT[:, b * P:(b + 1) * P],
                                        l_("wqkv")[:, 256:384], start=True, stop=True)
                    ins.then_inc(made[stage, step], 1)
                elif (stage, kind) == ("S", "wo"):
                    for source in latest(stage, step, ("S", ("oT",))):
                        pe.wait_ge(taken[source], now.use(*source))
                    for b in range(GB):
                        ins = pe.matmul(dst[:, b * KEPT:(b + 1) * KEPT], attT["S"][:, b * P:(b + 1) * P],
                                        l_("wo"), start=True, stop=True)
                    ins.then_inc(made[stage, step], 1)
                elif (stage, kind) == ("S", "xfT"):
                    pe.wait_ge(sems["s_xf"], now.at("s_xf", "S", GB))
                    transposes(dst, xf, stage, step)
                elif (stage, kind) == ("S", "gate"):
                    for source in latest(stage, step, ("S", ("xfT",))):
                        pe.wait_ge(taken[source], now.use(*source))
                    for b in range(GB):
                        ins = pe.matmul(dst[:, b * EXPERTS:(b + 1) * EXPERTS], xfT[:, b * P:(b + 1) * P],
                                        l_("gate"), start=True, stop=True)
                    ins.then_inc(made[stage, step], 1)
                elif stage == "M":
                    experts(now, step, dst)

            def experts(now, step, dst):
                e, what = step[0], step[1]
                if what == "out":
                    name = {"e0": "e0_down", "e1": "e1_down", "e2": "e2_l4", "e3": "e3_out"}[e]
                    src = {"e0": "e0", "e1": "e1", "e2": "e2c", "e3": "e3"}[e]
                    last = {"e0": "up", "e1": "w2", "e2": "l3", "e3": "up"}[e]
                    for source in latest("M", step, ("M", (e, last, 0)), ("M", (e, last, 1))):
                        pe.wait_ge(taken[source], now.use(*source))
                    for b in range(GB):
                        for c in range(2):
                            ins = pe.matmul(dst[:, b * KEPT:(b + 1) * KEPT], act[src][:, c, b * P:(b + 1) * P],
                                            l_(name)[:, c * KEPT:(c + 1) * KEPT], start=c == 0, stop=c == 1)
                    ins.then_inc(made["M", step], 1)
                    return
                c = step[2]
                if what in ("l2", "l3"):
                    src, prev = {"l2": ("e2a", "l1"), "l3": ("e2b", "l2")}[what]
                    for source in latest("M", step, ("M", ("e2", prev, 0)), ("M", ("e2", prev, 1))):
                        pe.wait_ge(taken[source], now.use(*source))
                    for k in range(2):
                        ins = pe.matmul(dst[:, :], l_(f"e2_{what}")[:, k * 256 + c * P:k * 256 + (c + 1) * P],
                                        act[src][:, k, :], start=k == 0, stop=k == 1)
                elif (e, what) == ("e3", "up"):
                    for source in latest("M", step, ("M", ("e3", "down", 0))):
                        pe.wait_ge(taken[source], now.use(*source))
                    ins = pe.matmul(dst[:, :], l_("e3_up")[:, c * P:(c + 1) * P], e3d[:], start=True, stop=True)
                else:
                    pe.wait_ge(taken["S", ("xfT",)], now.use("S", ("xfT",), back=1))
                    ins = pe.matmul(dst[:, :], l_(f"{e}_{what}")[:, c * P:(c + 1) * P], xfT[:],
                                    start=True, stop=True)
                ins.then_inc(made["M", step], 1)

            run(pe, emit)


def kernel(**inputs):
    import ml_dtypes
    import concourse.bacc as _bacc
    from concourse import mybir as _mybir
    from concourse.bass_utils import run_bass_kernel_spmd as _run

    a = {k: np.asarray(v) for k, v in inputs.items()}

    def rows(w):
        w = np.asarray(w)
        if w.shape[0] == 256:
            return np.concatenate([w[:128], w[128:]], axis=1)
        return np.concatenate([w, np.zeros((128 - w.shape[0], w.shape[1]), w.dtype)], axis=0)

    def every(row):
        return np.broadcast_to(row[None, :], (128, row.shape[0]))

    def by_head(w):
        return w.reshape(HEADS, HD, -1)[HEAD_ORDER].reshape(DIM, -1)

    x_, f_ = "L0_xattn_", "L0_ffn_"
    early = {
        "wq": a[x_ + "Wq"], "wk": rows(a[x_ + "Wk"]), "wv": rows(a[x_ + "Wv"]),
        "bq": every(a[x_ + "bq"]), "bk": every(a[x_ + "bk"]), "bv": every(a[x_ + "bv"]),
        "w1": by_head(a[x_ + "W1"]), "w2": rows(a[x_ + "W2"]), "b1": a[x_ + "b1"].reshape(2, 128).T,
        "b2": every(a[x_ + "b2"]), "gx": every(a["g_xattn"]), "gf": every(a["g_ffn"]),
        "ident": np.eye(128, dtype=np.float32),
    }
    late = {
        "n1w": a[f_ + "n1_w"][:, None], "n2w": a[f_ + "n2_w"][:, None],
        "qnw": every(np.tile(a[f_ + "qn_w"], HEADS)), "knw": every(np.tile(a[f_ + "kn_w"], HEADS)),
        "wqkv": np.concatenate([a[f_ + "wq"].T, a[f_ + "wk"].T, a[f_ + "wv"].T], axis=1),
        "wo": by_head(np.ascontiguousarray(a[f_ + "wo"].T[:, MASKED:])), "gate": a[f_ + "gate_w"].T,
        "before": every(np.tril(np.ones((EXPERTS, EXPERTS), np.float32), -1).ravel()),
        "e0_up": a[f_ + "e0_up"].T, "e0_down": rows(a[f_ + "e0_down"].T[:, MASKED:]),
        "e1_w1": a[f_ + "e1_w1"].T, "e1_w2": a[f_ + "e1_w2"].T, "e1_down": rows(a[f_ + "e1_down"].T[:, MASKED:]),
        "e2_l1": a[f_ + "e2_l1"].T, "e2_l2": rows(a[f_ + "e2_l2"].T), "e2_l3": rows(a[f_ + "e2_l3"].T),
        "e2_l4": rows(a[f_ + "e2_l4"].T[:, MASKED:]), "e3_down": a[f_ + "e3_down"].T,
        "e3_up": a[f_ + "e3_up"].T, "e3_out": rows(a[f_ + "e3_out"].T[:, MASKED:]),
    }
    pick = np.zeros((128, 8, 128), np.float32)
    for u in range(UNITS):
        for i in range(4):
            for part_row in (0, 16):
                pick[64 * (u % 2) + part_row + 4 * u + i, 4 * (u // 2) + i, :] = 1.0
    causal = np.where(np.arange(128)[None, :] <= np.arange(128)[:, None], 0.0, -1e30)
    consts = {"ident": np.eye(128), "causal": np.tile(causal, (1, 4)), "pick": pick.reshape(128, 1024)}

    def pack(parts, have, dtype):
        for name, n in parts:
            assert have[name].shape == (128, n), (name, have[name].shape)
        return np.ascontiguousarray(np.concatenate([have[name].astype(dtype, copy=False) for name, _ in parts], axis=1))

    arrays = {
        "x_rows": np.ascontiguousarray(a["x"].transpose(1, 0, 2).reshape(128, -1)),
        "ctx_cols": np.ascontiguousarray(a["ctx_768"].transpose(2, 0, 1).reshape(TEXT, -1)),
        "early": pack(EARLY, early, np.float32), "late": pack(LATE, late, np.float32),
        "consts": pack(CONSTS, consts, ml_dtypes.bfloat16),
    }
    nc = _bacc.Bacc("TRN2", target_bir_lowering=False, num_devices=1)
    args = [nc.dram_tensor(name, v.shape, _mybir.dt.from_np(v.dtype), kind="ExternalInput").ap()
            for name, v in arrays.items()]
    args.append(nc.dram_tensor("result", (128, BATCHES * DIM), F32, kind="ExternalOutput").ap())
    gated_block(nc, *args)
    r = _run(nc, [arrays], core_ids=[0])
    got = r.results[0]["result"]
    return np.ascontiguousarray(got.reshape(128, BATCHES, DIM).transpose(1, 0, 2))
```

```python
from contextlib import ExitStack

import numpy as np

import concourse.bass as bass
from concourse import mybir

F32 = mybir.dt.float32
BF16 = mybir.dt.bfloat16
I32 = mybir.dt.int32
ALU = mybir.AluOpType
ACT = mybir.ActivationFunctionType
AX_X = mybir.AxisListType.X

P = 128
BATCHES, TOKENS, DIM = 64, 128, 128
CTX, TEXT = 77, 96
HEADS, HD = 16, 8
HID, EXPERTS, MASKED = 256, 4, 32
KEPT = DIM - MASKED
GB = 4
GROUPS = BATCHES // GB
GT = GB * TOKENS
SLOTS = 6
ROWS = 64
USED = SLOTS * HD
PAIRS = HEADS // 2
UNITS = 4
LN_EPS, RMS_EPS = 1e-5, 1.1920929e-07
BIG = 3.4028234663852886e38
SCALE = float(HD) ** -0.5
RSQRT_SEED = 0x5F3759DF

Q_FIRST, Q_SECOND, Q_THIRD = (0, 3, 1), (3, 5, 1), (5, 6, 1)
K_FIRST, K_SECOND, K_THIRD = (1, 6, 2), (2, 5, 2), (0, 1, 1)


def head_of(u, i):
    return 8 * (u // 2) + u % 2 + 2 * i


HEAD_ORDER = [head_of(u, i) for u in range(UNITS) for i in range(4)]

EARLY = [("wq", 128), ("wk", 128), ("wv", 128), ("bq", 128), ("bk", 128), ("bv", 128), ("w1", 256),
         ("w2", 256), ("b1", 2), ("b2", 128), ("gx", 1), ("gf", 1), ("ident", 128)]
LATE = [("n1w", 1), ("n2w", 1), ("qnw", 128), ("knw", 128), ("wqkv", 384), ("wo", KEPT), ("gate", 4),
        ("before", 16), ("e0_up", 256), ("e0_down", 2 * KEPT), ("e1_w1", 256), ("e1_w2", 256),
        ("e1_down", 2 * KEPT), ("e2_l1", 256), ("e2_l2", 512), ("e2_l3", 512), ("e2_l4", 2 * KEPT),
        ("e3_down", 128), ("e3_up", 256), ("e3_out", 2 * KEPT)]
CONSTS = [("ident", 128), ("causal", 4 * P), ("pick", 8 * P)]


def columns(parts):
    at, out = 0, {}
    for name, n in parts:
        out[name] = (at, at + n)
        at += n
    return out, at



STEP = {}


def attention_steps(stage, at, before_q, before_k, before_v):
    keys = 0.6 if stage == "X" else 1.0
    begin, end = at

    def pace(b, part):
        return begin + (end - begin) * (b + part) / (GB + 2.319)

    def add(step, turns, before, share):
        STEP[stage, step] = (turns, [(stage, s) for s in before], share)

    for b in range(GB):
        add(("stk", b), [("PE", 0.5), ("DVE", 0.65 * keys)], [before_k], pace(b, 0.0))
        add(("stq", b), [("PE", 0.5), ("DVE", 0.65)], [before_q], pace(b, 0.1))
        for u in range(UNITS):
            add(("s1", b, u), [("PE", 0.15 + 0.3 * (stage == "S")), ("DVE", 0.65 * keys)],
                [("stk", b), ("stq", b)], pace(b, 0.3 + 0.15 * u))
        add(("nm", b), [("DVE", 0.3)], [("s1", b, UNITS - 1)], pace(b, 0.9))
        add(("nmT", b), [("PE", 0.1), ("ACT", 0.2)], [("nm", b)], pace(b, 1.162))
        for u in range(UNITS):
            add(("s2", b, u), [("PE", 0.5), ("ACT", 0.55 + 0.2 * (stage == "S"))], [("nmT", b)],
                pace(b, 1.111 + 0.11 * u))
            if stage == "S":
                add(("mask", b, u), [("POOL", 0.65)], [("s2", b, u)], pace(b, 1.111 + 0.11 * u))
        add(("pv", b), [("PE", 1.5), ("ACT", 0.55)],
            [("mask" if stage == "S" else "s2", b, u) for u in range(UNITS)] + [before_v], pace(b, 2.259))
        add(("bt", b), [("PE", 0.45), ("DVE", 0.45)], [("pv", b)], pace(b, 3.8))


def steps_of_x():
    def add(step, turns, before, share=0.0):
        STEP["X", step] = (turns, [("X", s) for s in before], share)

    add(("load",), [("SP", 4.0)], [])
    add(("ln",), [("DVE", 3.3)], [("load",)])
    add(("xn",), [("POOL", 2.6)], [("ln",)])
    add(("xk",), [("PE", 0.9), ("DVE", 0.65)], [("load",)])
    add(("p1", "k"), [("ACT", 1.4)], [("xk",)])
    add(("r", "k"), [("DVE", 0.65)], [("p1", "k")])
    add(("p2", "k"), [("ACT", 1.0)], [("r", "k")])
    add(("p3", "k"), [("DVE", 0.65)], [("p2", "k")])
    add(("xnT",), [("PE", 0.45), ("ACT", 0.6)], [("xn",)])
    add(("xq",), [("PE", 0.9), ("DVE", 0.65)], [("xnT",)])
    add(("p1", "q"), [("ACT", 1.4)], [("xq",), ("p1", "k")])
    add(("r", "q"), [("DVE", 0.65)], [("p1", "q"), ("r", "k")])
    add(("p2", "q"), [("ACT", 1.0)], [("r", "q"), ("p2", "k")])
    add(("p3", "q"), [("DVE", 0.65)], [("p2", "q"), ("p3", "k")])
    add(("xv",), [("PE", 0.9), ("DVE", 0.65)], [("load",)], 0.117)
    add(("xb",), [("POOL", 1.3)], [("xn",)], 0.3)
    attention_steps("X", PACE["X"], ("p3", "q"), ("p3", "k"), ("xv",))
    add(("oT",), [("PE", 0.45), ("ACT", 0.55)], [("bt", b) for b in range(GB)])
    add(("w1", 0), [("PE", 0.9), ("ACT", 0.6)], [("oT",)])
    add(("w1", 1), [("PE", 0.9), ("ACT", 0.6)], [("oT",), ("w1", 0)])
    add(("w2",), [("PE", 1.75), ("DVE", 0.7)], [("w1", 0), ("w1", 1), ("xb",)])


def steps_of_s():
    def add(step, turns, before, share=0.0):
        STEP["S", step] = (turns, [("S", s) for s in before], share)

    add(("ln",), [("DVE", 5.6)], [])
    add(("hn",), [("POOL", 2.6)], [("ln",)])
    add(("xl",), [("POOL", 4.2)], [("hn",)])
    add(("hT",), [("PE", 0.45), ("ACT", 0.6)], [("hn",)])
    add(("qk", 0), [("PE", 0.9), ("ACT", 0.55)], [("hT",)])
    add(("qk", 1), [("PE", 0.9), ("ACT", 0.55)], [("hT",), ("qk", 0)])
    add(("v",), [("PE", 0.9), ("ACT", 0.6)], [("hT",), ("qk", 1)])
    add(("sq",), [("ACT", 1.0)], [("qk", 0), ("qk", 1)])
    add(("qkn",), [("DVE", 6.1)], [("sq",)])
    add(("p1", "k"), [("ACT", 1.4)], [("qkn",)])
    add(("r", "k"), [("DVE", 0.65)], [("p1", "k")])
    add(("p1", "q"), [("ACT", 1.4)], [("p1", "k")])
    add(("p2", "k"), [("ACT", 1.0)], [("r", "k")])
    add(("r", "q"), [("DVE", 0.65)], [("p1", "q"), ("r", "k")])
    add(("p3", "k"), [("DVE", 0.65)], [("p2", "k")])
    add(("p2", "q"), [("ACT", 1.0)], [("r", "q"), ("p2", "k")])
    add(("p3", "q"), [("DVE", 0.65)], [("p2", "q"), ("p3", "k")])
    attention_steps("S", PACE["S"], ("p3", "q"), ("p3", "k"), ("v",))
    add(("oT",), [("PE", 0.45), ("ACT", 0.55)], [("bt", b) for b in range(GB)])
    add(("wo",), [("PE", 0.65), ("DVE", 0.5)], [("oT",), ("xl",)])
    add(("ss",), [("ACT", 1.1)], [("wo",)])
    add(("r3",), [("DVE", 1.5)], [("ss",)])
    add(("xf",), [("POOL", 2.8)], [("r3",)])
    add(("fin",), [("DVE", 0.7)], [("wo",), ("r3",)])
    add(("xfT",), [("PE", 0.45), ("ACT", 0.6)], [("xf",)])
    add(("gate",), [("PE", 0.1), ("DVE", 0.1)], [("xfT",)])
    add(("g1",), [("DVE", 1.0)], [("gate",)])
    add(("ge",), [("ACT", 0.2)], [("g1",)])
    add(("g2",), [("DVE", 2.1)], [("ge",)])


M_RUNS = [[("e3", "down", 0), ("e0", "up", 0), ("e0", "up", 1), ("e2", "l1", 0), ("e2", "l1", 1)],
          [("e3", "up", 0), ("e3", "up", 1), ("e2", "l2", 0), ("e2", "l2", 1)],
          [("e2", "l3", 0), ("e2", "l3", 1)],
          [("e1", "w1", 0), ("e1", "w1", 1)]]
M_OUTS = [("e0", "out"), ("e3", "out"), ("e2", "out"), ("e1", "out")]


def steps_of_m():
    before = {"e0up": [], "e1w1": [], "e1w2": [], "e2l1": [], "e3down": [],
              "e2l2": [("e2", "l1", 0), ("e2", "l1", 1)], "e2l3": [("e2", "l2", 0), ("e2", "l2", 1)],
              "e3up": [("e3", "down", 0)], "e0out": [("e0", "up", 0), ("e0", "up", 1)],
              "e3out": [("e3", "up", 0), ("e3", "up", 1)], "e2out": [("e2", "l3", 0), ("e2", "l3", 1)],
              "e1out": [("e1", "w2", 0), ("e1", "w2", 1)]}

    def add(step, turns, more, share=0.0):
        STEP["M", step] = (turns, [("M", s) for s in before[step[0] + step[1]] + more], share)

    last = None
    for n, steps in enumerate(M_RUNS):
        for m, step in enumerate(steps):
            first, final = m == 0, m == len(steps) - 1
            add(step, [("PE", 1.75 if step[1] in ("l2", "l3") else 0.9),
                       ("ACT", 0.55 + 1.35 * first + 1.35 * final)], [last] if last else [], M_PACE[n])
            last = step
        if n == 1:
            add(M_OUTS[0], [("PE", 1.7), ("DVE", 1.0)], [])
            add(M_OUTS[1], [("PE", 1.7), ("DVE", 1.0)], [M_OUTS[0]])
        if n == 2:
            add(M_OUTS[2], [("PE", 1.7), ("DVE", 1.0)], [M_OUTS[1]])
    for c in range(2):
        add(("e1", "w2", c), [("PE", 0.9), ("DVE", 0.65)], [("e1", "w1", c), ("e0", "out")], M_PACE[3])
    add(M_OUTS[3], [("PE", 1.7), ("DVE", 1.0)], [M_OUTS[2]])
    STEP["M", ("store",)] = ([("SP", 2.0)], [("M", M_OUTS[3])], 0.0)


AT = {"X": 0.0, "S": 0.264, "M": 0.073}
PERIOD = 112.263
PACE = {"X": (0.0, 0.441), "S": (0.0, 0.448)}
M_PACE = (0.0, 0.103, 0.413, 0.508)
CELL, HANDOVER = 0.05, 0.396
SLACK, PATIENCE = 20, 178
ENGINES = ("PE", "ACT", "DVE", "POOL", "SP")


def plan():
    cells, handover = round(PERIOD / CELL), round(HANDOVER / CELL)
    engine_used = {e: np.zeros(cells, bool) for e in ENGINES}
    bank_used = [np.zeros(cells, bool) for _ in range(8)]
    start, done, bank, last = {}, {}, {}, {}
    begin = {}

    def room(engine, at, need):
        if engine_used[engine][at % cells]:
            return None
        near = np.arange(at, at + need + SLACK)
        free = near[~engine_used[engine][near % cells]]
        return free[:need] if len(free) >= need else None

    def place(turns, stage, kind, t):
        out, now = [], t
        for n, (e, cost) in enumerate(turns):
            for u in range(now, now + (1 if n == 0 else PATIENCE)):
                taken = room(e, u, round(cost / CELL)) if u >= last.get((stage, kind, e), 0) else None
                if taken is not None:
                    break
            else:
                return None
            out.append((e, taken))
            now = int(taken[-1]) + 1 + handover
        if turns[0][0] != "PE":
            return out, None, now
        held = np.arange(t, now) % cells
        free = [k for k in range(8) if not bank_used[k][held].any()]
        if not free:
            return None
        before = np.arange(t - 1, t - cells, -1) % cells
        return out, max(free, key=lambda k: int(np.argmax(bank_used[k][before]))
                        if bank_used[k].any() else cells), now

    def turn(n_key):
        n, key = n_key
        own = [k for k in STEP if k[0] == key[0]]
        return (key[0] != "M", own.index(key) / len(own) if key[0] != "M" else 0, n)

    for _, (stage, step) in sorted(enumerate(STEP), key=turn):
        turns, before, share = STEP[stage, step]
        t = max([done[k] for k in before], default=round(AT[stage] * cells))
        begin.setdefault(stage, t)
        for t in range(max(t, begin[stage] + int(share * cells)), 20 * cells):
            found = place(turns, stage, step[0], t)
            if found:
                break
        else:
            raise ValueError(f"no room for {stage, step}")
        out, k, now = found
        for e, taken in out:
            engine_used[e][taken % cells] = True
            start[e, (stage, step)] = last[stage, step[0], e] = int(taken[0])
        if k is not None:
            bank[stage, step] = k
            bank_used[k][np.arange(t, now) % cells] = True
        done[stage, step] = now
    gap_s = done["X", ("w2",)] - start["DVE", ("S", ("ln",))]
    later_s = -(-gap_s // cells) * cells
    gap_m = later_s + max(done["S", ("xfT",)] - start["PE", ("M", M_RUNS[0][0])],
                          max(done["S", ("fin",)], done["S", ("g2",)]) - start["DVE", ("M", M_OUTS[0])])
    later = {"X": 0, "S": later_s, "M": -(-gap_m // cells) * cells}
    return {k: v + later[k[1][0]] for k, v in start.items()}, bank, cells


steps_of_m()
steps_of_x()
steps_of_s()
START, BANK, CELLS = plan()
LATE_BY = {k: v // CELLS for k, v in START.items()}
ORDER = {e: [key for _, key in sorted((v % CELLS, key) for (f, key), v in START.items() if f == e)]
         for e in ENGINES}
SPREAD = max(LATE_BY.values())
LAST = GROUPS + SPREAD - 1
LOOP = (SPREAD + 2, GROUPS)

PER = {"x_load": 16, "y_load": 16, "x_ln": 21, "x_xn": 5, "x_p1": 2, "x_r": 2, "x_p2": 2, "x_p3": 2,
       "x_nm": 8, "x_rc": 4, "s_ln": 37, "s_h": 9, "s_sq": 1, "s_qn": 16, "s_p1": 2, "s_r": 2,
       "s_p2": 2, "s_p3": 2, "s_nm": 8, "s_rc": 4, "s_pm": 16, "s_ss": 4, "s_r3": 12, "s_xf": 4,
       "s_F": 1, "s_g": 21, "s_ge": 1, "store": 16}


def active(engine, key, t):
    return 0 <= t - LATE_BY[engine, key] < GROUPS


PER_ITERATION = {k: sum(1 for v in BANK.values() if v == k) for k in range(8)}
USES_BEFORE = {(k, t): sum(1 for tt in range(t) for key in BANK if BANK[key] == k and active("PE", key, tt))
               for k in range(8) for t in range(LAST + 1)}


class Now:

    def __init__(self, t, reg, engine, key):
        self.t, self.reg, self.g = t, reg, t - LATE_BY[engine, key]

    def group(self):
        return self.g if self.reg is None else self.reg + self.g

    def had(self, back=1):
        return self.reg is not None or self.g - back >= 0

    def first(self):
        return self.reg is None and self.g == 0

    def at(self, name, k, back=0):
        first = (self.g - back) * PER[name] + k
        return first if self.reg is None else self.reg * PER[name] + first

    def use(self, stage, step, back=0):
        key, bank = (stage, step), BANK[stage, step]
        t = self.g - back + LATE_BY["PE", key]
        assert active("PE", key, t) and (self.reg is None or t >= SPREAD), (key, t, self.t)
        before = ORDER["PE"][:ORDER["PE"].index(key) + 1]
        n = USES_BEFORE[bank, t] + sum(1 for k in before if BANK.get(k) == bank and active("PE", k, t))
        return n if self.reg is None else self.reg * PER_ITERATION[bank] + n


class Chain:

    def __init__(self, sems, name, now, k=0):
        self.sem, self.name, self.now, self.k = sems[name], name, now, k

    def next(self):
        self.k += 1
        return self.value()

    def value(self):
        return self.now.at(self.name, self.k)

    def end(self):
        assert self.k == PER[self.name], (self.name, self.k)


def gated_block(nc, x, ctx_t, early, late, consts, out):
    E_AT, E_N = columns(EARLY)
    L_AT, L_N = columns(LATE)
    C_AT, C_N = columns(CONSTS)
    with ExitStack() as ctx:
        def sb(name, shape, dt=F32):
            return ctx.enter_context(nc.sbuf_tensor(name, shape, dt))

        banks = [ctx.enter_context(nc.psum_tensor(f"bank{k}", [P, 512], F32)) for k in range(8)]
        filled = [ctx.enter_context(nc.semaphore(f"filled{k}")) for k in range(8)]
        emptied = [ctx.enter_context(nc.semaphore(f"emptied{k}")) for k in range(8)]
        sems = {name: ctx.enter_context(nc.semaphore(name)) for name in PER}
        early_in = ctx.enter_context(nc.semaphore("early_in"))
        late_in = ctx.enter_context(nc.semaphore("late_in"))
        consts_in = ctx.enter_context(nc.semaphore("consts_in"))
        cleared = ctx.enter_context(nc.semaphore("cleared"))
        setup = ctx.enter_context(nc.semaphore("setup"))
        passed = ctx.enter_context(nc.semaphore("passed"))
        gates = ctx.enter_context(nc.semaphore("gates"))

        ew = sb("ew", [P, E_N])
        lw = sb("lw", [P, L_N])
        cw = sb("cw", [P, C_N], BF16)

        def e_(name):
            return ew[:, E_AT[name][0]:E_AT[name][1]]

        def l_(name):
            return lw[:, L_AT[name][0]:L_AT[name][1]]

        def c_(name):
            return cw[:, C_AT[name][0]:C_AT[name][1]]

        tg = sb("tg", [P, 2])
        b2g = sb("b2g", [P, DIM])
        qkw = sb("qkw", [P, DIM])
        x_in = sb("x_in", [P, GB, DIM])
        yT = sb("yT", [TEXT, GB, CTX])
        x_stat, x_mv = sb("x_stat", [P, GB, 6]), sb("x_mv", [P, GB, 2])
        x_small = sb("x_small", [P, 6, GB])
        xn, xb, xnT = sb("xn", [P, GB, DIM]), sb("xb", [P, GB, DIM]), sb("xnT", [P, GT])
        nat = {(s, o): sb(f"nat{s}{o}", [P, GT]) for s in "XS" for o in "qk"}
        rest = nat
        part = {(s, o): sb(f"part{s}{o}", [P, GB * HEADS, 8, HD], BF16) for s in "XS" for o in "qk"}
        stackT = {(s, o): sb(f"stackT{s}{o}", [P, GB, PAIRS, TOKENS if (s, o) != ("X", "k") else CTX], BF16)
                  for s in "XS" for o in "qk"}
        v_nat = {"X": sb("v_x", [CTX, GB, HEADS, 32]), "S": sb("v_s", [P, GB, HEADS, 32])}
        nmax = {s: sb(f"nmax{s}", [P, GB, HEADS]) for s in "XS"}
        nmax_parts = {s: sb(f"nmax_parts{s}", [P, GB, 2, 64], BF16) for s in "XS"}
        nmaxT = {s: sb(f"nmaxT{s}", [P, GB, TOKENS], BF16) for s in "XS"}
        prob = {"X": sb("prob_x", [CTX, 2, UNITS, 512]), "S": sb("prob_s", [P, 2, UNITS, 512])}
        qkr, sq = (prob["S"][:, n, 0:2, :].rearrange("p u (a o d) -> p (u a) o d", a=2, o=2) for n in range(2))
        raw = {s: sb(f"raw{s}", [P, 512]) for s in "XS"}
        rsum = {s: sb(f"rsum{s}", [P, GB, HEADS]) for s in "XS"}
        att = {s: sb(f"att{s}", [P, GB, DIM]) for s in "XS"}
        attT = {s: sb(f"attT{s}", [P, GT]) for s in "XS"}
        hx = sb("hx", [P, 2, GT])
        x2 = sb("x2", [P, GB, DIM])
        s_stat, s_mv = sb("s_stat", [P, GB, 6]), sb("s_mv", [P, GB, 2])
        s_small = sb("s_small", [P, 12, GB])
        x2s = sb("x2s", [P, GB, DIM])
        hn, xl, hT = sb("hn", [P, GB, DIM]), sb("xl", [P, GB, DIM]), sb("hT", [P, GT])
        ssq, qk_small = sb("ssq", [P, P]), sb("qk_small", [P, 4, P])
        ss3, r3_small = sb("ss3", [P, GB]), sb("r3_small", [P, 5, GB])
        xf = junk = hn
        g_eq = sb("g_eq", [P, GB * EXPERTS], I32)
        g_val = sb("g_val", [P, 8, GB * EXPERTS])
        g_row = sb("g_row", [P, 6, GB])
        g_pair = sb("g_pair", [P, 2, GB, EXPERTS, EXPERTS])
        xfT = sb("xfT", [P, GT])
        wts = sb("wts", [P, GB * EXPERTS])
        fin = sb("fin", [P, GB, DIM])
        act = {n: sb(f"act_{n}", [P, 2, GT]) for n in ("e0", "e2a", "e2b", "e3")}
        act["e1"] = act["e0"]
        act["e2c"] = act["e2a"]
        e3d = act["e2b"][:, 0, :]
        silu = act["e2b"]

        def bank_of(stage, step):
            return banks[BANK[stage, step]]

        def bank16(stage, step):
            return banks[BANK[stage, step]][:].bitcast(BF16)

        made = {key: filled[k] for key, k in BANK.items()}
        taken = {key: emptied[k] for key, k in BANK.items()}

        def waits_alone(eng):
            eng.sem_inc(passed, 1)

        def run(eng, name, emit):
            def iteration(t, reg=None):
                for key in ORDER[name]:
                    if reg is not None or active(name, key, t):
                        emit(Now(t, reg, name, key), *key)

            for t in range(LOOP[0]):
                iteration(t)
            with eng.Fori(0, LOOP[1] - LOOP[0]) as reg:
                iteration(LOOP[0], reg)
            for t in range(LOOP[1], LAST + 1):
                iteration(t)

        block = ctx.enter_context(nc.Block())

        @block.sync
        def _(sp):
            sp.dma_start(ew[:], early).then_inc(early_in, 16)
            sp.dma_start(cw[:], consts).then_inc(consts_in, 16)

            def emit(now, stage, step):
                if (stage, step) == ("X", ("load",)):
                    g = now.group()
                    if now.had():
                        sp.wait_ge(sems["x_xn"], now.at("x_xn", 5, back=1))
                    sp.dma_start(x_in[:].rearrange("p b d -> p (b d)"),
                                 x[:, bass.ds(g * GT, GT)]).then_inc(sems["x_load"], 16)
                    if now.had():
                        sp.wait_ge(made["X", ("xv",)], now.use("X", ("xv",), back=1))
                    sp.dma_start(yT[:].rearrange("p b m -> p (b m)"),
                                 ctx_t[:, bass.ds(g * (GB * CTX), GB * CTX)]).then_inc(sems["y_load"], 16)
                    if now.first():
                        sp.dma_start(lw[:], late).then_inc(late_in, 16)
                if (stage, step) == ("M", ("store",)):
                    sp.wait_ge(taken["M", ("e1", "out")], now.use("M", ("e1", "out")))
                    sp.dma_start(out[:, bass.ds(now.group() * GT, GT)],
                                 fin[:].rearrange("p b d -> p (b d)")).then_inc(sems["store"], 16)

            run(sp, "SP", emit)
            sp.wait_ge(sems["store"], 16 * GROUPS)

        @block.gpsimd
        def _(pool):
            for s in "XS":
                for o in "qk":
                    pool.memset(part[s, o][:], 0.0).then_inc(cleared, 1)
                pool.memset(nmax_parts[s][:], 0.0).then_inc(cleared, 1)
                pool.memset(v_nat[s][:], 0.0).then_inc(cleared, 1)
            pool.wait_ge(cleared, 8)
            for s in "XS":
                pool.memset(v_nat[s][:, :, :, HD:HD + 1], 1.0).then_inc(cleared, 1)
            pool.wait_ge(setup, 2)

            def emit(now, stage, step):
                if (stage, step) == ("X", ("xn",)):
                    pool.wait_ge(sems["x_ln"], now.at("x_ln", 21))
                    if now.had():
                        pool.wait_ge(made["X", ("xnT",)], now.use("X", ("xnT",), back=1))
                    waits_alone(pool)
                    for b in range(GB):
                        pool.tensor_scalar(xn[:, b, :], x_in[:, b, :], x_small[:, 4, b:b + 1],
                                           x_small[:, 5, b:b + 1], ALU.mult, ALU.add).then_inc(sems["x_xn"], 1)
                if (stage, step) == ("X", ("xb",)):
                    pool.wait_ge(sems["x_load"], now.at("x_load", 16))
                    if now.had():
                        pool.wait_ge(taken["X", ("w2",)], now.use("X", ("w2",), back=1))
                    pool.tensor_tensor(xb[:], x_in[:], b2g[:].unsqueeze(1).broadcast_to([P, GB, DIM]),
                                       ALU.add).then_inc(sems["x_xn"], 1)
                if (stage, step) == ("S", ("hn",)):
                    pool.wait_ge(sems["s_ln"], now.at("s_ln", 37))
                    if now.had():
                        pool.wait_ge(made["S", ("xfT",)], now.use("S", ("xfT",), back=1))
                    waits_alone(pool)
                    for b in range(GB):
                        pool.tensor_scalar(hn[:, b, :], x2[:, b, :], s_small[:, 10, b:b + 1],
                                           s_small[:, 11, b:b + 1], ALU.mult, ALU.add).then_inc(sems["s_h"], 1)
                if (stage, step) == ("S", ("xl",)):
                    pool.wait_ge(sems["s_ln"], now.at("s_ln", 37))
                    if now.had():
                        pool.wait_ge(sems["s_F"], now.at("s_F", 1, back=1))
                        pool.wait_ge(sems["s_xf"], now.at("s_xf", GB, back=1))
                    waits_alone(pool)
                    for b in range(GB):
                        pool.tensor_scalar(xl[:, b, :], x2[:, b, :], s_small[:, 4, b:b + 1],
                                           s_small[:, 5, b:b + 1], ALU.mult, ALU.add).then_inc(sems["s_h"], 1)
                    pool.tensor_copy(x2s[:], x2[:]).then_inc(sems["s_h"], 1)
                if stage == "S" and step[0] == "mask":
                    _, b, u = step
                    pool.wait_ge(taken["S", ("s2", b, u)], now.use("S", ("s2", b, u)))
                    waits_alone(pool)
                    pv = prob["S"][:, b % 2, u, :].rearrange("m (i n) -> m i n", i=4)
                    pool.affine_select(out=pv, in_=pv, compare_op=ALU.is_ge, fill=0.0, base=0,
                                       pattern=[[0, 4], [1, TOKENS]], channel_multiplier=-1
                                       ).then_inc(sems["s_pm"], 1)
                if (stage, step) == ("S", ("xf",)):
                    pool.wait_ge(sems["s_r3"], now.at("s_r3", 12))
                    waits_alone(pool)
                    for b in range(GB):
                        pool.tensor_scalar(xf[:, b, :], xl[:, b, :], r3_small[:, 4, b:b + 1], None,
                                           ALU.mult).then_inc(sems["s_xf"], 1)

            run(pool, "POOL", emit)

        @block.scalar
        def _(sc):
            sc.wait_ge(early_in, 16)
            sc.activation(tg[:], ew[:, E_AT["gx"][0]:E_AT["gf"][1]], ACT.Tanh).then_inc(gates, 1)
            sc.wait_ge(late_in, 16)

            def copies(stage, o, slots, src):
                n = CTX if (stage, o) == ("X", "k") else P
                a, b, c = slots
                k = b - a if c == 1 else len(range(a, b, c))
                return sc.activation(part[stage, o][0:n, :, a:b:c, :],
                                     src[0:n].rearrange("p (h d) -> p h d", d=HD).unsqueeze(2)
                                     .broadcast_to([n, GB * HEADS, k, HD]), ACT.Copy)

            def part_of(now, stage, which, o):
                pre, n = stage.lower(), 1 + (o == "q")
                if which == "p2":
                    sc.wait_ge(sems[f"{pre}_r"], now.at(f"{pre}_r", n))
                    copies(stage, o, Q_SECOND if o == "q" else K_SECOND, rest[stage, o][:]
                           ).then_inc(sems[f"{pre}_p2"], 1)
                    return
                if stage == "X":
                    sc.wait_ge(taken["X", ("x" + o,)], now.use("X", ("x" + o,)))
                else:
                    sc.wait_ge(sems["s_qn"], now.at("s_qn", 16))
                if now.had():
                    sc.wait_ge(made[stage, (f"st{o}", GB - 1)], now.use(stage, (f"st{o}", GB - 1), back=1))
                if now.first():
                    sc.wait_ge(cleared, 10)
                copies(stage, o, Q_FIRST if o == "q" else K_FIRST, nat[stage, o][:]
                       ).then_inc(sems[f"{pre}_p1"], 1)

            def emit(now, stage, step):
                kind = step[0]
                if (stage, step) in BANK:
                    src = bank_of(stage, step)
                if stage == "X" and kind == "xnT":
                    sc.wait_ge(made[stage, step], now.use(stage, step))
                    if now.had():
                        sc.wait_ge(made["X", ("xq",)], now.use("X", ("xq",), back=1))
                    sc.copy(xnT[:], src[:]).then_inc(taken[stage, step], 1)
                elif kind in ("p1", "p2"):
                    part_of(now, stage, kind, step[1])
                elif kind == "nmT":
                    b = step[1]
                    sc.wait_ge(made[stage, step], now.use(stage, step))
                    if now.had():
                        sc.wait_ge(made[stage, ("s2", b, UNITS - 1)], now.use(stage, ("s2", b, UNITS - 1), back=1))
                    sc.copy(nmaxT[stage][:, b, :], bank16(stage, step)[:, 0:TOKENS]).then_inc(taken[stage, step], 1)
                elif kind == "s2":
                    b, u = step[1:]
                    n = CTX if stage == "X" else P
                    sc.wait_ge(made[stage, step], now.use(stage, step))
                    user, back = ("pv", (b - 2) % GB), int(b < 2)
                    if now.had(back):
                        sc.wait_ge(made[stage, user], now.use(stage, user, back))
                    sc.activation(prob[stage][0:n, b % 2, u, :], src[0:n, :], ACT.Exp, scale=SCALE
                            ).then_inc(taken[stage, step], 1)
                elif kind == "pv":
                    sc.wait_ge(made[stage, step], now.use(stage, step))
                    b = step[1]
                    user, back = ("bt", (b - 1) % GB), int(b == 0)
                    if now.had(back):
                        sc.wait_ge(made[stage, user], now.use(stage, user, back))
                    sc.copy(raw[stage][:], src[:]).then_inc(taken[stage, step], 1)
                elif kind == "oT":
                    sc.wait_ge(made[stage, step], now.use(stage, step))
                    if stage == "X":
                        if now.had():
                            sc.wait_ge(made["X", ("w1", 1)], now.use("X", ("w1", 1), back=1))
                    else:
                        if now.had():
                            sc.wait_ge(made["S", ("wo",)], now.use("S", ("wo",), back=1))
                    sc.copy(attT[stage][:], src[:]).then_inc(taken[stage, step], 1)
                elif stage == "X" and kind == "w1":
                    c = step[1]
                    sc.wait_ge(made[stage, step], now.use(stage, step))
                    if now.had():
                        sc.wait_ge(made["X", ("w2",)], now.use("X", ("w2",), back=1))
                    sc.activation(hx[:, c, :], src[:], ACT.Relu,
                                        bias=e_("b1")[:, c:c + 1]).then_inc(taken[stage, step], 1)
                elif stage == "S" and kind == "hT":
                    sc.wait_ge(made[stage, step], now.use(stage, step))
                    if now.had():
                        sc.wait_ge(made["S", ("v",)], now.use("S", ("v",), back=1))
                    sc.activation(hT[:], src[:], ACT.Identity, scale=l_("n1w")).then_inc(taken[stage, step], 1)
                elif stage == "S" and kind == "qk":
                    c = step[1]
                    sc.wait_ge(made[stage, step], now.use(stage, step))
                    if now.had():
                        sc.wait_ge(made["S", ("pv", GB - 2)], now.use("S", ("pv", GB - 2), back=1))
                    sc.copy(qkr[:, 2 * c:2 * c + 2, :, :].rearrange("p b o d -> p (b o d)"), src[:]
                            ).then_inc(taken[stage, step], 1)
                elif stage == "S" and kind == "sq":
                    if now.had():
                        sc.wait_ge(made["S", ("pv", GB - 1)], now.use("S", ("pv", GB - 1), back=1))
                    sc.wait_ge(taken["S", ("qk", 0)], now.use("S", ("qk", 0)))
                    sc.wait_ge(taken["S", ("qk", 1)], now.use("S", ("qk", 1)))
                    sc.activation(sq[:], qkr[:], ACT.Square).then_inc(sems["s_sq"], 1)
                elif stage == "S" and kind == "v":
                    sc.wait_ge(made[stage, step], now.use(stage, step))
                    if now.had():
                        sc.wait_ge(made["S", ("pv", GB - 1)], now.use("S", ("pv", GB - 1), back=1))
                    sc.copy(v_nat["S"][:, :, :, 0:HD],
                                  src[:].rearrange("p (b h d) -> p b h d", b=GB, h=HEADS)
                                          ).then_inc(taken[stage, step], 1)
                elif stage == "S" and kind == "ss":
                    sc.wait_ge(taken["S", ("wo",)], now.use("S", ("wo",)))
                    if now.had():
                        sc.wait_ge(sems["s_r3"], now.at("s_r3", 12, back=1))
                    if now.had():
                        sc.wait_ge(sems["s_ss"], now.at("s_ss", GB, back=1))
                    for b in range(GB):
                        sc.activation(junk[:, b, :], xl[:, b, :], ACT.Square,
                                      accum_out=ss3[:, b:b + 1]).then_inc(sems["s_ss"], 1)
                elif stage == "S" and kind == "xfT":
                    sc.wait_ge(made[stage, step], now.use(stage, step))
                    if now.had():
                        sc.wait_ge(made["M", ("e1", "w2", 1)], now.use("M", ("e1", "w2", 1), back=1))
                    sc.activation(xfT[:], src[:], ACT.Identity, scale=l_("n2w")).then_inc(taken[stage, step], 1)
                elif stage == "S" and kind == "ge":
                    sc.wait_ge(sems["s_g"], now.at("s_g", 6))
                    sc.activation(g_val[:, 3, :], g_val[:, 2, :], ACT.Exp).then_inc(sems["s_ge"], 1)
                elif stage == "M" and step[1] == "w1":
                    c = step[2]
                    sc.wait_ge(made[stage, step], now.use(stage, step))
                    if now.had():
                        sc.wait_ge(taken["M", ("e1", "w2", c)], now.use("M", ("e1", "w2", c), back=1))
                    sc.activation(silu[:, c, :], src[:], ACT.Silu).then_inc(taken[stage, step], 1)
                elif stage == "M" and step[1] not in ("w2", "out"):
                    e, what, c = step
                    dst = {"e0up": (act["e0"], "out"), "e2l1": (act["e2a"], ("e2", "l2", 1)),
                           "e2l2": (act["e2b"], ("e2", "l3", 1)), "e2l3": (act["e2c"], "out"),
                           "e3up": (act["e3"], "out"), "e3down": (e3d, ("e3", "up", 1))}[e + what]
                    reader = (e, "out") if dst[1] == "out" else dst[1]
                    sc.wait_ge(made[stage, step], now.use(stage, step))
                    if now.had():
                        sc.wait_ge(made["M", reader], now.use("M", reader, back=1))
                    if what == "down" and now.had():
                        sc.wait_ge(taken["M", ("e1", "w2", 1)], now.use("M", ("e1", "w2", 1), back=1))
                    o = e3d if what == "down" else dst[0][:, c, :]
                    sc.activation(o, src[:], ACT.Gelu).then_inc(taken[stage, step], 1)

            run(sc, "ACT", emit)

        @block.vector
        def _(dve):
            dve.wait_ge(early_in, 16)
            dve.wait_ge(late_in, 16)
            dve.wait_ge(gates, 1)
            dve.tensor_scalar(b2g[:], e_("b2"), tg[:, 0:1], None, ALU.mult).then_inc(setup, 1)
            dve.tensor_tensor(qkw[:], l_("qnw"), l_("knw"), ALU.mult).then_inc(setup, 1)
            dve.wait_ge(setup, 2)

            def rsqrt(ch, y, a, t1, t2):
                dve.tensor_scalar(t1.bitcast(I32), a.bitcast(I32), 1, None, ALU.logical_shift_right).then_inc(ch.sem, 1)
                dve.wait_ge(ch.sem, ch.next())
                dve.tensor_scalar(y.bitcast(I32), t1.bitcast(I32), -1.0, float(RSQRT_SEED),
                                          ALU.mult, ALU.add).then_inc(ch.sem, 1)
                dve.wait_ge(ch.sem, ch.next())
                for _ in range(3):
                    dve.scalar_tensor_tensor(out=t1, in0=y, scalar=-0.5, in1=y,
                                                     op0=ALU.mult, op1=ALU.mult).then_inc(ch.sem, 1)
                    dve.wait_ge(ch.sem, ch.next())
                    dve.tensor_tensor(t2, t1, a, ALU.mult).then_inc(ch.sem, 1)
                    dve.wait_ge(ch.sem, ch.next())
                    dve.scalar_tensor_tensor(out=y, in0=t2, scalar=1.5, in1=y,
                                                     op0=ALU.add, op1=ALU.mult).then_inc(ch.sem, 1)
                    dve.wait_ge(ch.sem, ch.next())

            def layer_norm(ch, src, stat, mv, small):
                for b in range(GB):
                    dve.bn_stats(stat[:, b, :], src[:, b, :]).then_inc(ch.sem, 1)
                    ch.next()
                dve.wait_ge(ch.sem, ch.value())
                waits_alone(dve)
                for b in range(GB):
                    dve.bn_aggr(mv[:, b, :], stat[:, b, :]).then_inc(ch.sem, 1)
                    ch.next()
                dve.wait_ge(ch.sem, ch.value())
                dve.tensor_scalar(small[:, 0, :], mv[:, :, 1], LN_EPS, None, ALU.add).then_inc(ch.sem, 1)
                dve.wait_ge(ch.sem, ch.next())
                rsqrt(ch, small[:, 4, :], small[:, 0, :], small[:, 1, :], small[:, 2, :])
                dve.scalar_tensor_tensor(out=small[:, 5, :], in0=mv[:, :, 0], scalar=-1.0,
                                                 in1=small[:, 4, :], op0=ALU.mult, op1=ALU.mult).then_inc(ch.sem, 1)
                dve.wait_ge(ch.sem, ch.next())

            def left_of(now, stage, which, o):
                pre, n = stage.lower(), 1 + (o == "q")
                rows = CTX if (stage, o) == ("X", "k") else P
                one, two, three = [(Q, K)[o == "k"][0] for Q, K in
                                   ((Q_FIRST, K_FIRST), (Q_SECOND, K_SECOND), (Q_THIRD, K_THIRD))]
                whole = nat[stage, o][0:rows].rearrange("p (h d) -> p h d", d=HD)
                left = rest[stage, o][0:rows].rearrange("p (h d) -> p h d", d=HD)
                if which == "r":
                    dve.wait_ge(sems[f"{pre}_p1"], now.at(f"{pre}_p1", n))
                    dve.tensor_tensor(left, whole, part[stage, o][0:rows, :, one, :], ALU.subtract
                                      ).then_inc(sems[f"{pre}_r"], 1)
                else:
                    dve.wait_ge(sems[f"{pre}_p2"], now.at(f"{pre}_p2", n))
                    dve.tensor_tensor(part[stage, o][0:rows, :, three, :], left,
                                      part[stage, o][0:rows, :, two, :], ALU.subtract
                                      ).then_inc(sems[f"{pre}_p3"], 1)

            def weigh(ch, now, v, rows, over):
                dve.wait_ge(sems["s_ge"], now.at("s_ge", 1))
                dve.tensor_reduce(g_row[:, 1, :], rows(3), AX_X, ALU.add).then_inc(ch.sem, 1)
                dve.wait_ge(ch.sem, ch.next())
                dve.reciprocal(g_row[:, 2, :], g_row[:, 1, :]).then_inc(ch.sem, 1)
                dve.wait_ge(ch.sem, ch.next())
                dve.tensor_tensor(rows(4), rows(3), over(2), ALU.mult).then_inc(ch.sem, 1)
                dve.wait_ge(ch.sem, ch.next())
                other = rows(4).unsqueeze(2).broadcast_to([P, GB, EXPERTS, EXPERTS])
                own = rows(4).unsqueeze(3).broadcast_to([P, GB, EXPERTS, EXPERTS])
                before = l_("before").rearrange("p (e f) -> p e f", e=EXPERTS).unsqueeze(1) \
                    .broadcast_to([P, GB, EXPERTS, EXPERTS])
                dve.tensor_tensor(g_pair[:, 0], other, own, ALU.is_gt).then_inc(ch.sem, 1)
                ch.next()
                dve.tensor_tensor(g_pair[:, 1], other, own, ALU.is_equal).then_inc(ch.sem, 1)
                dve.wait_ge(ch.sem, ch.next())
                dve.tensor_tensor(g_pair[:, 1], g_pair[:, 1], before, ALU.mult).then_inc(ch.sem, 1)
                dve.wait_ge(ch.sem, ch.next())
                dve.tensor_tensor(g_pair[:, 0], g_pair[:, 0], g_pair[:, 1], ALU.add).then_inc(ch.sem, 1)
                dve.wait_ge(ch.sem, ch.next())
                dve.tensor_reduce(rows(5), g_pair[:, 0], AX_X, ALU.add).then_inc(ch.sem, 1)
                dve.wait_ge(ch.sem, ch.next())
                dve.tensor_scalar(v(6), v(5), 1.5, None, ALU.is_lt).then_inc(ch.sem, 1)
                dve.wait_ge(ch.sem, ch.next())
                dve.tensor_tensor(v(7), v(6), v(4), ALU.mult).then_inc(ch.sem, 1)
                dve.wait_ge(ch.sem, ch.next())
                dve.tensor_reduce(g_row[:, 3, :], rows(7), AX_X, ALU.add).then_inc(ch.sem, 1)
                dve.wait_ge(ch.sem, ch.next())
                dve.tensor_scalar(g_row[:, 4, :], g_row[:, 3, :], 1e-8, None, ALU.add).then_inc(ch.sem, 1)
                dve.wait_ge(ch.sem, ch.next())
                dve.reciprocal(g_row[:, 5, :], g_row[:, 4, :]).then_inc(ch.sem, 1)
                dve.wait_ge(ch.sem, ch.next())
                dve.tensor_tensor(rows(1), rows(7), over(5), ALU.mult).then_inc(ch.sem, 1)
                dve.wait_ge(ch.sem, ch.next())
                dve.tensor_scalar(wts[:], v(1), tg[:, 1:2], None, ALU.mult).then_inc(ch.sem, 1)
                dve.wait_ge(ch.sem, ch.next())
                ch.end()

            def emit(now, stage, step):
                kind = step[0]
                if (stage, step) in BANK:
                    src = bank_of(stage, step)
                pre = stage.lower()
                if (stage, kind) == ("X", "ln"):
                    ch = Chain(sems, "x_ln", now)
                    dve.wait_ge(sems["x_load"], now.at("x_load", 16))
                    if now.had():
                        dve.wait_ge(sems["x_xn"], now.at("x_xn", 4, back=1))
                    layer_norm(ch, x_in, x_stat, x_mv, x_small)
                    ch.end()
                elif (stage, kind) == ("X", "xq") or (stage, kind) == ("X", "xk"):
                    o = kind[1]
                    rows = P if o == "q" else CTX
                    dve.wait_ge(made[stage, step], now.use(stage, step))
                    if now.had():
                        dve.wait_ge(sems["x_p3"], now.at("x_p3", 1 + (o == "q"), back=1))
                    dve.tensor_tensor(
                        nat["X", o][0:rows].rearrange("p (b c) -> p b c", b=GB),
                        src[0:rows].rearrange("p (b c) -> p b c", b=GB),
                        e_("b" + o)[0:rows].unsqueeze(1).broadcast_to([rows, GB, DIM]), ALU.add
                                ).then_inc(taken[stage, step], 1)
                elif (stage, kind) == ("X", "xv"):
                    dve.wait_ge(made[stage, step], now.use(stage, step))
                    if now.had():
                        dve.wait_ge(made["X", ("pv", GB - 1)], now.use("X", ("pv", GB - 1), back=1))
                    if now.first():
                        dve.wait_ge(cleared, 10)
                    dve.tensor_tensor(
                        v_nat["X"][:, :, :, 0:HD], src[0:CTX].rearrange("p (b h d) -> p b h d", b=GB, h=HEADS),
                        e_("bv")[0:CTX].rearrange("p (h d) -> p h d", h=HEADS).unsqueeze(1)
                        .broadcast_to([CTX, GB, HEADS, HD]), ALU.add).then_inc(taken[stage, step], 1)
                elif kind in ("r", "p3"):
                    left_of(now, stage, kind, step[1])
                elif kind in ("stq", "stk"):
                    o, b = kind[2], step[1]
                    n = CTX if (stage, o) == ("X", "k") else TOKENS
                    dve.wait_ge(made[stage, step], now.use(stage, step))
                    if now.had():
                        dve.wait_ge(made[stage, ("s2", b, UNITS - 1)], now.use(stage, ("s2", b, UNITS - 1), back=1))
                    dve.tensor_copy(
                        stackT[stage, o][:, b, :, :],
                        bank16(stage, step)[:, 0:PAIRS * (n + n % 2)]
                        .rearrange("p (j n) -> p j n", j=PAIRS)[:, :, 0:n]).then_inc(taken[stage, step], 1)
                elif kind == "s1":
                    _, b, u = step
                    n = CTX if stage == "X" else TOKENS
                    dve.wait_ge(made[stage, step], now.use(stage, step))
                    dve.tensor_reduce(nmax[stage][:, b, 4 * u:4 * u + 4],
                                            src[:, 0:4 * n].rearrange("p (i m) -> p i m", i=4), AX_X, ALU.max,
                                            negate=True).then_inc(taken[stage, step], 1)
                elif kind == "nm":
                    b = step[1]
                    dve.wait_ge(taken[stage, ("s1", b, UNITS - 1)], now.use(stage, ("s1", b, UNITS - 1)))
                    if now.had():
                        dve.wait_ge(made[stage, ("nmT", b)], now.use(stage, ("nmT", b), back=1))
                    if now.first() and b == 0:
                        dve.wait_ge(cleared, 10)
                    both = nmax[stage][:, b, :].unsqueeze(1).broadcast_to([P, 2, HEADS])
                    hi, lo = nmax_parts[stage][:, b, :, 0:16], nmax_parts[stage][:, b, :, 16:32]
                    dve.tensor_copy(hi, both).then_inc(sems[f"{pre}_nm"], 1)
                    dve.wait_ge(sems[f"{pre}_nm"], now.at(f"{pre}_nm", 2 * b + 1))
                    dve.tensor_tensor(lo, both, hi, ALU.subtract).then_inc(sems[f"{pre}_nm"], 1)
                elif kind == "bt":
                    b = step[1]
                    dve.wait_ge(made[stage, step], now.use(stage, step))
                    if b == 0:
                        if now.had():
                            dve.wait_ge(made[stage, ("oT",)], now.use(stage, ("oT",), back=1))
                    heads = src[:].rearrange("p (h c) -> p h c", c=32)
                    dve.reciprocal(rsum[stage][:, b, :], heads[:, :, HD]).then_inc(sems[f"{pre}_rc"], 1)
                    dve.wait_ge(sems[f"{pre}_rc"], now.at(f"{pre}_rc", b + 1))
                    dve.tensor_tensor(att[stage][:, b, :].rearrange("p (h d) -> p h d", d=HD),
                                            heads[:, :, 0:HD],
                                            rsum[stage][:, b, :].unsqueeze(2).broadcast_to([P, HEADS, HD]),
                                            ALU.mult).then_inc(taken[stage, step], 1)
                elif (stage, kind) == ("X", "w2"):
                    dve.wait_ge(made[stage, step], now.use(stage, step))
                    dve.wait_ge(sems["x_xn"], now.at("x_xn", 5))
                    if now.had():
                        dve.wait_ge(sems["s_h"], now.at("s_h", 9, back=1))
                    dve.scalar_tensor_tensor(out=x2[:].rearrange("p b d -> p (b d)"), in0=src[:],
                                                   scalar=tg[:, 0:1], in1=xb[:].rearrange("p b d -> p (b d)"),
                                                   op0=ALU.mult, op1=ALU.add).then_inc(taken[stage, step], 1)
                elif (stage, kind) == ("S", "ln"):
                    ch = Chain(sems, "s_ln", now)
                    dve.wait_ge(taken["X", ("w2",)], now.use("X", ("w2",)))
                    if now.had():
                        dve.wait_ge(sems["s_h"], now.at("s_h", 8, back=1))
                    layer_norm(ch, x2, s_stat, s_mv, s_small)
                    dve.tensor_tensor(s_small[:, 6, :], s_small[:, 4, :], s_small[:, 4, :], ALU.mult
                            ).then_inc(ch.sem, 1)
                    dve.wait_ge(ch.sem, ch.next())
                    dve.tensor_tensor(s_small[:, 7, :], s_small[:, 6, :], s_mv[:, :, 1], ALU.mult).then_inc(ch.sem, 1)
                    dve.wait_ge(ch.sem, ch.next())
                    dve.tensor_scalar(s_small[:, 8, :], s_small[:, 7, :], RMS_EPS, None, ALU.add).then_inc(ch.sem, 1)
                    dve.wait_ge(ch.sem, ch.next())
                    rsqrt(ch, s_small[:, 9, :], s_small[:, 8, :], s_small[:, 1, :], s_small[:, 2, :])
                    dve.tensor_tensor(s_small[:, 10, :], s_small[:, 4, :], s_small[:, 9, :], ALU.mult
                            ).then_inc(ch.sem, 1)
                    dve.wait_ge(ch.sem, ch.next())
                    dve.tensor_tensor(s_small[:, 11, :], s_small[:, 5, :], s_small[:, 9, :], ALU.mult
                            ).then_inc(ch.sem, 1)
                    dve.wait_ge(ch.sem, ch.next())
                    ch.end()
                elif (stage, kind) == ("S", "qkn"):
                    ch = Chain(sems, "s_qn", now)
                    dve.wait_ge(sems["s_sq"], now.at("s_sq", 1))
                    dve.wait_ge(taken["S", ("qk", 0)], now.use("S", ("qk", 0)))
                    dve.wait_ge(taken["S", ("qk", 1)], now.use("S", ("qk", 1)))
                    if now.had():
                        dve.wait_ge(sems["s_p3"], now.at("s_p3", 2, back=1))
                    dve.tensor_reduce(ssq[:], sq[:].rearrange("p b o (h d) -> p (b o h) d", d=HD),
                                              AX_X, ALU.add).then_inc(ch.sem, 1)
                    dve.wait_ge(ch.sem, ch.next())
                    dve.tensor_scalar(qk_small[:, 0, :], ssq[:], 1.0 / HD, RMS_EPS, ALU.mult, ALU.add
                            ).then_inc(ch.sem, 1)
                    dve.wait_ge(ch.sem, ch.next())
                    rsqrt(ch, qk_small[:, 3, :], qk_small[:, 0, :], qk_small[:, 1, :], qk_small[:, 2, :])
                    r = qk_small[:, 3, :].rearrange("p (b o h) -> p b o h", b=GB, o=2)
                    for n, o in enumerate("qk"):
                        dve.tensor_tensor(
                            nat["S", o][:].rearrange("p (b h d) -> p b h d", b=GB, h=HEADS),
                            qkr[:, :, n, :].rearrange("p b (h d) -> p b h d", h=HEADS),
                            r[:, :, n, :].unsqueeze(3).broadcast_to([P, GB, HEADS, HD]), ALU.mult).then_inc(ch.sem, 1)
                        dve.wait_ge(ch.sem, ch.next())
                    dve.tensor_tensor(nat["S", "q"][:].rearrange("p (b c) -> p b c", b=GB),
                                              nat["S", "q"][:].rearrange("p (b c) -> p b c", b=GB),
                                              qkw[:].unsqueeze(1).broadcast_to([P, GB, DIM]), ALU.mult
                                                      ).then_inc(ch.sem, 1)
                    dve.wait_ge(ch.sem, ch.next())
                    ch.end()
                elif (stage, kind) == ("S", "wo"):
                    dve.wait_ge(made[stage, step], now.use(stage, step))
                    dve.wait_ge(sems["s_h"], now.at("s_h", 8))
                    dve.tensor_tensor(xl[:, :, MASKED:DIM],
                                            src[:, 0:GB * KEPT].rearrange("p (b c) -> p b c", b=GB),
                                            xl[:, :, MASKED:DIM], ALU.add).then_inc(taken[stage, step], 1)
                elif (stage, kind) == ("S", "r3"):
                    ch = Chain(sems, "s_r3", now)
                    dve.wait_ge(sems["s_ss"], now.at("s_ss", GB))
                    if now.had():
                        dve.wait_ge(sems["s_xf"], now.at("s_xf", GB, back=1))
                    dve.tensor_scalar(r3_small[:, 0, :], ss3[:], 1.0 / DIM, RMS_EPS, ALU.mult, ALU.add
                            ).then_inc(ch.sem, 1)
                    dve.wait_ge(ch.sem, ch.next())
                    rsqrt(ch, r3_small[:, 4, :], r3_small[:, 0, :], r3_small[:, 1, :], r3_small[:, 2, :])
                    ch.end()
                elif (stage, kind) == ("S", "fin"):
                    dve.wait_ge(taken["S", ("wo",)], now.use("S", ("wo",)))
                    dve.wait_ge(sems["s_h"], now.at("s_h", 9))
                    if now.had():
                        dve.wait_ge(sems["store"], now.at("store", 16, back=1))
                    dve.scalar_tensor_tensor(out=fin[:].rearrange("p b d -> p (b d)"),
                                             in0=xl[:].rearrange("p b d -> p (b d)"), scalar=tg[:, 1:2],
                                             in1=x2s[:].rearrange("p b d -> p (b d)"), op0=ALU.mult,
                                             op1=ALU.add).then_inc(sems["s_F"], 1)
                elif (stage, kind) == ("S", "gate"):
                    dve.wait_ge(made[stage, step], now.use(stage, step))
                    if now.had():
                        dve.wait_ge(sems["s_g"], now.at("s_g", 4, back=1))
                    dve.tensor_copy(g_val[:, 0, :], src[:, 0:GB * EXPERTS]).then_inc(taken[stage, step], 1)
                elif (stage, kind) in (("S", "g1"), ("S", "g2")):
                    ch = Chain(sems, "s_g", now, 0 if kind == "g1" else 6)

                    def v(k):
                        return g_val[:, k, :]

                    def rows(k):
                        return g_val[:, k, :].rearrange("p (b e) -> p b e", b=GB)

                    def over(k):
                        return g_row[:, k, :].unsqueeze(2).broadcast_to([P, GB, EXPERTS])

                    if kind == "g2":
                        weigh(ch, now, v, rows, over)
                        return
                    dve.wait_ge(taken["S", ("gate",)], now.use("S", ("gate",)))
                    dve.tensor_tensor(g_eq[:], v(0), v(0), ALU.is_equal).then_inc(ch.sem, 1)
                    ch.next()
                    dve.tensor_scalar(v(1), v(0), -BIG, BIG, ALU.max, ALU.min).then_inc(ch.sem, 1)
                    ch.next()
                    dve.memset(v(2), 0.0).then_inc(ch.sem, 1)
                    dve.wait_ge(ch.sem, ch.next())
                    waits_alone(dve)
                    dve.copy_predicated(v(2), g_eq[:], v(1)).then_inc(ch.sem, 1)
                    dve.wait_ge(ch.sem, ch.next())
                    dve.tensor_reduce(g_row[:, 0, :], rows(2), AX_X, ALU.max, negate=True).then_inc(ch.sem, 1)
                    dve.wait_ge(ch.sem, ch.next())
                    dve.tensor_tensor(rows(2), rows(2), over(0), ALU.add).then_inc(ch.sem, 1)
                    dve.wait_ge(ch.sem, ch.next())
                elif stage == "M" and step[1] == "w2":
                    c = step[2]
                    dve.wait_ge(made[stage, step], now.use(stage, step))
                    dve.wait_ge(taken["M", ("e1", "w1", c)], now.use("M", ("e1", "w1", c)))
                    if now.had():
                        dve.wait_ge(made["M", ("e1", "out")], now.use("M", ("e1", "out"), back=1))
                    dve.tensor_tensor(act["e1"][:, c, :], src[:], silu[:, c, :], ALU.mult
                            ).then_inc(taken[stage, step], 1)
                elif stage == "M" and step[1] == "out":
                    e = int(step[0][1])
                    dve.wait_ge(made[stage, step], now.use(stage, step))
                    at = M_OUTS.index(step)
                    if at:
                        dve.wait_ge(taken["M", M_OUTS[at - 1]], now.use("M", M_OUTS[at - 1]))
                    else:
                        dve.wait_ge(sems["s_F"], now.at("s_F", 1))
                        dve.wait_ge(sems["s_g"], now.at("s_g", PER["s_g"]))
                    for b in range(GB):
                        ins = dve.scalar_tensor_tensor(
                            out=fin[:, b, MASKED:DIM], in0=src[:, b * KEPT:(b + 1) * KEPT],
                            scalar=wts[:, b * EXPERTS + e:b * EXPERTS + e + 1], in1=fin[:, b, MASKED:DIM],
                            op0=ALU.mult, op1=ALU.add)
                    ins.then_inc(taken[stage, step], 1)

            run(dve, "DVE", emit)

        @block.tensor
        def _(pe):
            pe.wait_ge(early_in, 16)
            pe.wait_ge(consts_in, 16)
            ident = e_("ident")
            ident16 = c_("ident")

            def latest(stage, step, *made):
                last = {}
                for key in sorted(made, key=lambda k: START["PE", k]):
                    if BANK[key] != BANK[stage, step]:
                        last[BANK[key]] = key
                return last.values()

            def transposes(dst, src, stage, step):
                for b in range(GB):
                    ins = pe.transpose(dst[:, b * P:(b + 1) * P], src[:, b, :], ident)
                ins.then_inc(made[stage, step], 1)

            def attention(now, stage, step):
                kind, b = step[0], step[1]
                dst = bank_of(stage, step)
                keys = CTX if stage == "X" else P
                pre = stage.lower()
                q, k = stackT[stage, "q"], stackT[stage, "k"]
                if kind in ("stq", "stk"):
                    o = kind[2]
                    n = keys if o == "k" else P
                    pe.wait_ge(sems[f"{pre}_p3"], now.at(f"{pre}_p3", 1 + (o == "q")))
                    dst = bank16(stage, step)
                    for j in range(PAIRS):
                        h = b * HEADS + 2 * j
                        at = j * (n + n % 2)
                        ins = pe.transpose(dst[:, at:at + n],
                                           part[stage, o][0:n, h:h + 2, :, :].rearrange("p h s d -> p (h s d)"),
                                           ident16[0:n, 0:n])
                elif kind == "s1":
                    u = step[2]
                    for source in latest(stage, step, (stage, ("stq", b)), (stage, ("stk", b))):
                        pe.wait_ge(taken[source], now.use(*source))
                    if stage == "S":
                        pe.matmul(dst[:, :], ident16, c_("causal"), start=True, stop=False)
                    for i in range(4):
                        h = head_of(u, i)
                        r = ROWS * (h % 2)
                        ins = pe.matmul(dst[:, i * keys:(i + 1) * keys], q[r:r + USED, b, h // 2, :],
                                        k[r:r + USED, b, h // 2, :], start=stage == "X", stop=stage == "X" or i == 3)
                elif kind == "nmT":
                    pe.wait_ge(sems[f"{pre}_nm"], now.at(f"{pre}_nm", 2 * b + 2))
                    ins = pe.transpose(bank16(stage, step)[:, 0:TOKENS],
                                       nmax_parts[stage][:, b, :, :].rearrange("p a c -> p (a c)"), ident16)
                elif kind == "s2":
                    u = step[2]
                    for source in latest(stage, step, (stage, ("nmT", b))):
                        pe.wait_ge(taken[source], now.use(*source))
                    for i in range(4):
                        h = head_of(u, i)
                        r = ROWS * (h % 2)
                        c = 4 * (u // 2) + i
                        pe.matmul(dst[0:keys, i * P:(i + 1) * P],
                                  c_("pick")[r:r + ROWS, c * P:c * P + keys],
                                  nmaxT[stage][r:r + ROWS, b, :], start=i == 0, stop=False)
                    for i in range(4):
                        h = head_of(u, i)
                        r = ROWS * (h % 2)
                        ins = pe.matmul(dst[0:keys, i * P:(i + 1) * P], k[r:r + USED, b, h // 2, :],
                                        q[r:r + USED, b, h // 2, :], start=False, stop=i == 3)
                elif kind == "pv":
                    if stage == "X":
                        for source in latest(stage, step, ("X", ("xv",)), *[("X", ("s2", b, u)) for u in range(UNITS)]):
                            pe.wait_ge(taken[source], now.use(*source))
                    else:
                        for source in latest(stage, step, ("S", ("v",))):
                            pe.wait_ge(taken[source], now.use(*source))
                        pe.wait_ge(sems["s_pm"], now.at("s_pm", 4 * b + 4))
                    for u in range(UNITS):
                        for i in range(4):
                            ins = pe.matmul(dst[32 * i:32 * i + 32, u * P:(u + 1) * P],
                                            v_nat[stage][0:keys, b, head_of(u, i), :],
                                            prob[stage][0:keys, b % 2, u, i * P:(i + 1) * P],
                                            start=True, stop=True, skip_group_check=True)
                elif kind == "bt":
                    for source in latest(stage, step, (stage, ("pv", b))):
                        pe.wait_ge(taken[source], now.use(*source))
                    for u in range(UNITS):
                        ins = pe.transpose(dst[:, u * P:(u + 1) * P], raw[stage][:, u * P:(u + 1) * P], ident)
                ins.then_inc(made[stage, step], 1)

            def emit(now, stage, step):
                kind = step[0]
                if (stage, step) not in BANK:
                    return
                n = now.use(stage, step)
                if now.reg is not None or n > 1:
                    pe.wait_ge(taken[stage, step], n - 1)
                dst = bank_of(stage, step)
                if stage != "M" and kind in ("stq", "stk", "s1", "nmT", "s2", "pv", "bt"):
                    attention(now, stage, step)
                elif (stage, kind) == ("X", "xnT"):
                    pe.wait_ge(sems["x_xn"], now.at("x_xn", 4))
                    transposes(dst, xn, stage, step)
                elif (stage, kind) == ("X", "xq"):
                    for source in latest(stage, step, ("X", ("xnT",))):
                        pe.wait_ge(taken[source], now.use(*source))
                    for b in range(GB):
                        ins = pe.matmul(dst[:, b * P:(b + 1) * P], xnT[:, b * P:(b + 1) * P], e_("wq"),
                                        start=True, stop=True)
                    ins.then_inc(made[stage, step], 1)
                elif stage == "X" and kind in ("xk", "xv"):
                    pe.wait_ge(sems["y_load"], now.at("y_load", 16))
                    for b in range(GB):
                        ins = pe.matmul(dst[0:CTX, b * P:(b + 1) * P], yT[:, b, :],
                                        e_("w" + kind[1])[0:TEXT], start=True, stop=True)
                    ins.then_inc(made[stage, step], 1)
                elif kind == "oT":
                    for source in latest(stage, step, *[(stage, ("bt", b)) for b in range(GB)]):
                        pe.wait_ge(taken[source], now.use(*source))
                    transposes(dst, att[stage], stage, step)
                elif (stage, kind) == ("X", "w1"):
                    c = step[1]
                    for source in latest(stage, step, ("X", ("oT",))):
                        pe.wait_ge(taken[source], now.use(*source))
                    pe.matmul(dst[:, :], e_("w1")[:, c * P:(c + 1) * P], attT["X"][:], start=True, stop=True
                            ).then_inc(made[stage, step], 1)
                elif (stage, kind) == ("X", "w2"):
                    for source in latest(stage, step, ("X", ("w1", 0)), ("X", ("w1", 1))):
                        pe.wait_ge(taken[source], now.use(*source))
                    for b in range(GB):
                        for c in range(2):
                            ins = pe.matmul(dst[:, b * P:(b + 1) * P], hx[:, c, b * P:(b + 1) * P],
                                            e_("w2")[:, c * P:(c + 1) * P], start=c == 0, stop=c == 1)
                    ins.then_inc(made[stage, step], 1)
                elif (stage, kind) == ("S", "hT"):
                    pe.wait_ge(sems["s_h"], now.at("s_h", 4))
                    if now.first():
                        pe.wait_ge(late_in, 16)
                    transposes(dst, hn, stage, step)
                elif (stage, kind) == ("S", "qk"):
                    for source in latest(stage, step, ("S", ("hT",))):
                        pe.wait_ge(taken[source], now.use(*source))
                    for n in range(2):
                        b = 2 * step[1] + n
                        ins = pe.matmul(dst[:, n * 256:(n + 1) * 256], hT[:, b * P:(b + 1) * P],
                                        l_("wqkv")[:, 0:256], start=True, stop=True)
                    ins.then_inc(made[stage, step], 1)
                elif (stage, kind) == ("S", "v"):
                    for b in range(GB):
                        ins = pe.matmul(dst[:, b * P:(b + 1) * P], hT[:, b * P:(b + 1) * P],
                                        l_("wqkv")[:, 256:384], start=True, stop=True)
                    ins.then_inc(made[stage, step], 1)
                elif (stage, kind) == ("S", "wo"):
                    for source in latest(stage, step, ("S", ("oT",))):
                        pe.wait_ge(taken[source], now.use(*source))
                    for b in range(GB):
                        ins = pe.matmul(dst[:, b * KEPT:(b + 1) * KEPT], attT["S"][:, b * P:(b + 1) * P],
                                        l_("wo"), start=True, stop=True)
                    ins.then_inc(made[stage, step], 1)
                elif (stage, kind) == ("S", "xfT"):
                    pe.wait_ge(sems["s_xf"], now.at("s_xf", GB))
                    transposes(dst, xf, stage, step)
                elif (stage, kind) == ("S", "gate"):
                    for source in latest(stage, step, ("S", ("xfT",))):
                        pe.wait_ge(taken[source], now.use(*source))
                    for b in range(GB):
                        ins = pe.matmul(dst[:, b * EXPERTS:(b + 1) * EXPERTS], xfT[:, b * P:(b + 1) * P],
                                        l_("gate"), start=True, stop=True)
                    ins.then_inc(made[stage, step], 1)
                elif stage == "M":
                    experts(now, step, dst)

            def experts(now, step, dst):
                e, what = step[0], step[1]
                if what == "out":
                    name = {"e0": "e0_down", "e1": "e1_down", "e2": "e2_l4", "e3": "e3_out"}[e]
                    src = {"e0": "e0", "e1": "e1", "e2": "e2c", "e3": "e3"}[e]
                    last = {"e0": "up", "e1": "w2", "e2": "l3", "e3": "up"}[e]
                    for source in latest("M", step, ("M", (e, last, 0)), ("M", (e, last, 1))):
                        pe.wait_ge(taken[source], now.use(*source))
                    for b in range(GB):
                        for c in range(2):
                            ins = pe.matmul(dst[:, b * KEPT:(b + 1) * KEPT], act[src][:, c, b * P:(b + 1) * P],
                                            l_(name)[:, c * KEPT:(c + 1) * KEPT], start=c == 0, stop=c == 1)
                    ins.then_inc(made["M", step], 1)
                    return
                c = step[2]
                if what in ("l2", "l3"):
                    src, prev = {"l2": ("e2a", "l1"), "l3": ("e2b", "l2")}[what]
                    for source in latest("M", step, ("M", ("e2", prev, 0)), ("M", ("e2", prev, 1))):
                        pe.wait_ge(taken[source], now.use(*source))
                    for k in range(2):
                        ins = pe.matmul(dst[:, :], l_(f"e2_{what}")[:, k * 256 + c * P:k * 256 + (c + 1) * P],
                                        act[src][:, k, :], start=k == 0, stop=k == 1)
                elif (e, what) == ("e3", "up"):
                    for source in latest("M", step, ("M", ("e3", "down", 0))):
                        pe.wait_ge(taken[source], now.use(*source))
                    ins = pe.matmul(dst[:, :], l_("e3_up")[:, c * P:(c + 1) * P], e3d, start=True, stop=True)
                else:
                    pe.wait_ge(taken["S", ("xfT",)], now.use("S", ("xfT",)))
                    ins = pe.matmul(dst[:, :], l_(f"{e}_{what}")[:, c * P:(c + 1) * P], xfT[:],
                                    start=True, stop=True)
                ins.then_inc(made["M", step], 1)

            run(pe, "PE", emit)


def kernel(**inputs):
    import ml_dtypes
    import concourse.bacc as _bacc
    from concourse import mybir as _mybir
    from concourse.bass_utils import run_bass_kernel_spmd as _run

    a = {k: np.asarray(v) for k, v in inputs.items()}

    def rows(w):
        w = np.asarray(w)
        if w.shape[0] == 256:
            return np.concatenate([w[:128], w[128:]], axis=1)
        return np.concatenate([w, np.zeros((128 - w.shape[0], w.shape[1]), w.dtype)], axis=0)

    def every(row):
        return np.broadcast_to(row[None, :], (128, row.shape[0]))

    def by_head(w):
        return w.reshape(HEADS, HD, -1)[HEAD_ORDER].reshape(DIM, -1)

    x_, f_ = "L0_xattn_", "L0_ffn_"
    early = {
        "wq": a[x_ + "Wq"], "wk": rows(a[x_ + "Wk"]), "wv": rows(a[x_ + "Wv"]),
        "bq": every(a[x_ + "bq"]), "bk": every(a[x_ + "bk"]), "bv": every(a[x_ + "bv"]),
        "w1": by_head(a[x_ + "W1"]), "w2": rows(a[x_ + "W2"]), "b1": a[x_ + "b1"].reshape(2, 128).T,
        "b2": every(a[x_ + "b2"]), "gx": every(a["g_xattn"]), "gf": every(a["g_ffn"]),
        "ident": np.eye(128, dtype=np.float32),
    }
    late = {
        "n1w": a[f_ + "n1_w"][:, None], "n2w": a[f_ + "n2_w"][:, None],
        "qnw": every(np.tile(a[f_ + "qn_w"], HEADS)), "knw": every(np.tile(a[f_ + "kn_w"], HEADS)),
        "wqkv": np.concatenate([a[f_ + "wq"].T, a[f_ + "wk"].T, a[f_ + "wv"].T], axis=1),
        "wo": by_head(np.ascontiguousarray(a[f_ + "wo"].T[:, MASKED:])), "gate": a[f_ + "gate_w"].T,
        "before": every(np.tril(np.ones((EXPERTS, EXPERTS), np.float32), -1).ravel()),
        "e0_up": a[f_ + "e0_up"].T, "e0_down": rows(a[f_ + "e0_down"].T[:, MASKED:]),
        "e1_w1": a[f_ + "e1_w1"].T, "e1_w2": a[f_ + "e1_w2"].T, "e1_down": rows(a[f_ + "e1_down"].T[:, MASKED:]),
        "e2_l1": a[f_ + "e2_l1"].T, "e2_l2": rows(a[f_ + "e2_l2"].T), "e2_l3": rows(a[f_ + "e2_l3"].T),
        "e2_l4": rows(a[f_ + "e2_l4"].T[:, MASKED:]), "e3_down": a[f_ + "e3_down"].T,
        "e3_up": a[f_ + "e3_up"].T, "e3_out": rows(a[f_ + "e3_out"].T[:, MASKED:]),
    }
    pick = np.zeros((128, 8, 128), np.float32)
    for u in range(UNITS):
        for i in range(4):
            for part_row in (0, 16):
                pick[64 * (u % 2) + part_row + 4 * u + i, 4 * (u // 2) + i, :] = 1.0
    causal = np.where(np.arange(128)[None, :] <= np.arange(128)[:, None], 0.0, -1e30)
    consts = {"ident": np.eye(128), "causal": np.tile(causal, (1, 4)), "pick": pick.reshape(128, 1024)}

    def pack(parts, have, dtype):
        for name, n in parts:
            assert have[name].shape == (128, n), (name, have[name].shape)
        return np.ascontiguousarray(np.concatenate([have[name].astype(dtype, copy=False) for name, _ in parts], axis=1))

    arrays = {
        "x_rows": np.ascontiguousarray(a["x"].transpose(1, 0, 2).reshape(128, -1)),
        "ctx_cols": np.ascontiguousarray(a["ctx_768"].transpose(2, 0, 1).reshape(TEXT, -1)),
        "early": pack(EARLY, early, np.float32), "late": pack(LATE, late, np.float32),
        "consts": pack(CONSTS, consts, ml_dtypes.bfloat16),
    }
    nc = _bacc.Bacc("TRN2", target_bir_lowering=False, num_devices=1)
    args = [nc.dram_tensor(name, v.shape, _mybir.dt.from_np(v.dtype), kind="ExternalInput").ap()
            for name, v in arrays.items()]
    args.append(nc.dram_tensor("result", (128, BATCHES * DIM), F32, kind="ExternalOutput").ap())
    gated_block(nc, *args)
    r = _run(nc, [arrays], core_ids=[0])
    got = r.results[0]["result"]
    return np.ascontiguousarray(got.reshape(128, BATCHES, DIM).transpose(1, 0, 2))
```

```python
from contextlib import ExitStack

import numpy as np

import concourse.bass as bass
from concourse import mybir

F32 = mybir.dt.float32
BF16 = mybir.dt.bfloat16
I32 = mybir.dt.int32
ALU = mybir.AluOpType
ACT = mybir.ActivationFunctionType
AX_X = mybir.AxisListType.X

P = 128
BATCHES, TOKENS, DIM = 64, 128, 128
CTX, TEXT = 77, 96
HEADS, HD = 16, 8
HID, EXPERTS, MASKED = 256, 4, 32
KEPT = DIM - MASKED
GB = 4
GROUPS = BATCHES // GB
GT = GB * TOKENS
SLOTS = 6
ROWS = 64
USED = SLOTS * HD
BOUND = USED + 2
PAIRS = HEADS // 2
UNITS = 4
LN_EPS, RMS_EPS = 1e-5, 1.1920929e-07
BIG = 3.4028234663852886e38
SCALE = float(HD) ** -0.5
RSQRT_SEED = 0x5F3759DF

Q_FIRST, Q_SECOND, Q_THIRD = (0, 3, 1), (3, 5, 1), (5, 6, 1)
K_FIRST, K_SECOND, K_THIRD = (1, 6, 2), (2, 5, 2), (0, 1, 1)


def head_of(u, i):
    return 8 * (u // 2) + u % 2 + 2 * i


HEAD_ORDER = [head_of(u, i) for u in range(UNITS) for i in range(4)]

EARLY = [("wq", 128), ("wk", 128), ("wv", 128), ("bq", 128), ("bk", 128), ("bv", 128), ("w1", 256),
         ("w2", 256), ("b1", 2), ("b2", 128), ("gx", 1), ("gf", 1), ("ident", 128)]
LATE = [("n1w", 1), ("n2w", 1), ("qnw", 128), ("knw", 128), ("wqkv", 384), ("wo", KEPT), ("gate", 4),
        ("before", 16), ("e0_up", 256), ("e0_down", 2 * KEPT), ("e1_w1", 256), ("e1_w2", 256),
        ("e1_down", 2 * KEPT), ("e2_l1", 256), ("e2_l2", 512), ("e2_l3", 512), ("e2_l4", 2 * KEPT),
        ("e3_down", 128), ("e3_up", 256), ("e3_out", 2 * KEPT)]
CONSTS = [("ident", 128), ("causal", 4 * P)]


def columns(parts):
    at, out = 0, {}
    for name, n in parts:
        out[name] = (at, at + n)
        at += n
    return out, at


ORDER = {
    "PE": """
        X.xk@1 S.nmT.2+2@7 S.s1.3.2+2@4 S.s2.1.0+2@2 S.s2.1.1+2@0 S.s2.1.2+2@7 S.pv.0+2@3 S.s2.1.3+2@2 M.e3.out+3@0
        S.s1.3.3+2@7 S.s2.2.0+2@1 S.s2.2.1+2@2 S.bt.0+2@6 S.s2.2.2+2@5 X.xnT@0 S.pv.1+2@1 X.xq@5 M.e2.l3.0+3@7
        S.nmT.3+2@0 S.s2.2.3+2@6 X.stk.0@1 M.e2.l3.1+3@3 X.stk.1@6 S.bt.1+2@4 M.e1.w1.0+3@5 X.stq.0@1 S.pv.2+2@2
        X.stq.1@0 X.s1.0.0@3 M.e1.w1.1+3@6 X.s1.0.1@2 S.s2.3.0+2@1 X.s1.0.2@7 S.s2.3.1+2@5 X.stk.2@4 X.s1.0.3@6
        X.xv@3 S.bt.2+2@0 X.s1.1.0@6 X.nmT.0@2 S.s2.3.2+2@7 X.stq.2@1 X.s1.1.1@4 M.e1.w2.0+3@2 X.s1.1.2@5
        S.s2.3.3+2@3 M.e1.w2.1+3@1 X.stq.3@6 X.s1.1.3@4 M.e2.out+3@7 S.pv.3+2@2 X.s1.2.0@3 X.s1.2.1@7 X.nmT.1@4
        X.s2.0.0@6 S.bt.3+2@2 X.s1.2.2@5 X.stk.3@7 X.s1.2.3@1 S.oT+2@2 X.s2.0.1@6 X.s1.3.0@0 X.s2.0.2@3 X.s1.3.1@1
        S.wo+2@4 X.s1.3.2@2 X.nmT.2@0 X.s2.0.3@6 X.s1.3.3@5 X.s2.1.0@3 X.s2.1.1@5 X.nmT.3@2 X.s2.1.2@1 X.pv.0@4
        X.s2.1.3@7 M.e1.out+3@5 X.bt.0@7 X.s2.2.0@3 X.pv.1@4 X.s2.2.1@1 S.xfT+2@0 X.s2.2.2@2 X.s2.2.3@3 S.gate+2@1
        X.bt.1@2 X.s2.3.0@6 X.s2.3.1@3 X.s2.3.2@1 X.pv.2@7 S.hT+1@6 X.s2.3.3@2 X.bt.2@7 S.qk.0+1@0 X.pv.3@5
        S.qk.1+1@2 X.bt.3@4 M.e3.down.0+2@6 X.oT@5 M.e2.l1.0+2@4 M.e0.up.0+2@2 M.e0.up.1+2@1 X.w1.0@6 M.e3.up.0+2@0
        X.w1.1@2 M.e0.out+2@1 X.w2@4 S.v+1@6 M.e2.l1.1+2@3 M.e3.up.1+2@4 S.stk.0+1@7 S.stk.1+1@1 S.stq.0+1@3
        S.stq.1+1@2 S.stk.2+1@0 S.s1.0.0+1@5 S.s1.0.1+1@3 S.s1.0.2+1@7 S.s1.0.3+1@1 M.e2.l2.0+2@2 S.s1.1.0+1@3
        S.nmT.0+1@7 S.s1.1.1+1@1 S.s1.1.2+1@2 S.stq.2+1@0 S.s1.1.3+1@4 M.e2.l2.1+2@6 S.s1.2.0+1@5 S.stk.3+1@0
        S.nmT.1+1@1 S.s1.2.1+1@7 S.s2.0.0+1@6 S.stq.3+1@3 S.s2.0.1+1@2 S.s1.2.2+1@0 S.s1.2.3+1@1 S.s2.0.2+1@3
        S.s1.3.0+1@5 S.s2.0.3+1@4 S.s1.3.1+1@6""",
    "ACT": """
        S.pv.0+2 S.s2.1.3+2 X.p1.k S.s2.2.0+2 S.s2.2.1+2 X.xnT S.s2.2.2+2 S.pv.1+2 X.p2.k X.p1.q S.nmT.3+2
        S.s2.2.3+2 X.p2.q M.e2.l3.0+3 M.e2.l3.1+3 M.e1.w1.0+3 S.pv.2+2 M.e1.w1.1+3 S.s2.3.0+2 S.s2.3.1+2 X.nmT.0
        S.s2.3.2+2 S.s2.3.3+2 S.pv.3+2 X.nmT.1 X.s2.0.0 S.oT+2 X.s2.0.1 X.s2.0.2 X.nmT.2 S.ss+2 X.s2.0.3 X.s2.1.0
        X.s2.1.1 X.s2.1.2 X.s2.1.3 X.nmT.3 X.pv.0 X.s2.2.0 X.s2.2.1 S.xfT+2 X.s2.2.2 X.pv.1 X.s2.2.3 X.s2.3.0
        X.s2.3.1 X.s2.3.2 X.pv.2 S.ge+2 S.hT+1 X.s2.3.3 S.qk.0+1 X.pv.3 S.qk.1+1 S.sq+1 X.oT M.e3.down.0+2
        M.e0.up.0+2 X.w1.0 M.e0.up.1+2 M.e2.l1.0+2 X.w1.1 M.e3.up.0+2 S.p1.k+1 S.p1.q+1 S.p2.k+1 S.p2.q+1
        M.e2.l1.1+2 M.e2.l2.0+2 S.nmT.0+1 M.e3.up.1+2 S.v+1 M.e2.l2.1+2 S.nmT.1+1 S.s2.0.0+1 S.s2.0.1+1 S.s2.0.2+1
        S.s2.0.3+1 S.nmT.2+1 S.s2.1.0+1 S.s2.1.1+1 S.s2.1.2+1""",
    "DVE": """
        S.nm.2+2 X.ln S.s1.3.0+2 X.xk S.s1.3.1+2 M.e3.out+3 S.s1.3.2+2 X.r.k S.bt.0+2 S.s1.3.3+2 S.nm.3+2 X.xq
        X.p3.k X.r.q X.stk.0 X.p3.q S.bt.1+2 X.stk.1 X.stq.0 X.stq.1 X.s1.0.0 X.s1.0.1 X.s1.0.2 X.s1.0.3 X.nm.0
        X.stk.2 X.xv X.s1.1.0 X.stq.2 X.s1.1.1 M.e1.w2.0+3 M.e1.w2.1+3 X.s1.1.2 X.s1.1.3 S.bt.2+2 X.nm.1 M.e2.out+3
        X.stq.3 X.s1.2.0 X.s1.2.1 S.bt.3+2 X.s1.2.2 X.stk.3 X.s1.2.3 X.s1.3.0 X.nm.2 X.s1.3.1 S.wo+2 X.s1.3.2
        X.s1.3.3 X.nm.3 S.r3+2 S.ln+1 S.gate+2 X.bt.0 S.g1+2 X.bt.1 M.e1.out+3 S.g2+2 X.bt.2 S.fin+2 X.bt.3 S.qkn+1
        M.e0.out+2 S.r.k+1 X.w2 S.r.q+1 S.p3.k+1 S.p3.q+1 S.stk.0+1 S.stq.0+1 S.stk.1+1 S.stq.1+1 S.s1.0.0+1
        S.s1.0.1+1 S.s1.0.2+1 S.s1.0.3+1 S.nm.0+1 S.stk.2+1 S.s1.1.0+1 S.s1.1.1+1 S.s1.1.2+1 S.stq.2+1 S.s1.1.3+1
        S.nm.1+1 S.s1.2.0+1 S.stk.3+1 S.s1.2.1+1 S.stq.3+1 S.s1.2.2+1 S.s1.2.3+1""",
    "POOL": """
        X.xn S.mask.1.3+2 S.mask.2.0+2 S.mask.2.1+2 S.mask.2.2+2 S.mask.2.3+2 S.mask.3.0+2 S.mask.3.1+2 S.mask.3.2+2
        S.mask.3.3+2 S.xf+2 X.xb S.hn+1 S.xl+1 S.mask.0.0+1 S.mask.0.1+1 S.mask.0.2+1 S.mask.0.3+1 S.mask.1.0+1
        S.mask.1.1+1 S.mask.1.2+1""",
    "SP": """
        M.store+4 S.nmD.0+2 X.load S.nmD.1+2 S.nmD.2+2 S.nmD.3+2 X.nmD.0 X.nmD.1 X.nmD.2 X.nmD.3""",
}
M_OUTS = [("e0", "out"), ("e3", "out"), ("e2", "out"), ("e1", "out")]


def read_order():
    order, late, bank = {}, {}, {}
    for engine, text in ORDER.items():
        order[engine] = []
        for word in text.split():
            word, _, k = word.partition("@")
            word, _, n = word.partition("+")
            stage, *step = word.split(".")
            key = (stage, tuple(int(s) if s.isdigit() else s for s in step))
            order[engine].append(key)
            late[engine, key] = int(n or 0)
            if k:
                bank[key] = int(k)
    return order, late, bank


ORDER, LATE_BY, BANK = read_order()
SPREAD = max(LATE_BY.values())
LAST = GROUPS + SPREAD - 1
LOOP = (SPREAD + 2, GROUPS)

PER = {**{f"{s}_nd{b}": 64 for s in "xs" for b in range(GB)}, "x_load": 16, "y_load": 16, "x_ln": 21, "x_xn": 5, "x_p1": 2, "x_r": 2, "x_p2": 2, "x_p3": 2,
       "x_nm": 8, "x_rc": 4, "s_ln": 37, "s_h": 9, "s_sq": 1, "s_qn": 16, "s_p1": 2, "s_r": 2,
       "s_p2": 2, "s_p3": 2, "s_nm": 8, "s_rc": 4, "s_pm": 16, "s_ss": 4, "s_r3": 12, "s_xf": 4,
       "s_F": 1, "s_g": 21, "s_ge": 1, "store": 16}


def active(engine, key, t):
    return 0 <= t - LATE_BY[engine, key] < GROUPS


PER_ITERATION = {k: sum(1 for v in BANK.values() if v == k) for k in range(8)}
USES_BEFORE = {(k, t): sum(1 for tt in range(t) for key in BANK if BANK[key] == k and active("PE", key, tt))
               for k in range(8) for t in range(LAST + 1)}


class Now:

    def __init__(self, t, reg, engine, key):
        self.t, self.reg, self.key, self.g = t, reg, key, t - LATE_BY[engine, key]

    def group(self):
        return self.g if self.reg is None else self.reg + self.g

    def had(self, back=1):
        return self.reg is not None or self.g - back >= 0

    def apart(self, stage, step, back=1):
        return self.had(back) and BANK[stage, step] != BANK.get(self.key)

    def first(self):
        return self.reg is None and self.g == 0

    def at(self, name, k, back=0):
        first = (self.g - back) * PER[name] + k
        return first if self.reg is None else self.reg * PER[name] + first

    def use(self, stage, step, back=0):
        key, bank = (stage, step), BANK[stage, step]
        t = self.g - back + LATE_BY["PE", key]
        assert active("PE", key, t) and (self.reg is None or t >= SPREAD), (key, t, self.t)
        before = ORDER["PE"][:ORDER["PE"].index(key) + 1]
        n = USES_BEFORE[bank, t] + sum(1 for k in before if BANK.get(k) == bank and active("PE", k, t))
        return n if self.reg is None else self.reg * PER_ITERATION[bank] + n


class Chain:

    def __init__(self, sems, name, now, k=0):
        self.sem, self.name, self.now, self.k = sems[name], name, now, k

    def next(self):
        self.k += 1
        return self.value()

    def value(self):
        return self.now.at(self.name, self.k)

    def end(self):
        assert self.k == PER[self.name], (self.name, self.k)


def gated_block(nc, x, ctx_t, early, late, consts, out):
    E_AT, E_N = columns(EARLY)
    L_AT, L_N = columns(LATE)
    C_AT, C_N = columns(CONSTS)
    with ExitStack() as ctx:
        def sb(name, shape, dt=F32):
            return ctx.enter_context(nc.sbuf_tensor(name, shape, dt))

        banks = [ctx.enter_context(nc.psum_tensor(f"bank{k}", [P, 512], F32)) for k in range(8)]
        filled = [ctx.enter_context(nc.semaphore(f"filled{k}")) for k in range(8)]
        emptied = [ctx.enter_context(nc.semaphore(f"emptied{k}")) for k in range(8)]
        sems = {name: ctx.enter_context(nc.semaphore(name)) for name in PER}
        early_in = ctx.enter_context(nc.semaphore("early_in"))
        late_in = ctx.enter_context(nc.semaphore("late_in"))
        consts_in = ctx.enter_context(nc.semaphore("consts_in"))
        cleared = ctx.enter_context(nc.semaphore("cleared"))
        setup = ctx.enter_context(nc.semaphore("setup"))
        passed = ctx.enter_context(nc.semaphore("passed"))
        gates = ctx.enter_context(nc.semaphore("gates"))

        ew = sb("ew", [P, E_N])
        lw = sb("lw", [P, L_N])
        cw = sb("cw", [P, C_N], BF16)

        def e_(name):
            return ew[:, E_AT[name][0]:E_AT[name][1]]

        def l_(name):
            return lw[:, L_AT[name][0]:L_AT[name][1]]

        def c_(name):
            return cw[:, C_AT[name][0]:C_AT[name][1]]

        tg = sb("tg", [P, 2])
        b2g = sb("b2g", [P, DIM])
        qkw = sb("qkw", [P, DIM])
        x_in = sb("x_in", [P, GB, DIM])
        yT = sb("yT", [TEXT, GB, CTX])
        x_stat, x_mv = sb("x_stat", [P, GB, 6]), sb("x_mv", [P, GB, 2])
        x_small = sb("x_small", [P, 6, GB])
        xb = sb("xb", [P, GB, DIM])
        nat2 = {s: sb(f"nat{s}", [P, 2, GT]) for s in "XS"}
        nat = {(s, o): nat2[s][:, n, :] for s in "XS" for n, o in enumerate("qk")}
        rest = nat
        part = {(s, o): sb(f"part{s}{o}", [P, GB * HEADS, 8, HD], BF16) for s in "XS" for o in "qk"}
        stackT = {(s, o): sb(f"stackT{s}{o}", [P, GB, PAIRS, TOKENS if (s, o) != ("X", "k") else CTX], BF16)
                  for s in "XS" for o in "qk"}
        v_nat = {"X": sb("v_x", [CTX, GB, HEADS, 32]), "S": sb("v_s", [P, GB, HEADS, 32])}
        nmax = {s: sb(f"nmax{s}", [P, GB, HEADS]) for s in "XS"}
        nmax_parts = {s: sb(f"nmax_parts{s}", [P, GB, 2, HEADS], BF16) for s in "XS"}
        nmaxT = {s: sb(f"nmaxT{s}", [2 * HEADS, GB, TOKENS], BF16) for s in "XS"}
        prob = {"X": sb("prob_x", [CTX, 2, UNITS, 512]), "S": sb("prob_s", [P, 2, UNITS, 512])}
        qkr = sb("qkr", [P, GB, 2, DIM])
        raw = {s: sb(f"raw{s}", [P, 512]) for s in "XS"}
        rsum = {s: sb(f"rsum{s}", [P, GB, HEADS]) for s in "XS"}
        att = {s: sb(f"att{s}", [P, GB, DIM]) for s in "XS"}
        attT = {s: sb(f"attT{s}", [P, GT]) for s in "XS"}
        xnT = att["X"][:].rearrange("p b c -> p (b c)")
        xn = attT["X"][:].rearrange("p (b c) -> p b c", b=GB)
        hx = sb("hx", [P, 2, GT])
        x2 = sb("x2", [P, GB, DIM])
        s_stat, s_mv = sb("s_stat", [P, GB, 6]), sb("s_mv", [P, GB, 2])
        s_small = sb("s_small", [P, 12, GB])
        x2s = sb("x2s", [P, GB, DIM])
        hn, xl, hT = sb("hn", [P, GB, DIM]), sb("xl", [P, GB, DIM]), sb("hT", [P, GT])
        ssq, qk_small = sb("ssq", [P, P]), sb("qk_small", [P, 4, P])
        ss3, r3_small = sb("ss3", [P, GB]), sb("r3_small", [P, 5, GB])
        xf = junk = sb("xf", [P, GB, DIM])
        g_eq = sb("g_eq", [P, GB * EXPERTS], I32)
        g_val = sb("g_val", [P, 8, GB * EXPERTS])
        g_row = sb("g_row", [P, 6, GB])
        g_pair = sb("g_pair", [P, 2, GB, EXPERTS, EXPERTS])
        xfT = sb("xfT", [P, GT])
        wts = sb("wts", [P, GB * EXPERTS])
        fin = sb("fin", [P, GB, DIM])
        act = {n: sb(f"act_{n}", [P, 2, GT]) for n in ("e0", "e2a", "e2b", "e3")}
        act["e1"] = act["e0"]
        act["e2c"] = act["e2a"]
        e3d = act["e2b"][:, 0, :]
        silu = act["e2b"]

        def bank_of(stage, step):
            return banks[BANK[stage, step]]

        def bank16(stage, step):
            return banks[BANK[stage, step]][:].bitcast(BF16)

        made = {key: filled[k] for key, k in BANK.items()}
        taken = {key: emptied[k] for key, k in BANK.items()}

        def latest(own, *keys):
            last = {}
            for key in sorted(keys, key=lambda k: (LATE_BY["PE", k], ORDER["PE"].index(k))):
                if own is None or BANK[key] != BANK[own]:
                    last[BANK[key]] = key
            return last.values()

        def waits_alone(eng):
            eng.sem_inc(passed, 1)

        def run(eng, name, emit):
            def iteration(t, reg=None):
                for key in ORDER[name]:
                    if reg is not None or active(name, key, t):
                        emit(Now(t, reg, name, key), *key)

            for t in range(LOOP[0]):
                iteration(t)
            with eng.Fori(0, LOOP[1] - LOOP[0]) as reg:
                iteration(LOOP[0], reg)
            for t in range(LOOP[1], LAST + 1):
                iteration(t)

        block = ctx.enter_context(nc.Block())

        @block.sync
        def _(sp):
            sp.dma_start(ew[:], early).then_inc(early_in, 16)
            sp.dma_start(cw[:], consts).then_inc(consts_in, 16)

            def emit(now, stage, step):
                if (stage, step) == ("X", ("load",)):
                    g = now.group()
                    if now.had():
                        sp.wait_ge(sems["x_xn"], now.at("x_xn", 5, back=1))
                    sp.dma_start(x_in[:].rearrange("p b d -> p (b d)"),
                                 x[:, bass.ds(g * GT, GT)]).then_inc(sems["x_load"], 16)
                    if now.apart("X", ("xv",)):
                        sp.wait_ge(made["X", ("xv",)], now.use("X", ("xv",), back=1))
                    sp.dma_start(yT[:].rearrange("p b m -> p (b m)"),
                                 ctx_t[:, bass.ds(g * (GB * CTX), GB * CTX)]).then_inc(sems["y_load"], 16)
                    if now.first():
                        sp.dma_start(lw[:], late).then_inc(late_in, 16)
                if step[0] == "nmD":
                    b, name = step[1], f"{stage.lower()}_nd{step[1]}"
                    sp.wait_ge(taken[stage, ("nmT", b)], now.use(stage, ("nmT", b)))
                    for part_n in range(2):
                        for parity in range(2):
                            row, to = part_n * HEADS + parity * PAIRS, ROWS * parity + USED + part_n
                            sp.dma_start(stackT[stage, "q"][to:to + 1, b, :, :],
                                         nmaxT[stage][row:row + PAIRS, b, :]).then_inc(sems[name], 16)
                if (stage, step) == ("M", ("store",)):
                    sp.wait_ge(taken["M", ("e1", "out")], now.use("M", ("e1", "out")))
                    sp.dma_start(out[:, bass.ds(now.group() * GT, GT)],
                                 fin[:].rearrange("p b d -> p (b d)")).then_inc(sems["store"], 16)

            run(sp, "SP", emit)
            sp.wait_ge(sems["store"], 16 * GROUPS)

        @block.gpsimd
        def _(pool):
            for s in "XS":
                for o in "qk":
                    pool.memset(part[s, o][:], 0.0).then_inc(cleared, 1)
                pool.memset(v_nat[s][:], 0.0).then_inc(cleared, 1)
            pool.wait_ge(cleared, 6)
            for s in "XS":
                pool.memset(part[s, "k"][:, :, SLOTS, 0:2], 1.0).then_inc(cleared, 1)
                pool.memset(v_nat[s][:, :, :, HD:HD + 1], 1.0).then_inc(cleared, 1)
            pool.wait_ge(setup, 2)

            def emit(now, stage, step):
                if (stage, step) == ("X", ("xn",)):
                    pool.wait_ge(sems["x_ln"], now.at("x_ln", 21))
                    if now.apart("X", ("w1", 1)):
                        pool.wait_ge(made["X", ("w1", 1)], now.use("X", ("w1", 1), back=1))
                    waits_alone(pool)
                    for b in range(GB):
                        pool.tensor_scalar(xn[:, b, :], x_in[:, b, :], x_small[:, 4, b:b + 1],
                                           x_small[:, 5, b:b + 1], ALU.mult, ALU.add).then_inc(sems["x_xn"], 1)
                if (stage, step) == ("X", ("xb",)):
                    pool.wait_ge(sems["x_load"], now.at("x_load", 16))
                    if now.had():
                        pool.wait_ge(taken["X", ("w2",)], now.use("X", ("w2",), back=1))
                    pool.tensor_tensor(xb[:], x_in[:], b2g[:].unsqueeze(1).broadcast_to([P, GB, DIM]),
                                       ALU.add).then_inc(sems["x_xn"], 1)
                if (stage, step) == ("S", ("hn",)):
                    pool.wait_ge(sems["s_ln"], now.at("s_ln", 37))
                    if now.apart("S", ("hT",)):
                        pool.wait_ge(made["S", ("hT",)], now.use("S", ("hT",), back=1))
                    waits_alone(pool)
                    for b in range(GB):
                        pool.tensor_scalar(hn[:, b, :], x2[:, b, :], s_small[:, 10, b:b + 1],
                                           s_small[:, 11, b:b + 1], ALU.mult, ALU.add).then_inc(sems["s_h"], 1)
                if (stage, step) == ("S", ("xl",)):
                    pool.wait_ge(sems["s_ln"], now.at("s_ln", 37))
                    if now.had():
                        pool.wait_ge(sems["s_F"], now.at("s_F", 1, back=1))
                        pool.wait_ge(sems["s_xf"], now.at("s_xf", GB, back=1))
                    waits_alone(pool)
                    for b in range(GB):
                        pool.tensor_scalar(xl[:, b, :], x2[:, b, :], s_small[:, 4, b:b + 1],
                                           s_small[:, 5, b:b + 1], ALU.mult, ALU.add).then_inc(sems["s_h"], 1)
                    pool.tensor_copy(x2s[:], x2[:]).then_inc(sems["s_h"], 1)
                if stage == "S" and step[0] == "mask":
                    _, b, u = step
                    pool.wait_ge(taken["S", ("s2", b, u)], now.use("S", ("s2", b, u)))
                    waits_alone(pool)
                    pv = prob["S"][:, b % 2, u, :].rearrange("m (i n) -> m i n", i=4)
                    pool.affine_select(out=pv, in_=pv, compare_op=ALU.is_ge, fill=0.0, base=0,
                                       pattern=[[0, 4], [1, TOKENS]], channel_multiplier=-1
                                       ).then_inc(sems["s_pm"], 1)
                if (stage, step) == ("S", ("xf",)):
                    pool.wait_ge(sems["s_r3"], now.at("s_r3", 12))
                    waits_alone(pool)
                    for b in range(GB):
                        pool.tensor_scalar(xf[:, b, :], xl[:, b, :], r3_small[:, 4, b:b + 1], None,
                                           ALU.mult).then_inc(sems["s_xf"], 1)

            run(pool, "POOL", emit)

        @block.scalar
        def _(sc):
            sc.wait_ge(early_in, 16)
            sc.activation(tg[:], ew[:, E_AT["gx"][0]:E_AT["gf"][1]], ACT.Tanh).then_inc(gates, 1)
            sc.wait_ge(late_in, 16)

            def copies(stage, o, slots, src):
                n = CTX if (stage, o) == ("X", "k") else P
                a, b, c = slots
                k = b - a if c == 1 else len(range(a, b, c))
                return sc.activation(part[stage, o][0:n, :, a:b:c, :],
                                     src[0:n].rearrange("p (h d) -> p h d", d=HD).unsqueeze(2)
                                     .broadcast_to([n, GB * HEADS, k, HD]), ACT.Copy)

            def part_of(now, stage, which, o):
                pre, n = stage.lower(), 1 + (o == "q")
                if which == "p2":
                    sc.wait_ge(sems[f"{pre}_r"], now.at(f"{pre}_r", n))
                    copies(stage, o, Q_SECOND if o == "q" else K_SECOND, rest[stage, o][:]
                           ).then_inc(sems[f"{pre}_p2"], 1)
                    return
                if stage == "X":
                    sc.wait_ge(taken["X", ("x" + o,)], now.use("X", ("x" + o,)))
                else:
                    sc.wait_ge(sems["s_qn"], now.at("s_qn", 16))
                if now.apart(stage, (f"st{o}", GB - 1)):
                    sc.wait_ge(made[stage, (f"st{o}", GB - 1)], now.use(stage, (f"st{o}", GB - 1), back=1))
                if now.first():
                    sc.wait_ge(cleared, 10)
                copies(stage, o, Q_FIRST if o == "q" else K_FIRST, nat[stage, o][:]
                       ).then_inc(sems[f"{pre}_p1"], 1)

            def emit(now, stage, step):
                kind = step[0]
                if (stage, step) in BANK:
                    src = bank_of(stage, step)
                if stage == "X" and kind == "xnT":
                    sc.wait_ge(made[stage, step], now.use(stage, step))
                    if now.apart("X", ("oT",)):
                        sc.wait_ge(made["X", ("oT",)], now.use("X", ("oT",), back=1))
                    sc.copy(xnT, src[:]).then_inc(taken[stage, step], 1)
                elif kind in ("p1", "p2"):
                    part_of(now, stage, kind, step[1])
                elif kind == "nmT":
                    b = step[1]
                    sc.wait_ge(made[stage, step], now.use(stage, step))
                    if now.had():
                        name = f"{stage.lower()}_nd{b}"
                        sc.wait_ge(sems[name], now.at(name, 64, back=1))
                    sc.copy(nmaxT[stage][:, b, :], bank16(stage, step)[0:2 * HEADS, 0:TOKENS]).then_inc(taken[stage, step], 1)
                elif kind == "s2":
                    b, u = step[1:]
                    n = CTX if stage == "X" else P
                    sc.wait_ge(made[stage, step], now.use(stage, step))
                    user, back = ("pv", (b - 2) % GB), int(b < 2)
                    if u == 0 and now.apart(stage, user, back):
                        sc.wait_ge(made[stage, user], now.use(stage, user, back))
                    sc.activation(prob[stage][0:n, b % 2, u, :], src[0:n, :], ACT.Exp, scale=SCALE
                            ).then_inc(taken[stage, step], 1)
                elif kind == "pv":
                    sc.wait_ge(made[stage, step], now.use(stage, step))
                    b = step[1]
                    user, back = ("bt", (b - 1) % GB), int(b == 0)
                    if now.apart(stage, user, back):
                        sc.wait_ge(made[stage, user], now.use(stage, user, back))
                    sc.copy(raw[stage][:], src[:]).then_inc(taken[stage, step], 1)
                elif kind == "oT":
                    sc.wait_ge(made[stage, step], now.use(stage, step))
                    if stage == "X":
                        if now.apart("X", ("w1", 1)):
                            sc.wait_ge(made["X", ("w1", 1)], now.use("X", ("w1", 1), back=1))
                    else:
                        if now.apart("S", ("wo",)):
                            sc.wait_ge(made["S", ("wo",)], now.use("S", ("wo",), back=1))
                    sc.copy(attT[stage][:], src[:]).then_inc(taken[stage, step], 1)
                elif stage == "X" and kind == "w1":
                    c = step[1]
                    sc.wait_ge(made[stage, step], now.use(stage, step))
                    if now.apart("X", ("w2",)):
                        sc.wait_ge(made["X", ("w2",)], now.use("X", ("w2",), back=1))
                    sc.activation(hx[:, c, :], src[:], ACT.Relu,
                                        bias=e_("b1")[:, c:c + 1]).then_inc(taken[stage, step], 1)
                elif stage == "S" and kind == "hT":
                    sc.wait_ge(made[stage, step], now.use(stage, step))
                    if now.apart("S", ("v",)):
                        sc.wait_ge(made["S", ("v",)], now.use("S", ("v",), back=1))
                    sc.activation(hT[:], src[:], ACT.Identity, scale=l_("n1w")).then_inc(taken[stage, step], 1)
                elif stage == "S" and kind == "qk":
                    c = step[1]
                    sc.wait_ge(made[stage, step], now.use(stage, step))
                    if now.had():
                        sc.wait_ge(sems["s_qn"], now.at("s_qn", 16, back=1))
                    sc.copy(qkr[:, 2 * c:2 * c + 2, :, :].rearrange("p b o d -> p (b o d)"), src[:]
                            ).then_inc(taken[stage, step], 1)
                elif stage == "S" and kind == "sq":
                    if now.had():
                        sc.wait_ge(sems["s_p3"], now.at("s_p3", 2, back=1))
                    for source in latest(None, ("S", ("qk", 0)), ("S", ("qk", 1))):
                        sc.wait_ge(taken[source], now.use(*source))
                    sc.activation(nat2["S"][:].rearrange("p o (b c) -> p b o c", b=GB), qkr[:], ACT.Square).then_inc(sems["s_sq"], 1)
                elif stage == "S" and kind == "v":
                    sc.wait_ge(made[stage, step], now.use(stage, step))
                    if now.apart("S", ("pv", GB - 1)):
                        sc.wait_ge(made["S", ("pv", GB - 1)], now.use("S", ("pv", GB - 1), back=1))
                    sc.copy(v_nat["S"][:, :, :, 0:HD],
                                  src[:].rearrange("p (b h d) -> p b h d", b=GB, h=HEADS)
                                          ).then_inc(taken[stage, step], 1)
                elif stage == "S" and kind == "ss":
                    sc.wait_ge(taken["S", ("wo",)], now.use("S", ("wo",)))
                    if now.had():
                        sc.wait_ge(sems["s_r3"], now.at("s_r3", 12, back=1))
                    if now.had():
                        sc.wait_ge(sems["s_ss"], now.at("s_ss", GB, back=1))
                    for b in range(GB):
                        sc.activation(junk[:, b, :], xl[:, b, :], ACT.Square,
                                      accum_out=ss3[:, b:b + 1]).then_inc(sems["s_ss"], 1)
                elif stage == "S" and kind == "xfT":
                    sc.wait_ge(made[stage, step], now.use(stage, step))
                    if now.apart("M", ("e1", "w2", 1)):
                        sc.wait_ge(made["M", ("e1", "w2", 1)], now.use("M", ("e1", "w2", 1), back=1))
                    sc.activation(xfT[:], src[:], ACT.Identity, scale=l_("n2w")).then_inc(taken[stage, step], 1)
                elif stage == "S" and kind == "ge":
                    sc.wait_ge(sems["s_g"], now.at("s_g", 6))
                    sc.activation(g_val[:, 3, :], g_val[:, 2, :], ACT.Exp).then_inc(sems["s_ge"], 1)
                elif stage == "M" and step[1] == "w1":
                    c = step[2]
                    sc.wait_ge(made[stage, step], now.use(stage, step))
                    if now.had():
                        sc.wait_ge(taken["M", ("e1", "w2", c)], now.use("M", ("e1", "w2", c), back=1))
                    sc.activation(silu[:, c, :], src[:], ACT.Silu).then_inc(taken[stage, step], 1)
                elif stage == "M" and step[1] not in ("w2", "out"):
                    e, what, c = step
                    dst = {"e0up": (act["e0"], "out"), "e2l1": (act["e2a"], ("e2", "l2", 1)),
                           "e2l2": (act["e2b"], ("e2", "l3", 1)), "e2l3": (act["e2c"], "out"),
                           "e3up": (act["e3"], "out"), "e3down": (e3d, ("e3", "up", 1))}[e + what]
                    reader = (e, "out") if dst[1] == "out" else dst[1]
                    sc.wait_ge(made[stage, step], now.use(stage, step))
                    if now.apart("M", reader):
                        sc.wait_ge(made["M", reader], now.use("M", reader, back=1))
                    if what == "down" and now.had():
                        sc.wait_ge(taken["M", ("e1", "w2", 1)], now.use("M", ("e1", "w2", 1), back=1))
                    o = e3d if what == "down" else dst[0][:, c, :]
                    sc.activation(o, src[:], ACT.Gelu).then_inc(taken[stage, step], 1)

            run(sc, "ACT", emit)

        @block.vector
        def _(dve):
            dve.wait_ge(early_in, 16)
            dve.wait_ge(late_in, 16)
            dve.wait_ge(gates, 1)
            dve.tensor_scalar(b2g[:], e_("b2"), tg[:, 0:1], None, ALU.mult).then_inc(setup, 1)
            dve.tensor_tensor(qkw[:], l_("qnw"), l_("knw"), ALU.mult).then_inc(setup, 1)
            dve.wait_ge(setup, 2)

            def rsqrt(ch, y, a, t1, t2):
                dve.tensor_scalar(t1.bitcast(I32), a.bitcast(I32), 1, None, ALU.logical_shift_right).then_inc(ch.sem, 1)
                dve.wait_ge(ch.sem, ch.next())
                dve.tensor_scalar(y.bitcast(I32), t1.bitcast(I32), -1.0, float(RSQRT_SEED),
                                          ALU.mult, ALU.add).then_inc(ch.sem, 1)
                dve.wait_ge(ch.sem, ch.next())
                for _ in range(3):
                    dve.scalar_tensor_tensor(out=t1, in0=y, scalar=-0.5, in1=y,
                                                     op0=ALU.mult, op1=ALU.mult).then_inc(ch.sem, 1)
                    dve.wait_ge(ch.sem, ch.next())
                    dve.tensor_tensor(t2, t1, a, ALU.mult).then_inc(ch.sem, 1)
                    dve.wait_ge(ch.sem, ch.next())
                    dve.scalar_tensor_tensor(out=y, in0=t2, scalar=1.5, in1=y,
                                                     op0=ALU.add, op1=ALU.mult).then_inc(ch.sem, 1)
                    dve.wait_ge(ch.sem, ch.next())

            def layer_norm(ch, src, stat, mv, small):
                for b in range(GB):
                    dve.bn_stats(stat[:, b, :], src[:, b, :]).then_inc(ch.sem, 1)
                    ch.next()
                dve.wait_ge(ch.sem, ch.value())
                waits_alone(dve)
                for b in range(GB):
                    dve.bn_aggr(mv[:, b, :], stat[:, b, :]).then_inc(ch.sem, 1)
                    ch.next()
                dve.wait_ge(ch.sem, ch.value())
                dve.tensor_scalar(small[:, 0, :], mv[:, :, 1], LN_EPS, None, ALU.add).then_inc(ch.sem, 1)
                dve.wait_ge(ch.sem, ch.next())
                rsqrt(ch, small[:, 4, :], small[:, 0, :], small[:, 1, :], small[:, 2, :])
                dve.scalar_tensor_tensor(out=small[:, 5, :], in0=mv[:, :, 0], scalar=-1.0,
                                                 in1=small[:, 4, :], op0=ALU.mult, op1=ALU.mult).then_inc(ch.sem, 1)
                dve.wait_ge(ch.sem, ch.next())

            def left_of(now, stage, which, o):
                pre, n = stage.lower(), 1 + (o == "q")
                rows = CTX if (stage, o) == ("X", "k") else P
                one, two, three = [(Q, K)[o == "k"][0] for Q, K in
                                   ((Q_FIRST, K_FIRST), (Q_SECOND, K_SECOND), (Q_THIRD, K_THIRD))]
                whole = nat[stage, o][0:rows].rearrange("p (h d) -> p h d", d=HD)
                left = rest[stage, o][0:rows].rearrange("p (h d) -> p h d", d=HD)
                if which == "r":
                    dve.wait_ge(sems[f"{pre}_p1"], now.at(f"{pre}_p1", n))
                    dve.tensor_tensor(left, whole, part[stage, o][0:rows, :, one, :], ALU.subtract
                                      ).then_inc(sems[f"{pre}_r"], 1)
                else:
                    dve.wait_ge(sems[f"{pre}_p2"], now.at(f"{pre}_p2", n))
                    dve.tensor_tensor(part[stage, o][0:rows, :, three, :], left,
                                      part[stage, o][0:rows, :, two, :], ALU.subtract
                                      ).then_inc(sems[f"{pre}_p3"], 1)

            def weigh(ch, now, v, rows, over):
                dve.wait_ge(sems["s_ge"], now.at("s_ge", 1))
                dve.tensor_reduce(g_row[:, 1, :], rows(3), AX_X, ALU.add).then_inc(ch.sem, 1)
                dve.wait_ge(ch.sem, ch.next())
                dve.reciprocal(g_row[:, 2, :], g_row[:, 1, :]).then_inc(ch.sem, 1)
                dve.wait_ge(ch.sem, ch.next())
                dve.tensor_tensor(rows(4), rows(3), over(2), ALU.mult).then_inc(ch.sem, 1)
                dve.wait_ge(ch.sem, ch.next())
                other = rows(4).unsqueeze(2).broadcast_to([P, GB, EXPERTS, EXPERTS])
                own = rows(4).unsqueeze(3).broadcast_to([P, GB, EXPERTS, EXPERTS])
                before = l_("before").rearrange("p (e f) -> p e f", e=EXPERTS).unsqueeze(1) \
                    .broadcast_to([P, GB, EXPERTS, EXPERTS])
                dve.tensor_tensor(g_pair[:, 0], other, own, ALU.is_gt).then_inc(ch.sem, 1)
                ch.next()
                dve.tensor_tensor(g_pair[:, 1], other, own, ALU.is_equal).then_inc(ch.sem, 1)
                dve.wait_ge(ch.sem, ch.next())
                dve.tensor_tensor(g_pair[:, 1], g_pair[:, 1], before, ALU.mult).then_inc(ch.sem, 1)
                dve.wait_ge(ch.sem, ch.next())
                dve.tensor_tensor(g_pair[:, 0], g_pair[:, 0], g_pair[:, 1], ALU.add).then_inc(ch.sem, 1)
                dve.wait_ge(ch.sem, ch.next())
                dve.tensor_reduce(rows(5), g_pair[:, 0], AX_X, ALU.add).then_inc(ch.sem, 1)
                dve.wait_ge(ch.sem, ch.next())
                dve.tensor_scalar(v(6), v(5), 1.5, None, ALU.is_lt).then_inc(ch.sem, 1)
                dve.wait_ge(ch.sem, ch.next())
                dve.tensor_tensor(v(7), v(6), v(4), ALU.mult).then_inc(ch.sem, 1)
                dve.wait_ge(ch.sem, ch.next())
                dve.tensor_reduce(g_row[:, 3, :], rows(7), AX_X, ALU.add).then_inc(ch.sem, 1)
                dve.wait_ge(ch.sem, ch.next())
                dve.tensor_scalar(g_row[:, 4, :], g_row[:, 3, :], 1e-8, None, ALU.add).then_inc(ch.sem, 1)
                dve.wait_ge(ch.sem, ch.next())
                dve.reciprocal(g_row[:, 5, :], g_row[:, 4, :]).then_inc(ch.sem, 1)
                dve.wait_ge(ch.sem, ch.next())
                dve.tensor_tensor(rows(1), rows(7), over(5), ALU.mult).then_inc(ch.sem, 1)
                dve.wait_ge(ch.sem, ch.next())
                dve.tensor_scalar(wts[:], v(1), tg[:, 1:2], None, ALU.mult).then_inc(ch.sem, 1)
                dve.wait_ge(ch.sem, ch.next())
                ch.end()

            def emit(now, stage, step):
                kind = step[0]
                if (stage, step) in BANK:
                    src = bank_of(stage, step)
                pre = stage.lower()
                if (stage, kind) == ("X", "ln"):
                    ch = Chain(sems, "x_ln", now)
                    dve.wait_ge(sems["x_load"], now.at("x_load", 16))
                    if now.had():
                        dve.wait_ge(sems["x_xn"], now.at("x_xn", 4, back=1))
                    layer_norm(ch, x_in, x_stat, x_mv, x_small)
                    ch.end()
                elif (stage, kind) == ("X", "xq") or (stage, kind) == ("X", "xk"):
                    o = kind[1]
                    rows = P if o == "q" else CTX
                    dve.wait_ge(made[stage, step], now.use(stage, step))
                    if now.had():
                        dve.wait_ge(sems["x_p3"], now.at("x_p3", 1 + (o == "q"), back=1))
                    dve.tensor_tensor(
                        nat["X", o][0:rows].rearrange("p (b c) -> p b c", b=GB),
                        src[0:rows].rearrange("p (b c) -> p b c", b=GB),
                        e_("b" + o)[0:rows].unsqueeze(1).broadcast_to([rows, GB, DIM]), ALU.add
                                ).then_inc(taken[stage, step], 1)
                elif (stage, kind) == ("X", "xv"):
                    dve.wait_ge(made[stage, step], now.use(stage, step))
                    if now.apart("X", ("pv", GB - 1)):
                        dve.wait_ge(made["X", ("pv", GB - 1)], now.use("X", ("pv", GB - 1), back=1))
                    if now.first():
                        dve.wait_ge(cleared, 10)
                    dve.tensor_tensor(
                        v_nat["X"][:, :, :, 0:HD], src[0:CTX].rearrange("p (b h d) -> p b h d", b=GB, h=HEADS),
                        e_("bv")[0:CTX].rearrange("p (h d) -> p h d", h=HEADS).unsqueeze(1)
                        .broadcast_to([CTX, GB, HEADS, HD]), ALU.add).then_inc(taken[stage, step], 1)
                elif kind in ("r", "p3"):
                    left_of(now, stage, kind, step[1])
                elif kind in ("stq", "stk"):
                    o, b = kind[2], step[1]
                    n = CTX if (stage, o) == ("X", "k") else TOKENS
                    dve.wait_ge(made[stage, step], now.use(stage, step))
                    if now.apart(stage, ("s2", b, UNITS - 1)):
                        dve.wait_ge(made[stage, ("s2", b, UNITS - 1)], now.use(stage, ("s2", b, UNITS - 1), back=1))
                    dve.tensor_copy(
                        stackT[stage, o][:, b, :, :],
                        bank16(stage, step)[:, 0:PAIRS * (n + n % 2)]
                        .rearrange("p (j n) -> p j n", j=PAIRS)[:, :, 0:n]).then_inc(taken[stage, step], 1)
                elif kind == "s1":
                    _, b, u = step
                    n = CTX if stage == "X" else TOKENS
                    dve.wait_ge(made[stage, step], now.use(stage, step))
                    dve.tensor_reduce(nmax[stage][:, b, 4 * u:4 * u + 4],
                                            src[:, 0:4 * n].rearrange("p (i m) -> p i m", i=4), AX_X, ALU.max,
                                            negate=True).then_inc(taken[stage, step], 1)
                elif kind == "nm":
                    b = step[1]
                    dve.wait_ge(taken[stage, ("s1", b, UNITS - 1)], now.use(stage, ("s1", b, UNITS - 1)))
                    if now.apart(stage, ("nmT", b)):
                        dve.wait_ge(made[stage, ("nmT", b)], now.use(stage, ("nmT", b), back=1))
                    whole = nmax[stage][:, b, :].rearrange("p (half parity i) -> p parity half i", half=2, parity=2)
                    hi, lo = (nmax_parts[stage][:, b, n, :]
                              .rearrange("p (parity half i) -> p parity half i", half=2, parity=2) for n in range(2))
                    dve.tensor_copy(hi, whole).then_inc(sems[f"{pre}_nm"], 1)
                    dve.wait_ge(sems[f"{pre}_nm"], now.at(f"{pre}_nm", 2 * b + 1))
                    dve.tensor_tensor(lo, whole, hi, ALU.subtract).then_inc(sems[f"{pre}_nm"], 1)
                elif kind == "bt":
                    b = step[1]
                    dve.wait_ge(made[stage, step], now.use(stage, step))
                    if b == 0:
                        if now.apart(stage, ("oT",)):
                            dve.wait_ge(made[stage, ("oT",)], now.use(stage, ("oT",), back=1))
                    heads = src[:].rearrange("p (h c) -> p h c", c=32)
                    dve.reciprocal(rsum[stage][:, b, :], heads[:, :, HD]).then_inc(sems[f"{pre}_rc"], 1)
                    dve.wait_ge(sems[f"{pre}_rc"], now.at(f"{pre}_rc", b + 1))
                    dve.tensor_tensor(att[stage][:, b, :].rearrange("p (h d) -> p h d", d=HD),
                                            heads[:, :, 0:HD],
                                            rsum[stage][:, b, :].unsqueeze(2).broadcast_to([P, HEADS, HD]),
                                            ALU.mult).then_inc(taken[stage, step], 1)
                elif (stage, kind) == ("X", "w2"):
                    dve.wait_ge(made[stage, step], now.use(stage, step))
                    dve.wait_ge(sems["x_xn"], now.at("x_xn", 5))
                    if now.had():
                        dve.wait_ge(sems["s_h"], now.at("s_h", 9, back=1))
                    dve.scalar_tensor_tensor(out=x2[:].rearrange("p b d -> p (b d)"), in0=src[:],
                                                   scalar=tg[:, 0:1], in1=xb[:].rearrange("p b d -> p (b d)"),
                                                   op0=ALU.mult, op1=ALU.add).then_inc(taken[stage, step], 1)
                elif (stage, kind) == ("S", "ln"):
                    ch = Chain(sems, "s_ln", now)
                    dve.wait_ge(taken["X", ("w2",)], now.use("X", ("w2",)))
                    if now.had():
                        dve.wait_ge(sems["s_h"], now.at("s_h", 8, back=1))
                    layer_norm(ch, x2, s_stat, s_mv, s_small)
                    dve.tensor_tensor(s_small[:, 6, :], s_small[:, 4, :], s_small[:, 4, :], ALU.mult
                            ).then_inc(ch.sem, 1)
                    dve.wait_ge(ch.sem, ch.next())
                    dve.tensor_tensor(s_small[:, 7, :], s_small[:, 6, :], s_mv[:, :, 1], ALU.mult).then_inc(ch.sem, 1)
                    dve.wait_ge(ch.sem, ch.next())
                    dve.tensor_scalar(s_small[:, 8, :], s_small[:, 7, :], RMS_EPS, None, ALU.add).then_inc(ch.sem, 1)
                    dve.wait_ge(ch.sem, ch.next())
                    rsqrt(ch, s_small[:, 9, :], s_small[:, 8, :], s_small[:, 1, :], s_small[:, 2, :])
                    dve.tensor_tensor(s_small[:, 10, :], s_small[:, 4, :], s_small[:, 9, :], ALU.mult
                            ).then_inc(ch.sem, 1)
                    dve.wait_ge(ch.sem, ch.next())
                    dve.tensor_tensor(s_small[:, 11, :], s_small[:, 5, :], s_small[:, 9, :], ALU.mult
                            ).then_inc(ch.sem, 1)
                    dve.wait_ge(ch.sem, ch.next())
                    ch.end()
                elif (stage, kind) == ("S", "qkn"):
                    ch = Chain(sems, "s_qn", now)
                    dve.wait_ge(sems["s_sq"], now.at("s_sq", 1))
                    for source in latest(None, ("S", ("qk", 0)), ("S", ("qk", 1))):
                        dve.wait_ge(taken[source], now.use(*source))
                    if now.had():
                        dve.wait_ge(sems["s_p3"], now.at("s_p3", 2, back=1))
                    dve.tensor_reduce(ssq[:], nat2["S"][:].rearrange("p o (n d) -> p (o n) d", d=HD),
                                              AX_X, ALU.add).then_inc(ch.sem, 1)
                    dve.wait_ge(ch.sem, ch.next())
                    dve.tensor_scalar(qk_small[:, 0, :], ssq[:], 1.0 / HD, RMS_EPS, ALU.mult, ALU.add
                            ).then_inc(ch.sem, 1)
                    dve.wait_ge(ch.sem, ch.next())
                    rsqrt(ch, qk_small[:, 3, :], qk_small[:, 0, :], qk_small[:, 1, :], qk_small[:, 2, :])
                    r = qk_small[:, 3, :].rearrange("p (o b h) -> p b o h", b=GB, o=2)
                    for n, o in enumerate("qk"):
                        dve.tensor_tensor(
                            nat["S", o].rearrange("p (b h d) -> p b h d", b=GB, h=HEADS),
                            qkr[:, :, n, :].rearrange("p b (h d) -> p b h d", h=HEADS),
                            r[:, :, n, :].unsqueeze(3).broadcast_to([P, GB, HEADS, HD]), ALU.mult).then_inc(ch.sem, 1)
                        dve.wait_ge(ch.sem, ch.next())
                    dve.tensor_tensor(nat["S", "q"].rearrange("p (b c) -> p b c", b=GB),
                                              nat["S", "q"].rearrange("p (b c) -> p b c", b=GB),
                                              qkw[:].unsqueeze(1).broadcast_to([P, GB, DIM]), ALU.mult
                                                      ).then_inc(ch.sem, 1)
                    dve.wait_ge(ch.sem, ch.next())
                    ch.end()
                elif (stage, kind) == ("S", "wo"):
                    dve.wait_ge(made[stage, step], now.use(stage, step))
                    dve.wait_ge(sems["s_h"], now.at("s_h", 8))
                    dve.tensor_tensor(xl[:, :, MASKED:DIM],
                                            src[:, 0:GB * KEPT].rearrange("p (b c) -> p b c", b=GB),
                                            xl[:, :, MASKED:DIM], ALU.add).then_inc(taken[stage, step], 1)
                elif (stage, kind) == ("S", "r3"):
                    ch = Chain(sems, "s_r3", now)
                    dve.wait_ge(sems["s_ss"], now.at("s_ss", GB))
                    if now.had():
                        dve.wait_ge(sems["s_xf"], now.at("s_xf", GB, back=1))
                    dve.tensor_scalar(r3_small[:, 0, :], ss3[:], 1.0 / DIM, RMS_EPS, ALU.mult, ALU.add
                            ).then_inc(ch.sem, 1)
                    dve.wait_ge(ch.sem, ch.next())
                    rsqrt(ch, r3_small[:, 4, :], r3_small[:, 0, :], r3_small[:, 1, :], r3_small[:, 2, :])
                    ch.end()
                elif (stage, kind) == ("S", "fin"):
                    dve.wait_ge(taken["S", ("wo",)], now.use("S", ("wo",)))
                    dve.wait_ge(sems["s_h"], now.at("s_h", 9))
                    if now.had():
                        dve.wait_ge(sems["store"], now.at("store", 16, back=1))
                    dve.scalar_tensor_tensor(out=fin[:].rearrange("p b d -> p (b d)"),
                                             in0=xl[:].rearrange("p b d -> p (b d)"), scalar=tg[:, 1:2],
                                             in1=x2s[:].rearrange("p b d -> p (b d)"), op0=ALU.mult,
                                             op1=ALU.add).then_inc(sems["s_F"], 1)
                elif (stage, kind) == ("S", "gate"):
                    dve.wait_ge(made[stage, step], now.use(stage, step))
                    if now.had():
                        dve.wait_ge(sems["s_g"], now.at("s_g", 4, back=1))
                    dve.tensor_copy(g_val[:, 0, :], src[:, 0:GB * EXPERTS]).then_inc(taken[stage, step], 1)
                elif (stage, kind) in (("S", "g1"), ("S", "g2")):
                    ch = Chain(sems, "s_g", now, 0 if kind == "g1" else 6)

                    def v(k):
                        return g_val[:, k, :]

                    def rows(k):
                        return g_val[:, k, :].rearrange("p (b e) -> p b e", b=GB)

                    def over(k):
                        return g_row[:, k, :].unsqueeze(2).broadcast_to([P, GB, EXPERTS])

                    if kind == "g2":
                        weigh(ch, now, v, rows, over)
                        return
                    dve.wait_ge(taken["S", ("gate",)], now.use("S", ("gate",)))
                    dve.tensor_tensor(g_eq[:], v(0), v(0), ALU.is_equal).then_inc(ch.sem, 1)
                    ch.next()
                    dve.tensor_scalar(v(1), v(0), -BIG, BIG, ALU.max, ALU.min).then_inc(ch.sem, 1)
                    ch.next()
                    dve.memset(v(2), 0.0).then_inc(ch.sem, 1)
                    dve.wait_ge(ch.sem, ch.next())
                    waits_alone(dve)
                    dve.copy_predicated(v(2), g_eq[:], v(1)).then_inc(ch.sem, 1)
                    dve.wait_ge(ch.sem, ch.next())
                    dve.tensor_reduce(g_row[:, 0, :], rows(2), AX_X, ALU.max, negate=True).then_inc(ch.sem, 1)
                    dve.wait_ge(ch.sem, ch.next())
                    dve.tensor_tensor(rows(2), rows(2), over(0), ALU.add).then_inc(ch.sem, 1)
                    dve.wait_ge(ch.sem, ch.next())
                elif stage == "M" and step[1] == "w2":
                    c = step[2]
                    dve.wait_ge(made[stage, step], now.use(stage, step))
                    dve.wait_ge(taken["M", ("e1", "w1", c)], now.use("M", ("e1", "w1", c)))
                    if now.apart("M", ("e1", "out")):
                        dve.wait_ge(made["M", ("e1", "out")], now.use("M", ("e1", "out"), back=1))
                    dve.tensor_tensor(act["e1"][:, c, :], src[:], silu[:, c, :], ALU.mult
                            ).then_inc(taken[stage, step], 1)
                elif stage == "M" and step[1] == "out":
                    e = int(step[0][1])
                    dve.wait_ge(made[stage, step], now.use(stage, step))
                    at = M_OUTS.index(step)
                    if at:
                        dve.wait_ge(taken["M", M_OUTS[at - 1]], now.use("M", M_OUTS[at - 1]))
                    else:
                        dve.wait_ge(sems["s_F"], now.at("s_F", 1))
                        dve.wait_ge(sems["s_g"], now.at("s_g", PER["s_g"]))
                    for b in range(GB):
                        ins = dve.scalar_tensor_tensor(
                            out=fin[:, b, MASKED:DIM], in0=src[:, b * KEPT:(b + 1) * KEPT],
                            scalar=wts[:, b * EXPERTS + e:b * EXPERTS + e + 1], in1=fin[:, b, MASKED:DIM],
                            op0=ALU.mult, op1=ALU.add)
                    ins.then_inc(taken[stage, step], 1)

            run(dve, "DVE", emit)

        @block.tensor
        def _(pe):
            pe.wait_ge(early_in, 16)
            pe.wait_ge(consts_in, 16)
            ident = e_("ident")
            ident16 = c_("ident")

            def transposes(dst, src, stage, step):
                for b in range(GB):
                    ins = pe.transpose(dst[:, b * P:(b + 1) * P], src[:, b, :], ident)
                ins.then_inc(made[stage, step], 1)

            def attention(now, stage, step):
                kind, b = step[0], step[1]
                dst = bank_of(stage, step)
                keys = CTX if stage == "X" else P
                pre = stage.lower()
                q, k = stackT[stage, "q"], stackT[stage, "k"]
                if kind in ("stq", "stk"):
                    o = kind[2]
                    n = keys if o == "k" else P
                    pe.wait_ge(sems[f"{pre}_p3"], now.at(f"{pre}_p3", 1 + (o == "q")))
                    dst = bank16(stage, step)
                    for j in range(PAIRS):
                        h = b * HEADS + 2 * j
                        at = j * (n + n % 2)
                        ins = pe.transpose(dst[:, at:at + n],
                                           part[stage, o][0:n, h:h + 2, :, :].rearrange("p h s d -> p (h s d)"),
                                           ident16[0:n, 0:n])
                elif kind == "s1":
                    u = step[2]
                    if u == 0:
                        for source in latest((stage, step), (stage, ("stq", b)), (stage, ("stk", b))):
                            pe.wait_ge(taken[source], now.use(*source))
                    if stage == "S":
                        pe.matmul(dst[:, :], ident16, c_("causal"), start=True, stop=False)
                    for i in range(4):
                        h = head_of(u, i)
                        r = ROWS * (h % 2)
                        ins = pe.matmul(dst[:, i * keys:(i + 1) * keys], q[r:r + USED, b, h // 2, :],
                                        k[r:r + USED, b, h // 2, :], start=stage == "X", stop=stage == "X" or i == 3)
                elif kind == "nmT":
                    pe.wait_ge(sems[f"{pre}_nm"], now.at(f"{pre}_nm", 2 * b + 2))
                    ins = pe.transpose(bank16(stage, step)[0:2 * HEADS, 0:TOKENS],
                                       nmax_parts[stage][:, b, :, :].rearrange("p a c -> p (a c)"), ident16)
                elif kind == "s2":
                    u = step[2]
                    if u == 0:
                        pe.wait_ge(sems[f"{pre}_nd{b}"], now.at(f"{pre}_nd{b}", 64))
                    for i in range(4):
                        h = head_of(u, i)
                        r = ROWS * (h % 2)
                        ins = pe.matmul(dst[0:keys, i * P:(i + 1) * P], k[r:r + BOUND, b, h // 2, :],
                                        q[r:r + BOUND, b, h // 2, :], start=True, stop=True)
                elif kind == "pv":
                    if stage == "X":
                        for source in latest((stage, step), ("X", ("xv",)), *[("X", ("s2", b, u)) for u in range(UNITS)]):
                            pe.wait_ge(taken[source], now.use(*source))
                    else:
                        for source in latest((stage, step), ("S", ("v",))):
                            pe.wait_ge(taken[source], now.use(*source))
                        pe.wait_ge(sems["s_pm"], now.at("s_pm", 4 * b + 4))
                    for u in range(UNITS):
                        for i in range(4):
                            ins = pe.matmul(dst[32 * i:32 * i + 32, u * P:(u + 1) * P],
                                            v_nat[stage][0:keys, b, head_of(u, i), :],
                                            prob[stage][0:keys, b % 2, u, i * P:(i + 1) * P],
                                            start=True, stop=True, skip_group_check=True)
                elif kind == "bt":
                    for source in latest((stage, step), (stage, ("pv", b))):
                        pe.wait_ge(taken[source], now.use(*source))
                    for u in range(UNITS):
                        ins = pe.transpose(dst[:, u * P:(u + 1) * P], raw[stage][:, u * P:(u + 1) * P], ident)
                ins.then_inc(made[stage, step], 1)

            def emit(now, stage, step):
                kind = step[0]
                if (stage, step) not in BANK:
                    return
                n = now.use(stage, step)
                if now.reg is not None or n > 1:
                    pe.wait_ge(taken[stage, step], n - 1)
                dst = bank_of(stage, step)
                if stage != "M" and kind in ("stq", "stk", "s1", "nmT", "s2", "pv", "bt"):
                    attention(now, stage, step)
                elif (stage, kind) == ("X", "xnT"):
                    pe.wait_ge(sems["x_xn"], now.at("x_xn", 4))
                    transposes(dst, xn, stage, step)
                elif (stage, kind) == ("X", "xq"):
                    for source in latest((stage, step), ("X", ("xnT",))):
                        pe.wait_ge(taken[source], now.use(*source))
                    for b in range(GB):
                        ins = pe.matmul(dst[:, b * P:(b + 1) * P], xnT[:, b * P:(b + 1) * P], e_("wq"),
                                        start=True, stop=True)
                    ins.then_inc(made[stage, step], 1)
                elif stage == "X" and kind in ("xk", "xv"):
                    pe.wait_ge(sems["y_load"], now.at("y_load", 16))
                    for b in range(GB):
                        ins = pe.matmul(dst[0:CTX, b * P:(b + 1) * P], yT[:, b, :],
                                        e_("w" + kind[1])[0:TEXT], start=True, stop=True)
                    ins.then_inc(made[stage, step], 1)
                elif kind == "oT":
                    for source in latest((stage, step), *[(stage, ("bt", b)) for b in range(GB)]):
                        pe.wait_ge(taken[source], now.use(*source))
                    transposes(dst, att[stage], stage, step)
                elif (stage, kind) == ("X", "w1"):
                    c = step[1]
                    if c == 0:
                        for source in latest((stage, step), ("X", ("oT",))):
                            pe.wait_ge(taken[source], now.use(*source))
                    pe.matmul(dst[:, :], e_("w1")[:, c * P:(c + 1) * P], attT["X"][:], start=True, stop=True
                            ).then_inc(made[stage, step], 1)
                elif (stage, kind) == ("X", "w2"):
                    for source in latest((stage, step), ("X", ("w1", 0)), ("X", ("w1", 1))):
                        pe.wait_ge(taken[source], now.use(*source))
                    for b in range(GB):
                        for c in range(2):
                            ins = pe.matmul(dst[:, b * P:(b + 1) * P], hx[:, c, b * P:(b + 1) * P],
                                            e_("w2")[:, c * P:(c + 1) * P], start=c == 0, stop=c == 1)
                    ins.then_inc(made[stage, step], 1)
                elif (stage, kind) == ("S", "hT"):
                    pe.wait_ge(sems["s_h"], now.at("s_h", 4))
                    if now.first():
                        pe.wait_ge(late_in, 16)
                    transposes(dst, hn, stage, step)
                elif (stage, kind) == ("S", "qk"):
                    for source in latest((stage, step), ("S", ("hT",))):
                        pe.wait_ge(taken[source], now.use(*source))
                    for n in range(2):
                        b = 2 * step[1] + n
                        ins = pe.matmul(dst[:, n * 256:(n + 1) * 256], hT[:, b * P:(b + 1) * P],
                                        l_("wqkv")[:, 0:256], start=True, stop=True)
                    ins.then_inc(made[stage, step], 1)
                elif (stage, kind) == ("S", "v"):
                    for b in range(GB):
                        ins = pe.matmul(dst[:, b * P:(b + 1) * P], hT[:, b * P:(b + 1) * P],
                                        l_("wqkv")[:, 256:384], start=True, stop=True)
                    ins.then_inc(made[stage, step], 1)
                elif (stage, kind) == ("S", "wo"):
                    for source in latest((stage, step), ("S", ("oT",))):
                        pe.wait_ge(taken[source], now.use(*source))
                    for b in range(GB):
                        ins = pe.matmul(dst[:, b * KEPT:(b + 1) * KEPT], attT["S"][:, b * P:(b + 1) * P],
                                        l_("wo"), start=True, stop=True)
                    ins.then_inc(made[stage, step], 1)
                elif (stage, kind) == ("S", "xfT"):
                    pe.wait_ge(sems["s_xf"], now.at("s_xf", GB))
                    transposes(dst, xf, stage, step)
                elif (stage, kind) == ("S", "gate"):
                    for source in latest((stage, step), ("S", ("xfT",))):
                        pe.wait_ge(taken[source], now.use(*source))
                    for b in range(GB):
                        ins = pe.matmul(dst[:, b * EXPERTS:(b + 1) * EXPERTS], xfT[:, b * P:(b + 1) * P],
                                        l_("gate"), start=True, stop=True)
                    ins.then_inc(made[stage, step], 1)
                elif stage == "M":
                    experts(now, step, dst)

            def experts(now, step, dst):
                e, what = step[0], step[1]
                if what == "out":
                    name = {"e0": "e0_down", "e1": "e1_down", "e2": "e2_l4", "e3": "e3_out"}[e]
                    src = {"e0": "e0", "e1": "e1", "e2": "e2c", "e3": "e3"}[e]
                    last = {"e0": "up", "e1": "w2", "e2": "l3", "e3": "up"}[e]
                    for source in latest(("M", step), ("M", (e, last, 0)), ("M", (e, last, 1))):
                        pe.wait_ge(taken[source], now.use(*source))
                    for b in range(GB):
                        for c in range(2):
                            ins = pe.matmul(dst[:, b * KEPT:(b + 1) * KEPT], act[src][:, c, b * P:(b + 1) * P],
                                            l_(name)[:, c * KEPT:(c + 1) * KEPT], start=c == 0, stop=c == 1)
                    ins.then_inc(made["M", step], 1)
                    return
                c = step[2]
                if what in ("l2", "l3"):
                    src, prev = {"l2": ("e2a", "l1"), "l3": ("e2b", "l2")}[what]
                    if c == 0:
                        for source in latest(("M", step), ("M", ("e2", prev, 0)), ("M", ("e2", prev, 1))):
                            pe.wait_ge(taken[source], now.use(*source))
                    for k in range(2):
                        ins = pe.matmul(dst[:, :], l_(f"e2_{what}")[:, k * 256 + c * P:k * 256 + (c + 1) * P],
                                        act[src][:, k, :], start=k == 0, stop=k == 1)
                elif (e, what) == ("e3", "up"):
                    if c == 0:
                        for source in latest(("M", step), ("M", ("e3", "down", 0))):
                            pe.wait_ge(taken[source], now.use(*source))
                    ins = pe.matmul(dst[:, :], l_("e3_up")[:, c * P:(c + 1) * P], e3d, start=True, stop=True)
                else:
                    for source in latest(("M", step), ("S", ("xfT",))):
                        pe.wait_ge(taken[source], now.use(*source))
                    ins = pe.matmul(dst[:, :], l_(f"{e}_{what}")[:, c * P:(c + 1) * P], xfT[:],
                                    start=True, stop=True)
                ins.then_inc(made["M", step], 1)

            run(pe, "PE", emit)


def kernel(**inputs):
    import ml_dtypes
    import concourse.bacc as _bacc
    from concourse import mybir as _mybir
    from concourse.bass_utils import run_bass_kernel_spmd as _run

    a = {k: np.asarray(v) for k, v in inputs.items()}

    def rows(w):
        w = np.asarray(w)
        if w.shape[0] == 256:
            return np.concatenate([w[:128], w[128:]], axis=1)
        return np.concatenate([w, np.zeros((128 - w.shape[0], w.shape[1]), w.dtype)], axis=0)

    def every(row):
        return np.broadcast_to(row[None, :], (128, row.shape[0]))

    def by_head(w):
        return w.reshape(HEADS, HD, -1)[HEAD_ORDER].reshape(DIM, -1)

    x_, f_ = "L0_xattn_", "L0_ffn_"
    early = {
        "wq": a[x_ + "Wq"], "wk": rows(a[x_ + "Wk"]), "wv": rows(a[x_ + "Wv"]),
        "bq": every(a[x_ + "bq"]), "bk": every(a[x_ + "bk"]), "bv": every(a[x_ + "bv"]),
        "w1": by_head(a[x_ + "W1"]), "w2": rows(a[x_ + "W2"]), "b1": a[x_ + "b1"].reshape(2, 128).T,
        "b2": every(a[x_ + "b2"]), "gx": every(a["g_xattn"]), "gf": every(a["g_ffn"]),
        "ident": np.eye(128, dtype=np.float32),
    }
    late = {
        "n1w": a[f_ + "n1_w"][:, None], "n2w": a[f_ + "n2_w"][:, None],
        "qnw": every(np.tile(a[f_ + "qn_w"], HEADS)), "knw": every(np.tile(a[f_ + "kn_w"], HEADS)),
        "wqkv": np.concatenate([a[f_ + "wq"].T, a[f_ + "wk"].T, a[f_ + "wv"].T], axis=1),
        "wo": by_head(np.ascontiguousarray(a[f_ + "wo"].T[:, MASKED:])), "gate": a[f_ + "gate_w"].T,
        "before": every(np.tril(np.ones((EXPERTS, EXPERTS), np.float32), -1).ravel()),
        "e0_up": a[f_ + "e0_up"].T, "e0_down": rows(a[f_ + "e0_down"].T[:, MASKED:]),
        "e1_w1": a[f_ + "e1_w1"].T, "e1_w2": a[f_ + "e1_w2"].T, "e1_down": rows(a[f_ + "e1_down"].T[:, MASKED:]),
        "e2_l1": a[f_ + "e2_l1"].T, "e2_l2": rows(a[f_ + "e2_l2"].T), "e2_l3": rows(a[f_ + "e2_l3"].T),
        "e2_l4": rows(a[f_ + "e2_l4"].T[:, MASKED:]), "e3_down": a[f_ + "e3_down"].T,
        "e3_up": a[f_ + "e3_up"].T, "e3_out": rows(a[f_ + "e3_out"].T[:, MASKED:]),
    }
    causal = np.where(np.arange(128)[None, :] <= np.arange(128)[:, None], 0.0, -1e30)
    consts = {"ident": np.eye(128), "causal": np.tile(causal, (1, 4))}

    def pack(parts, have, dtype):
        for name, n in parts:
            assert have[name].shape == (128, n), (name, have[name].shape)
        return np.ascontiguousarray(np.concatenate([have[name].astype(dtype, copy=False) for name, _ in parts], axis=1))

    arrays = {
        "x_rows": np.ascontiguousarray(a["x"].transpose(1, 0, 2).reshape(128, -1)),
        "ctx_cols": np.ascontiguousarray(a["ctx_768"].transpose(2, 0, 1).reshape(TEXT, -1)),
        "early": pack(EARLY, early, np.float32), "late": pack(LATE, late, np.float32),
        "consts": pack(CONSTS, consts, ml_dtypes.bfloat16),
    }
    nc = _bacc.Bacc("TRN2", target_bir_lowering=False, num_devices=1)
    args = [nc.dram_tensor(name, v.shape, _mybir.dt.from_np(v.dtype), kind="ExternalInput").ap()
            for name, v in arrays.items()]
    args.append(nc.dram_tensor("result", (128, BATCHES * DIM), F32, kind="ExternalOutput").ap())
    gated_block(nc, *args)
    r = _run(nc, [arrays], core_ids=[0])
    got = r.results[0]["result"]
    return np.ascontiguousarray(got.reshape(128, BATCHES, DIM).transpose(1, 0, 2))
```
